# Optimizing a Trainium2 kernel written in Bass

```python
import numpy as np
import jax
import jax.numpy as jnp

def _softmax(x, axis=-1):
    return jax.nn.softmax(x, axis=axis)

def _gelu(x):
    return jax.nn.gelu(x, approximate=True)

def _silu(x):
    return jax.nn.silu(x)

def _sigmoid(x):
    return jax.nn.sigmoid(x)

def _layernorm(x, axis=-1, eps=1e-05):
    m = jnp.mean(x, axis=axis, keepdims=True)
    v = jnp.var(x, axis=axis, keepdims=True)
    return (x - m) / jnp.sqrt(v + eps)

def _scatter_add(tgt, idx, src, axis=0):
    return tgt.at[idx].add(src)

def _segment_sum(src, seg, n):
    return jax.ops.segment_sum(src, seg, n)
kernel_name = 'mk_flamingo_gated_d2_seqx_r8_79eb75'

def setup_inputs(seed: int=0):
    np.random.seed(seed)
    _w = jnp.asarray

    def _rec_inputs():
        import jax
        import jax.numpy as jnp
        _rk = jax.random.key(seed)
        x = 0.0003765 + 1 * jax.random.normal(jax.random.fold_in(_rk, 1), (16, 128, 256), jnp.float32)
        _lenS = 128 - jax.random.randint(jax.random.fold_in(_rk, 7), (16,), 0, max(1, 128 // 4) + 1, jnp.int32)
        _lenS2 = 128 - jax.random.randint(jax.random.fold_in(_rk, 8), (16,), 0, max(1, 128 // 4) + 1, jnp.int32)
        _ctx_2048P = jax.random.normal(jax.random.fold_in(_rk, 11), (16, 16, 256), jnp.float32)
        _ctx_2048c = jax.random.dirichlet(jax.random.fold_in(_rk, 511), 0.3 * jnp.ones((16,), jnp.float32), (16, 128))
        _ctx_2048t = jnp.einsum('bsk,bkd->bsd', _ctx_2048c, _ctx_2048P)
        _ctx_2048t = _ctx_2048t * jax.lax.rsqrt(jnp.mean(jnp.square(_ctx_2048t)) + 1e-12) * 0.953939
        ctx_2048 = -0.000292821 + 1.00034 * (_ctx_2048t + 0.3 * jax.random.normal(jax.random.fold_in(_rk, 611), (16, 128, 256), jnp.float32))
        _g = jax.random.normal(jax.random.fold_in(_rk, 9001), (2, 2), jnp.float32)
        _g = jnp.sign(_g) * jnp.maximum(jnp.abs(_g), 1.0) + (_g == 0) * 1.0
        g_xattn = _g[0]
        g_ffn = _g[1]
        return (x, ctx_2048, g_xattn, g_ffn)
    x, ctx_2048, g_xattn, g_ffn = _rec_inputs()

    def _L0_xattn_setup():
        import jax, jax.numpy as jnp
        import numpy as np
        key = jax.random.key(seed)
        k1, k2, k3, k4, k5 = jax.random.split(key, 5)
        B, D_MODEL, L = (2, 128, 256)
        HEAD_DIM = 8
        H = D_MODEL // HEAD_DIM
        return {'k': jax.random.normal(k1, (B, D_MODEL, L), dtype=jnp.float32), 'v': jax.random.normal(k2, (B, D_MODEL, L), dtype=jnp.float32), 'q': jax.random.normal(k3, (B, D_MODEL, L), dtype=jnp.float32), 'ssm_kernel': jax.random.normal(k4, (H, L), dtype=jnp.float32), 'D': jax.random.normal(k5, (H,), dtype=jnp.float32), 'head_dim': HEAD_DIM}
    _L0_xattn_all = _L0_xattn_setup()
    _L0_xattn_in = {k: v for k, v in _L0_xattn_all.items() if k in ('ssm_kernel', 'D')}
    del _L0_xattn_all

    def _L0_ffn_setup():
        import jax, jax.numpy as jnp
        import numpy as np
        B, S, D = (2, 256, 256)
        E = 8
        TOPK = 2
        H_SHARED = 1024
        H_ROUTED = 128
        STD = 0.02
        key = jax.random.key(seed)
        ks = jax.random.split(key, 7)
        return {'x': jax.random.normal(ks[0], (B, S, D), jnp.float32), 'w12': jax.random.normal(ks[1], (E, 2 * H_ROUTED, D), jnp.float32) * STD, 'w3': jax.random.normal(ks[2], (E, D, H_ROUTED), jnp.float32) * STD, 'router_w': jax.random.normal(ks[3], (E, D), jnp.float32) * STD, 'expert_bias': jnp.zeros((E,), jnp.float32), 'sw1': jax.random.normal(ks[4], (H_SHARED, D), jnp.float32) * STD, 'sw2': jax.random.normal(ks[5], (H_SHARED, D), jnp.float32) * STD, 'sw3': jax.random.normal(ks[6], (D, H_SHARED), jnp.float32) * STD}
    _L0_ffn_all = _L0_ffn_setup()
    _L0_ffn_in = {k: v for k, v in _L0_ffn_all.items() if k in ('w12', 'w3', 'router_w', 'expert_bias', 'sw1', 'sw2', 'sw3')}
    del _L0_ffn_all

    def _L1_xattn_setup():
        import jax, jax.numpy as jnp
        import numpy as np
        HIDDEN = 256
        NUM_HEADS = 16
        HEAD_DIM = HIDDEN // NUM_HEADS
        CHUNK = 128
        SCALE = HEAD_DIM ** (-0.5)

        def _chunked_causal_attention(q, k, v):
            B, H, S, D = q.shape
            n_chunks = S // CHUNK
            kc = k.reshape(B, H, n_chunks, CHUNK, D).transpose(2, 0, 1, 3, 4)
            vc = v.reshape(B, H, n_chunks, CHUNK, D).transpose(2, 0, 1, 3, 4)
            j0s = jnp.arange(n_chunks) * CHUNK
            q_idx = jnp.arange(S)[:, None]
            k_off = jnp.arange(CHUNK)[None, :]
            out0 = jnp.zeros_like(q)
            m0 = jnp.full((B, H, S, 1), -jnp.inf, dtype=q.dtype)
            s0 = jnp.zeros((B, H, S, 1), dtype=q.dtype)

            def step(carry, inputs):
                out, m, s = carry
                kj, vj, j0 = inputs
                scores = jnp.einsum('bhqd,bhkd->bhqk', q, kj) * SCALE
                causal = j0 + k_off > q_idx
                scores = jnp.where(causal[None, None], -jnp.inf, scores)
                chunk_max = scores.max(axis=-1, keepdims=True)
                new_m = jnp.maximum(m, chunk_max)
                exp_old = jnp.exp(m - new_m)
                exp_c = jnp.exp(scores - new_m)
                new_s = s * exp_old + exp_c.sum(axis=-1, keepdims=True)
                out = out * (s / new_s) * exp_old + jnp.einsum('bhqk,bhkd->bhqd', exp_c / new_s, vj)
                return ((out, new_m, new_s), None)
            (out, _, _), _ = jax.lax.scan(step, (out0, m0, s0), (kc, vc, j0s))
            return out
        key = jax.random.key(seed)
        kq, kk, kv = jax.random.split(key, 3)
        B, S = (2, 512)
        return {'query': jax.random.normal(kq, (B, S, HIDDEN), dtype=jnp.float32), 'key': jax.random.normal(kk, (B, S, HIDDEN), dtype=jnp.float32), 'value': jax.random.normal(kv, (B, S, HIDDEN), dtype=jnp.float32)}
    _L1_xattn_all = _L1_xattn_setup()
    _L1_xattn_in = {k: v for k, v in _L1_xattn_all.items() if k in ()}
    del _L1_xattn_all

    def _L1_ffn_setup():
        import jax, jax.numpy as jnp
        import numpy as np
        D = 256
        M = 128
        E = 32
        K = 6
        G = 8
        KG = 4
        SH = 256
        SCALE = 2.5

        def _route(xf, Wr, br):
            T = xf.shape[0]
            s = jax.nn.sigmoid(xf @ Wr.T + br)
            sg = s.reshape(T, G, E // G)
            group_w = jax.lax.top_k(sg, 2)[0].sum(-1)
            top_g = jax.lax.top_k(group_w, KG)[1]
            gmask = jnp.zeros((T, G), bool).at[jnp.arange(T)[:, None], top_g].set(True)
            masked = jnp.where(gmask[:, :, None], sg, 0.0).reshape(T, E)
            idx = jax.lax.top_k(masked, K)[1]
            w = jnp.take_along_axis(s, idx, axis=1)
            w = w / (w.sum(-1, keepdims=True) + 1e-20)
            return (idx, w * SCALE)
        key = jax.random.key(seed)
        ks = jax.random.split(key, 7)
        w = 0.02
        return {'hidden_tensor': jax.random.normal(ks[0], (2, 256, D), dtype=jnp.float32), 'Wr': jax.random.normal(ks[1], (E, D), dtype=jnp.float32) * w, 'br': jax.random.normal(ks[2], (E,), dtype=jnp.float32) * w, 'W1': jax.random.normal(ks[3], (E, M, D), dtype=jnp.float32) * w, 'W2': jax.random.normal(ks[4], (E, D, M), dtype=jnp.float32) * w, 'Ws1': jax.random.normal(ks[5], (SH, D), dtype=jnp.float32) * w, 'Ws2': jax.random.normal(ks[6], (D, SH), dtype=jnp.float32) * w}
    _L1_ffn_all = _L1_ffn_setup()
    _L1_ffn_in = {k: v for k, v in _L1_ffn_all.items() if k in ('Wr', 'br', 'W1', 'W2', 'Ws1', 'Ws2')}
    del _L1_ffn_all
    return {'x': x, 'ctx_2048': ctx_2048, 'g_xattn': g_xattn, 'g_ffn': g_ffn, 'L0_xattn_ssm_kernel': _L0_xattn_in['ssm_kernel'], 'L0_xattn_D': _L0_xattn_in['D'], 'L0_ffn_w12': _L0_ffn_in['w12'], 'L0_ffn_w3': _L0_ffn_in['w3'], 'L0_ffn_router_w': _L0_ffn_in['router_w'], 'L0_ffn_expert_bias': _L0_ffn_in['expert_bias'], 'L0_ffn_sw1': _L0_ffn_in['sw1'], 'L0_ffn_sw2': _L0_ffn_in['sw2'], 'L0_ffn_sw3': _L0_ffn_in['sw3'], 'L1_ffn_Wr': _L1_ffn_in['Wr'], 'L1_ffn_br': _L1_ffn_in['br'], 'L1_ffn_W1': _L1_ffn_in['W1'], 'L1_ffn_W2': _L1_ffn_in['W2'], 'L1_ffn_Ws1': _L1_ffn_in['Ws1'], 'L1_ffn_Ws2': _L1_ffn_in['Ws2']}

def reference(x, ctx_2048, g_xattn, g_ffn, L0_xattn_ssm_kernel, L0_xattn_D, L0_ffn_w12, L0_ffn_w3, L0_ffn_router_w, L0_ffn_expert_bias, L0_ffn_sw1, L0_ffn_sw2, L0_ffn_sw3, L1_ffn_Wr, L1_ffn_br, L1_ffn_W1, L1_ffn_W2, L1_ffn_Ws1, L1_ffn_Ws2):
    import jax
    import jax.numpy as jnp

    def _L0_xattn_ref(k, v, q, ssm_kernel, D, head_dim):
        import jax, jax.numpy as jnp
        import numpy as np
        B, HD, L = k.shape
        H = HD // head_dim
        fft_size = 2 * L
        k_ = k.reshape(B, H, head_dim, L)
        v_ = v.reshape(B, H, head_dim, L)
        q_ = q.reshape(B, H, head_dim, L)
        kv = jnp.einsum('bhil,bhjl->bijhl', k_, v_)
        kv_f = jnp.fft.rfft(kv, n=fft_size)
        kernel_f = jnp.fft.rfft(ssm_kernel, n=fft_size)
        y = jnp.fft.irfft(kv_f * kernel_f, n=fft_size)[..., :L]
        out = y + kv * D[None, None, None, :, None]
        out = jnp.einsum('bijhl,bhil->bjhl', out, q_)
        out = jnp.transpose(out, (0, 2, 1, 3)).reshape(B, H * head_dim, L)
        return out.astype(k.dtype)

    def _L0_ffn_ref(x, w12, w3, router_w, expert_bias, sw1, sw2, sw3):
        import jax, jax.numpy as jnp
        import numpy as np
        B, S, D = (2, 256, 256)
        E = 8
        TOPK = 2
        H_SHARED = 1024
        H_ROUTED = 128
        STD = 0.02
        b, s, d = x.shape
        g = x @ sw1.T
        u = x @ sw2.T
        shared_out = jax.nn.silu(g) * u @ sw3.T
        scores = jax.nn.sigmoid(x @ router_w.T)
        selection_scores = scores + expert_bias
        _, top_idx = jax.lax.top_k(selection_scores, TOPK)
        top_scores = jnp.take_along_axis(scores, top_idx, axis=-1)
        top_scores = top_scores / (top_scores.sum(-1, keepdims=True) + 1e-09)
        flat_x = x.reshape(-1, d)
        T = flat_x.shape[0]
        flat_idx = top_idx.reshape(T, TOPK)
        flat_sc = top_scores.reshape(T, TOPK)
        combine = jnp.zeros((T, E), x.dtype).at[jnp.arange(T)[:, None], flat_idx].add(flat_sc)
        h12 = jnp.einsum('td,ehd->teh', flat_x, w12)
        h1, h2 = jnp.split(h12, 2, axis=-1)
        h = jax.nn.silu(h1) * h2
        out_e = jnp.einsum('teh,edh->ted', h, w3)
        routed_out = jnp.einsum('ted,te->td', out_e, combine).reshape(b, s, d)
        return shared_out + routed_out

    def _L1_xattn_ref(query, key, value):
        import jax, jax.numpy as jnp
        import numpy as np
        HIDDEN = 256
        NUM_HEADS = 16
        HEAD_DIM = HIDDEN // NUM_HEADS
        CHUNK = 128
        SCALE = HEAD_DIM ** (-0.5)

        def _chunked_causal_attention(q, k, v):
            B, H, S, D = q.shape
            n_chunks = S // CHUNK
            kc = k.reshape(B, H, n_chunks, CHUNK, D).transpose(2, 0, 1, 3, 4)
            vc = v.reshape(B, H, n_chunks, CHUNK, D).transpose(2, 0, 1, 3, 4)
            j0s = jnp.arange(n_chunks) * CHUNK
            q_idx = jnp.arange(S)[:, None]
            k_off = jnp.arange(CHUNK)[None, :]
            out0 = jnp.zeros_like(q)
            m0 = jnp.full((B, H, S, 1), -jnp.inf, dtype=q.dtype)
            s0 = jnp.zeros((B, H, S, 1), dtype=q.dtype)

            def step(carry, inputs):
                out, m, s = carry
                kj, vj, j0 = inputs
                scores = jnp.einsum('bhqd,bhkd->bhqk', q, kj) * SCALE
                causal = j0 + k_off > q_idx
                scores = jnp.where(causal[None, None], -jnp.inf, scores)
                chunk_max = scores.max(axis=-1, keepdims=True)
                new_m = jnp.maximum(m, chunk_max)
                exp_old = jnp.exp(m - new_m)
                exp_c = jnp.exp(scores - new_m)
                new_s = s * exp_old + exp_c.sum(axis=-1, keepdims=True)
                out = out * (s / new_s) * exp_old + jnp.einsum('bhqk,bhkd->bhqd', exp_c / new_s, vj)
                return ((out, new_m, new_s), None)
            (out, _, _), _ = jax.lax.scan(step, (out0, m0, s0), (kc, vc, j0s))
            return out
        B, S, _ = query.shape
        q = query.reshape(B, S, NUM_HEADS, HEAD_DIM).transpose(0, 2, 1, 3)
        k = key.reshape(B, S, NUM_HEADS, HEAD_DIM).transpose(0, 2, 1, 3)
        v = value.reshape(B, S, NUM_HEADS, HEAD_DIM).transpose(0, 2, 1, 3)
        out = _chunked_causal_attention(q, k, v)
        return out.transpose(0, 2, 1, 3).reshape(B, S, HIDDEN)

    def _L1_ffn_ref(hidden_tensor, Wr, br, W1, W2, Ws1, Ws2):
        import jax, jax.numpy as jnp
        import numpy as np
        D = 256
        M = 128
        E = 32
        K = 6
        G = 8
        KG = 4
        SH = 256
        SCALE = 2.5

        def _route(xf, Wr, br):
            T = xf.shape[0]
            s = jax.nn.sigmoid(xf @ Wr.T + br)
            sg = s.reshape(T, G, E // G)
            group_w = jax.lax.top_k(sg, 2)[0].sum(-1)
            top_g = jax.lax.top_k(group_w, KG)[1]
            gmask = jnp.zeros((T, G), bool).at[jnp.arange(T)[:, None], top_g].set(True)
            masked = jnp.where(gmask[:, :, None], sg, 0.0).reshape(T, E)
            idx = jax.lax.top_k(masked, K)[1]
            w = jnp.take_along_axis(s, idx, axis=1)
            w = w / (w.sum(-1, keepdims=True) + 1e-20)
            return (idx, w * SCALE)
        B, Tlen, C = hidden_tensor.shape
        xf = hidden_tensor.reshape(-1, C).astype(jnp.float32)
        T = xf.shape[0]
        idx, w = _route(xf, Wr, br)
        gate = jnp.zeros((T, E), w.dtype).at[jnp.arange(T)[:, None], idx].add(w)

        def step(acc, ew):
            w1, w2, g = ew
            h = jnp.square(jax.nn.relu(xf @ w1.T)) @ w2.T
            return (acc + g[:, None] * h, None)
        acc, _ = jax.lax.scan(step, jnp.zeros_like(xf), (W1, W2, gate.T))
        moe_out = acc.reshape(B, Tlen, C).astype(hidden_tensor.dtype)
        shared = jnp.square(jax.nn.relu(hidden_tensor @ Ws1.T)) @ Ws2.T
        return shared + moe_out
    x = x + jnp.tanh(g_xattn[0]) * _L0_xattn_ref(ctx_2048, ctx_2048, _layernorm(x, axis=-1), L0_xattn_ssm_kernel, L0_xattn_D, 8)
    x = x + jnp.tanh(g_ffn[0]) * _L0_ffn_ref(_layernorm(x, axis=-1), L0_ffn_w12, L0_ffn_w3, L0_ffn_router_w, L0_ffn_expert_bias, L0_ffn_sw1, L0_ffn_sw2, L0_ffn_sw3)
    x = x + jnp.tanh(g_xattn[1]) * _L1_xattn_ref(_layernorm(x, axis=-1), ctx_2048, ctx_2048)
    x = x + jnp.tanh(g_ffn[1]) * _L1_ffn_ref(_layernorm(x, axis=-1), L1_ffn_Wr, L1_ffn_br, L1_ffn_W1, L1_ffn_W2, L1_ffn_Ws1, L1_ffn_Ws2)
    return x

_drawn_inputs = setup_inputs


def setup_inputs(seed=0):
    import zlib

    import numpy as np

    out = dict(_drawn_inputs(seed))
    spreads = {'g_ffn': (-1.0, 0.6), 'L0_ffn_expert_bias': (0.0, 0.8)}
    factors = {'L0_ffn_w12': 8.0,
     'L0_ffn_w3': 8.0,
     'L0_ffn_router_w': 8.0,
     'L0_ffn_sw1': 8.0,
     'L0_ffn_sw2': 8.0,
     'L0_ffn_sw3': 8.0,
     'L1_ffn_Wr': 8.0,
     'L1_ffn_br': 8.0,
     'L1_ffn_W1': 8.0,
     'L1_ffn_W2': 8.0,
     'L1_ffn_Ws1': 8.0,
     'L1_ffn_Ws2': 8.0}
    for name, (base, spread) in spreads.items():
        noise = np.random.default_rng([zlib.crc32(name.encode()), seed]).standard_normal(out[name].shape)
        drawn = base * np.exp(spread * noise) if base else spread * noise
        out[name] = jnp.asarray(drawn.astype(out[name].dtype))
    for name, factor in factors.items():
        out[name] = (out[name] * factor).astype(out[name].dtype)
    return out
```

```python
from contextlib import ExitStack

import concourse.bass as bass
from concourse import mybir

F32 = mybir.dt.float32
F32R = mybir.dt.float32r
ALU = mybir.AluOpType
ACT = mybir.ActivationFunctionType
AX_X = mybir.AxisListType.X

P = 128
NB = 16
D = 256
T = NB * P
NH0, HD0 = 16, 8
NH1, HD1 = 16, 16
E0, E1 = 8, 32
U0 = 1024 // P + E0
U1 = E1 + 256 // P
TOP0, TOP1, G1, KG1 = 2, 6, 8, 4
SCALE1 = HD1 ** -0.5
ROUTE_SCALE = 2.5
BLK = 512
NBLK = T // BLK
BPB = BLK // P
EPS = 1e-5
FILL = -1.0e30
TAKEN = -2.0e30
S = 4


class Steps:

    def __init__(self, sem, start=0):
        self.sem, self.n = sem, start

    def up(self, ins, by=1):
        ins.then_inc(self.sem, by)
        self.n += by
        return self.n


def ap_of(view, offset, dims):
    return bass.AP(view.tensor, view.offset + offset, [list(view.ap[0])] + dims)


def build(nc, x, ctx_rev, ctx_rev_t, ctx_nat, ctx_nat_t, g_x, g_f, kpad, d_skip, wu0, rw0, eb0, wu1, rw1, br1,
          ident_c, anti_c, rowmask_c, parity_c, causal_c, out):
    top = ExitStack()
    with top:
        def sb(name, shape, dt=F32, ctx=top):
            return ctx.enter_context(nc.sbuf_tensor(name, shape, dt))

        def sem(name):
            return top.enter_context(nc.semaphore(name))

        bank = [top.enter_context(nc.psum_tensor(f"bank{i}", [P, 2, 512], F32)) for i in range(4)]

        def bk(i):
            return bank[i // 2][:, i % 2, :]

        X = sb("X", [P, NB, D])
        mv = sb("mv", [P, NB, 2])
        rstd = sb("rstd", [P, NB])
        ident = sb("ident", [P, P])
        tg = sb("tg", [P, 4])
        stats = sb("stats", [P, NB, 6])
        mhalf = sb("mhalf", [P, NB])
        vpe = sb("vpe", [P, NB])

        gates0 = nc.dram_tensor("gates0", (U0, T), F32, kind="Internal").ap()
        gates1 = nc.dram_tensor("gates1", (U1, T), F32, kind="Internal").ap()

        def ln_scale(eng_v, eng_p, tag, v=None, p=None):
            pass

        s_x = [sem(f"x_loaded{i}") for i in range(4)]
        s_c = sem("consts_loaded")
        s_tg = sem("gate_tanh")
        s_held = sem("held")
        s_st = sem("start_step")
        s_mh = sem("mhalf_set")
        s_ve0 = sem("var0_ready")
        s_rs = sem("rstd_ready")
        n_rs = [0]
        graw = sb("graw", [P, 4])

        def variances(dve, done, n, ready):
            for b in range(NB):
                last = dve.bn_aggr(mv[:, b, :], stats[:, b, :])
            last.then_inc(done, 1)
            dve.wait_ge(done, n + 1)
            dve.tensor_scalar(vpe[:], mv[:, :, 1], EPS, None, ALU.add).then_inc(ready, 1)

        with nc.Block() as block:
            @block.sync
            def _(sp):
                xv = x.rearrange("(b p) d -> p b d", p=P)
                for i in range(4):
                    sp.dma_start(X[:, 4 * i:4 * i + 4, :], xv[:, 4 * i:4 * i + 4, :]).then_inc(s_x[i], 16)

            @block.scalar
            def _(act):
                act.dma_start(ident[:], ident_c).then_inc(s_c, 16)
                act.dma_start(graw[:, 0:2], g_x.partition_broadcast(P)).then_inc(s_c, 16)
                act.dma_start(graw[:, 2:4], g_f.partition_broadcast(P)).then_inc(s_c, 16)
                act.wait_ge(s_c, 48)
                act.activation(tg[:], graw[:], ACT.Tanh).then_inc(s_tg, 1)

            @block.gpsimd
            def _(pool):
                pool.memset(mhalf[:], -0.5).then_inc(s_mh, 1)
                pool.wait_ge(s_mh, 1)
                pool.wait_ge(s_ve0, 1)
                pool.tensor_tensor(rstd[:], vpe[:], mhalf[:], ALU.pow).then_inc(s_rs, 1)

            @block.vector
            def _(dve):
                st = Steps(s_st)
                for b in range(NB):
                    if b % 4 == 0:
                        dve.wait_ge(s_x[b // 4], 16)
                    st.up(dve.bn_stats(stats[:, b, :], X[:, b, :]))
                dve.wait_ge(s_st, st.n)
                variances(dve, s_st, st.n, s_ve0)
                dve.wait_ge(s_rs, 1)

        def plain(eng):
            eng.sem_inc(s_held, 1)

        def rstd_part(phase):
            return sem(f"var_ready{phase}"), sem(f"rstd_ready{phase}")

        pa = ExitStack()
        with pa:
            cR = sb("ctx_rev_sb", [P, NB, D], ctx=pa)
            cRT = sb("ctx_rev_t_sb", [P, 2, T], ctx=pa)
            TM = sb("toeplitz", [P, 4, 4, 384], ctx=pa)
            dtmp = sb("dtmp", [P, 4, P], ctx=pa)
            anti = sb("anti", [P, P], ctx=pa)
            dbc = sb("dbc", [P, NH0], ctx=pa)
            rowmask = sb("rowmask", [P, 4], ctx=pa)
            KM = sb("k_masked", [P, 2, 4, D], ctx=pa)
            VP = sb("v_padded", [P, 2, 2, 4, P], ctx=pa)
            q0 = sb("q0", [P, 2, D], ctx=pa)
            W = sb("w_decayed", [P, 4, 2, 384], ctx=pa)

            s_ca = sem("a_consts")
            s_cx = [sem(f"a_ctx{i}") for i in range(2)]
            s_ks = sem("a_kernel_loaded")
            s_ms = sem("a_masks_loaded")
            s_vz = sem("a_vpad_zeroed")
            s_tm = sem("a_toeplitz_step")
            s_km = sem("a_k_ready")
            s_vp = sem("a_v_ready")
            s_q = sem("a_q_ready")
            s_a1 = sem("a_products_ready")
            s_w = sem("a_decayed_ready")
            s_a2 = sem("a_quads_done")
            s_xd = sem("a_residual_done")
            s_sd = sem("a_dve_step")
            NPAIR = NB * 8

            def pair_bank(n):
                return bank[n % 2]

            def acc_bank(b):
                return bk(4 + b % 2)[:, 0:D]

            with nc.Block() as block:
                @block.sync
                def _(sp):
                    for v in range(4):
                        src = bass.AP(kpad.tensor, kpad.offset + v * 384, [[1, P], [4 * 384, 4], [1, D]])
                        sp.dma_start(TM[:, v, :, 0:D], src).then_inc(s_ks, 16)
                    for i in range(2):
                        h = slice(8 * i, 8 * i + 8)
                        ht = slice(T // 2 * i, T // 2 * (i + 1))
                        sp.dma_start(cR[:, h, :], ctx_rev.rearrange("(b p) d -> p b d", p=P)[:, h, :]).then_inc(s_cx[i], 16)
                        sp.dma_start(cRT[:, :, ht], ctx_rev_t.rearrange("(c p) t -> p c t", p=P)[:, :, ht]).then_inc(s_cx[i], 16)

                @block.gpsimd
                def _(pool):
                    pool.memset(VP[:], 0.0).then_inc(s_vz, 1)

                @block.scalar
                def _(act):
                    act.dma_start(rowmask[:], rowmask_c).then_inc(s_ms, 16)
                    act.dma_start(anti[:], anti_c).then_inc(s_ca, 16)
                    act.dma_start(dbc[:], d_skip.partition_broadcast(P)).then_inc(s_ca, 16)
                    act.wait_ge(s_ms, 16)
                    act.wait_ge(s_vz, 1)

                    def operands(b, u):
                        act.wait_ge(s_a1, 8 * b + 8)
                        for v in range(4):
                            last = act.activation(KM[:, u, v, :], cR[:, bass.ds(b, 1), :].rearrange("p a d -> p (a d)"),
                                                  ACT.Copy, scale=rowmask[:, v:v + 1])
                        last.then_inc(s_km, 1)
                        act.wait_ge(s_a2, 4 * b + 4)
                        for blk in range(2):
                            dst = ap_of(VP[:, u, blk].rearrange("p a b -> p (a b)"), 0, [[P, 4], [40, 4], [1, 8]])
                            src = cRT[:, 1 - blk, bass.ds(b * P, P)].rearrange("p (g v i) -> p g v i", g=4, v=4)
                            last = act.activation(dst, src, ACT.Copy)
                        last.then_inc(s_vp, 1)

                    for i in range(2):
                        act.wait_ge(s_cx[i], 32)
                        with act.Fori(0, NB // 4) as j:
                            for u in range(2):
                                operands(8 * i + j * 2 + u, u)

                @block.tensor
                def _(pe):
                    pe.sem_inc(s_a1, 16)
                    pe.sem_inc(s_a2, 8)

                    def products(b, u, j):
                        n = 8 * b + j
                        if j == 0:
                            pe.wait_ge(s_km, b + 1)
                            pe.wait_ge(s_q, b + 1)
                        pe.wait_ge(s_w, n + 1)
                        v = j // 2
                        for hh in range(2):
                            g = 2 * (j % 2) + hh
                            r = slice(32 * g, 32 * g + 32)
                            o = bank[j % 2][:, hh, :]
                            pe.matmul(o[:, 0:D], KM[r, u, v, P:D], q0[r, u, :], start=True, stop=True)
                            last = pe.matmul(o[:, D:384], KM[r, u, v, 0:P], q0[r, u, P:D], start=True, stop=True)
                        last.then_inc(s_a1, 1)

                    def values(b, u, t):
                        pe.wait_ge(s_w, 2 + 8 * b + 2 * t + 2)
                        if t == 0:
                            pe.wait_ge(s_vp, b + 1)
                            pe.wait_ge(s_xd, b + 1)
                        for blk in range(2):
                            for g in range(4):
                                slot = (2 * t + g // 2) % 4
                                cols = slice(0, D) if blk == 0 else slice(P, D)
                                wc = slice(0, D) if blk == 0 else slice(D, 384)
                                last = pe.matmul(acc_bank(u)[32 * g:32 * g + 32, cols], VP[:, u, blk, g, 32 * t:32 * t + 32],
                                                 W[:, slot, g % 2, wc], start=(t == 0 and blk == 0),
                                                 stop=(t == 3 and blk == 1), skip_group_check=True)
                        last.then_inc(s_a2, 1)

                    def batch(b, u, has_next):
                        for t in range(4):
                            for j in (2 * t + 2, 2 * t + 3):
                                if j < 8:
                                    products(b, u, j)
                                elif has_next:
                                    products(b + 1, 1 - u, j - 8)
                            values(b, u, t)

                    products(0, 0, 0)
                    products(0, 0, 1)
                    with pe.Fori(0, NB // 2 - 1) as i:
                        for u in range(2):
                            batch(i * 2 + u, u, True)
                    batch(NB - 2, 0, True)
                    batch(NB - 1, 1, False)

                @block.vector
                def _(dve):
                    dve.sem_inc(s_w, 2)
                    dve.sem_inc(s_xd, 2)
                    dve.wait_ge(s_ks, 64)
                    dve.wait_ge(s_ca, 32)
                    tm = Steps(s_tm)
                    for v in range(4):
                        dv = dbc[:].rearrange("p (g v) -> p v g", v=4)[:, v, :]
                        n = tm.up(dve.tensor_tensor(dtmp[:], anti[:].unsqueeze(1).broadcast_to((P, 4, P)),
                                                    dv.unsqueeze(2).broadcast_to((P, 4, P)), ALU.mult))
                        dve.wait_ge(s_tm, n)
                        n = tm.up(dve.tensor_tensor(TM[:, v, :, 0:P], TM[:, v, :, 0:P], dtmp[:], ALU.add))
                        dve.wait_ge(s_tm, n)
                        tm.up(dve.tensor_copy(TM[:, v, :, D:384], TM[:, v, :, 0:P]))
                    dve.wait_ge(s_tm, tm.n)

                    def query(b, u):
                        dve.wait_ge(s_a1, 8 * b + 8)
                        xb = X[:, bass.ds(b, 1), :].rearrange("p a d -> p (a d)")
                        dve.tensor_scalar(q0[:, u, :], xb, mv[:, bass.ds(b, 1), 0:1].rearrange("p a d -> p (a d)"),
                                          rstd[:, bass.ds(b, 1)], ALU.subtract, ALU.mult).then_inc(s_q, 1)

                    def decay(b, u, j):
                        n = 8 * b + j
                        dve.wait_ge(s_a1, 16 + n + 1)
                        if j % 2 == 0:
                            dve.wait_ge(s_a2, 4 * b + j // 2 + 7)
                        v, g = j // 2, 2 * (j % 2)
                        dve.tensor_tensor(W[:, j % 4, :, :], bank[j % 2][:, :, 0:384], TM[:, v, g:g + 2, :],
                                          ALU.mult).then_inc(s_w, 1)

                    def residual(b, u):
                        dve.wait_ge(s_a2, 4 * b + 12)
                        xb = X[:, bass.ds(b, 1), :].rearrange("p a d -> p (a d)")
                        dve.scalar_tensor_tensor(xb, acc_bank(u), tg[:, 0:1], xb, ALU.mult, ALU.add).then_inc(s_xd, 1)
                        dve.wait_ge(s_xd, b + 3)
                        plain(dve)
                        dve.bn_stats(stats[:, bass.ds(b, 1), :].rearrange("p a d -> p (a d)"), xb).then_inc(s_sd, 1)

                    def batch(b, u, has_prev, has_next):
                        for j in range(8):
                            decay(b, u, j)
                            if j == 1 and has_prev:
                                residual(b - 1, 1 - u)
                            if j == 4 and has_next:
                                query(b + 1, 1 - u)

                    query(0, 0)
                    batch(0, 0, False, True)
                    batch(1, 1, True, True)
                    with dve.Fori(1, NB // 2 - 1) as i:
                        for u in range(2):
                            batch(i * 2 + u, u, True, True)
                    batch(NB - 2, 0, True, True)
                    batch(NB - 1, 1, True, False)
                    residual(NB - 1, 1)

        def feed_forward(tag, E, U, gated, rw, rbias, wu, gates, tgcol, route, final):
            WC = 768 if gated else 512
            HB = 2 if gated else 4
            LA = 1 if gated else 2
            WA = 2 if gated else 1
            YL = 0 if gated else 1
            NU = NBLK * U
            pf = ExitStack()
            with pf:
                xh = sb(f"xh{tag}", [P, 2, T], F32R, pf)
                xl = sb(f"xl{tag}", [P, 2, T], F32R, pf)
                pr = ExitStack()
                with pr:
                    xn = sb(f"xn{tag}", [P, BPB, D], F32, pr)
                    rwf = sb(f"rwf{tag}", [P, 2, E], F32, pr)
                    rwh = sb(f"rwh{tag}", [P, 2, E], F32R, pr)
                    rwl = sb(f"rwl{tag}", [P, 2, E], F32R, pr)
                    bias = sb(f"bias{tag}", [P, E], F32, pr)
                    lts = sb(f"lts{tag}", [E, BLK], F32, pr)
                    lg = sb(f"lg{tag}", [P, NB, E], F32, pr)
                    gt = sb(f"gt{tag}", [P, NB, U], F32, pr)
                    gts = sb(f"gts{tag}", [U, T], F32, pr)
                    s_v, s_r = rstd_part(tag)
                    s_ag = sem(f"{tag}_moments")
                    s_rl = sem(f"{tag}_router_loaded")
                    s_rw = sem(f"{tag}_router_split")
                    s_n = sem(f"{tag}_normed")
                    s_t = sem(f"{tag}_transposed")
                    s_h = sem(f"{tag}_hi_ready")
                    s_l = sem(f"{tag}_lo_ready")
                    s_lt = sem(f"{tag}_logits_t")
                    s_lc = sem(f"{tag}_logits_t_copied")
                    s_lg = sem(f"{tag}_logits")
                    s_lgc = sem(f"{tag}_logits_copied")
                    s_sg = sem(f"{tag}_sigmoid")
                    s_ro = sem(f"{tag}_route_step")
                    s_gt = sem(f"{tag}_gates_ready")
                    s_gT = sem(f"{tag}_gates_t")
                    s_gc = sem(f"{tag}_gates_t_copied")
                    s_gst = sem(f"{tag}_gates_stored")
                    rt = route(pr, tag, lg, gt, bias, s_ro, s_sg)
                    with nc.Block() as block:
                        @block.sync
                        def _(sp):
                            sp.dma_start(rwf[:], rw.rearrange("(c p) e -> p c e", p=P)).then_inc(s_rl, 16)
                            sp.dma_start(bias[:], rbias.partition_broadcast(P)).then_inc(s_rl, 16)
                            sp.wait_ge(s_gc, 4)
                            sp.dma_start(gates, gts[:]).then_inc(s_gst, 16)
                            sp.wait_ge(s_gst, 16)

                        @block.gpsimd
                        def _(pool):
                            pool.wait_ge(s_v, 1)
                            pool.tensor_tensor(rstd[:], vpe[:], mhalf[:], ALU.pow).then_inc(s_r, 1)

                        @block.tensor
                        def _(pe):
                            pe.sem_inc(s_t, 1)
                            pe.wait_ge(s_rw, 4)
                            with pe.Fori(0, NBLK) as k:
                                pe.wait_ge(s_n, k + 1)
                                pe.wait_ge(s_l, k + 1)
                                for c in range(2):
                                    for j in range(BPB):
                                        last = pe.transpose(bk(c)[:, j * P:(j + 1) * P], xn[:, j, c * P:(c + 1) * P], ident[:])
                                last.then_inc(s_t, 1)
                                pe.wait_ge(s_h, k + 1)
                                pe.wait_ge(s_l, k + 2)
                                m = 0
                                for c in range(2):
                                    for w_, x_ in ((rwh, xh), (rwh, xl), (rwl, xh)):
                                        last = pe.matmul(bk(2)[0:E, :], w_[:, c, :], x_[:, c, bass.ds(k * BLK, BLK)],
                                                         start=(m == 0), stop=(m == 5))
                                        m += 1
                                last.then_inc(s_lt, 1)
                                pe.wait_ge(s_lc, k + 1)
                                pe.wait_ge(s_lgc, k + 1)
                                plain(pe)
                                for j in range(BPB):
                                    last = pe.transpose(bk(3)[:, j * E:(j + 1) * E], lts[:, j * P:(j + 1) * P], ident[0:E, 0:E])
                                last.then_inc(s_lg, 1)
                            pe.wait_ge(s_gt, 1)
                            for b in range(NB):
                                last = pe.transpose(bk(4 + b // 4)[0:U, (b % 4) * P:(b % 4 + 1) * P], gt[:, b, :], ident[:])
                                if b % 4 == 3:
                                    last.then_inc(s_gT, 1)

                        @block.scalar
                        def _(act):
                            act.wait_ge(s_rl, 32)
                            act.activation(rwh[:].rearrange("p c e -> p (c e)"), rwf[:].rearrange("p c e -> p (c e)"), ACT.Copy).then_inc(s_rw, 1)
                            with act.Fori(0, NBLK) as k:
                                act.wait_ge(s_t, k + 2)
                                for c in range(2):
                                    last = act.activation(xh[:, c, bass.ds(k * BLK, BLK)], bk(c), ACT.Copy)
                                last.then_inc(s_h, 1)
                                act.wait_ge(s_lt, k + 1)
                                act.activation(lts[:], bk(2)[0:E, :], ACT.Copy).then_inc(s_lc, 1)
                            rt.scalar(act)
                            for i in range(4):
                                act.wait_ge(s_gT, i + 1)
                                act.activation(gts[:, i * BLK:(i + 1) * BLK], bk(4 + i)[0:U, :], ACT.Copy).then_inc(s_gc, 1)

                        @block.vector
                        def _(dve):
                            dve.sem_inc(s_l, 1)
                            dve.sem_inc(s_lgc, 1)
                            variances(dve, s_ag, 0, s_v)
                            dve.wait_ge(s_rw, 1)
                            dve.tensor_tensor(rwl[:], rwf[:], rwh[:].bitcast(F32), ALU.subtract).then_inc(s_rw, 3)
                            dve.wait_ge(s_r, 1)
                            with dve.Fori(0, NBLK) as k:
                                dve.wait_ge(s_t, k + 1)
                                for j in range(BPB):
                                    last = dve.tensor_scalar(xn[:, j, :], X[:, bass.ds(k * BPB + j, 1), :].rearrange("p a d -> p (a d)"),
                                                             mv[:, bass.ds(k * BPB + j, 1), 0:1].rearrange("p a d -> p (a d)"),
                                                             rstd[:, bass.ds(k * BPB + j, 1)], ALU.subtract, ALU.mult)
                                last.then_inc(s_n, 1)
                                dve.wait_ge(s_h, k + 1)
                                for c in range(2):
                                    last = dve.tensor_tensor(xl[:, c, bass.ds(k * BLK, BLK)], bk(c),
                                                             xh[:, c, bass.ds(k * BLK, BLK)].bitcast(F32), ALU.subtract)
                                last.then_inc(s_l, 1)
                                dve.wait_ge(s_lg, k + 1)
                                dve.tensor_copy(lg[:, bass.ds(k * BPB, BPB), :].rearrange("p b e -> p (b e)"),
                                                bk(3)[:, 0:BPB * E]).then_inc(s_lgc, 1)
                            dve.wait_ge(s_lgc, NBLK + 1)
                            rt.vector(dve, s_gt)

                wraw = sb(f"wraw{tag}", [P, S, WC], F32, pf)
                whi = sb(f"whi{tag}", [P, S, WC], F32R, pf)
                wlo = sb(f"wlo{tag}", [P, S, WC], F32R, pf)
                G = sb(f"G{tag}", [P, S, BLK], F32, pf)
                r = sb(f"r{tag}", [P, S, BLK], F32, pf)
                t = sb(f"t{tag}", [P, S, BLK], F32, pf)
                y = sb(f"y{tag}", [P, S, BLK], F32, pf)
                yhi = sb(f"yhi{tag}", [P, S, BLK], F32R, pf)
                ylo = sb(f"ylo{tag}", [P, S, BLK], F32R, pf)
                os_ = sb(f"os{tag}", [P, 2, BLK], F32, pf)
                s_wl = [sem(f"{tag}_w_loaded{i}") for i in range(S)]
                s_gl = [sem(f"{tag}_g_loaded{i}") for i in range(S)]
                s_wh = sem(f"{tag}_w_hi")
                s_wo = sem(f"{tag}_w_lo")
                s_hd = sem(f"{tag}_hidden")
                s_ac = sem(f"{tag}_activated")
                s_td = sem(f"{tag}_t_done")
                s_yd = sem(f"{tag}_y_done")
                s_yh = sem(f"{tag}_y_hi")
                s_yl = sem(f"{tag}_y_lo")
                s_od = sem(f"{tag}_unit_out")
                s_os = sem(f"{tag}_out_scaled")
                s_ot = sem(f"{tag}_out_t")
                s_xa = sem(f"{tag}_x_added")
                s_xs = sem(f"{tag}_x_step")
                s_fin = sem(f"{tag}_stored")

                def acc(blk):
                    return bank[2 + blk % 2]

                with nc.Block() as block:
                    def slot_value(blk, n, loop):
                        if loop is None:
                            return 16 * ((blk * U + n) // S + 1)
                        i, u = loop
                        return i * 16 + 16 * ((blk * U + u) // S + 1)

                    def walk(eng, unit, epilogue=None, after=1):
                        for blk in range(NBLK):
                            base = blk * U
                            groups = U // S - 2
                            for n in range(S):
                                unit(blk, base + n, n, (base + n) % S, slot_value(blk, n, None))
                                if n == after and blk > 0 and epilogue:
                                    epilogue(blk - 1)
                            with eng.Fori(1, 1 + groups) as i:
                                for u in range(S):
                                    unit(blk, i * S + (base + u), i * S + u, (base + u) % S, slot_value(blk, None, (i, u)))
                            for n in range((1 + groups) * S, U):
                                unit(blk, base + n, n, (base + n) % S, slot_value(blk, n, None))
                        if epilogue:
                            epilogue(NBLK - 1)

                    def is_int(v):
                        return isinstance(v, int)

                    @block.sync
                    def _(sp):
                        def unit(blk, N, n, slot, landed):
                            sp.wait_ge(s_wo, N + 1)
                            src = wu[n] if is_int(n) else wu[bass.ds(n, 1), :, :].rearrange("a p c -> (a p) c")
                            sp.dma_start(wraw[:, slot, :], src).then_inc(s_wl[slot], 16)
                            sp.wait_ge(s_yd, N + 1)
                            cols = slice(blk * BLK, (blk + 1) * BLK)
                            row = gates[n:n + 1, cols] if is_int(n) else gates[bass.ds(n, 1), cols]
                            sp.dma_start(G[:, slot, :], row.rearrange("a t -> (a t)").partition_broadcast(P)).then_inc(s_gl[slot], 16)

                        walk(sp, unit)
                        if final:
                            for blk in range(NBLK):
                                sp.wait_ge(s_xa, blk + 3)
                                sp.dma_start(out.rearrange("(b p) d -> p b d", p=P)[:, blk * BPB:(blk + 1) * BPB, :],
                                             X[:, blk * BPB:(blk + 1) * BPB, :]).then_inc(s_fin, 16)
                            sp.wait_ge(s_fin, 16 * NBLK)

                    @block.gpsimd
                    def _(pool):
                        pool.sem_inc(s_wo if gated else s_yd, S)

                        def mult(blk, N, n, slot, landed):
                            pool.wait_ge(s_td, N + S + 1)
                            pool.tensor_tensor(y[:, slot, :], t[:, slot, :], r[:, slot, :], ALU.mult).then_inc(s_yd, 1)

                        def w_lo(blk, N, n, slot, landed):
                            pool.wait_ge(s_wh, N + 1)
                            pool.tensor_tensor(wlo[:, slot, :], wraw[:, slot, :], whi[:, slot, :].bitcast(F32),
                                               ALU.subtract).then_inc(s_wo, 1)

                        walk(pool, w_lo if gated else mult)

                    @block.scalar
                    def _(act):
                        def w_hi(N, slot, landed):
                            act.wait_ge(s_wl[slot], landed)
                            act.wait_ge(s_od, N + 1)
                            act.activation(whi[:, slot, :], wraw[:, slot, :], ACT.Copy).then_inc(s_wh, 1)

                        def y_hi(N, slot):
                            act.wait_ge(s_yd, N + S + 1)
                            act.wait_ge(s_od, N + 1)
                            act.activation(yhi[:, slot, :], y[:, slot, :], ACT.Copy).then_inc(s_yh, 1)

                        def hidden(N, slot, hb):
                            act.wait_ge(s_hd, N + 1)
                            act.wait_ge(s_yd, N + 1)
                            if gated:
                                act.activation(r[:, slot, :], bank[hb][:, 0, :], ACT.Silu).then_inc(s_ac, 1)
                            else:
                                act.activation(r[:, slot, :], bk(hb), ACT.Relu).then_inc(s_ac, 1)

                        def unit(blk, N, n, slot, landed):
                            def weights():
                                if not (is_int(N) and N + WA >= NU):
                                    w_hi(N + WA, (slot + WA) % S, landed + 16 * ((slot + WA) // S))

                            if not gated:
                                weights()
                            hidden(N, slot, slot % HB)
                            if gated:
                                weights()
                            if YL == 0:
                                y_hi(N, slot)
                            elif not (is_int(N) and N == 0):
                                y_hi(N - 1, (slot - 1) % S)

                        def epilogue(blk):
                            if YL == 1 and blk == NBLK - 1:
                                y_hi(NU - 1, (NU - 1) % S)
                            act.wait_ge(s_od, S + (blk + 1) * U)
                            if blk > 0:
                                act.wait_ge(s_ot, blk)
                            for c in range(2):
                                last = act.activation(os_[:, c, :], acc(blk)[:, c, :], ACT.Copy, scale=tg[:, tgcol:tgcol + 1])
                            last.then_inc(s_os, 1)

                        for N in range(WA):
                            w_hi(N, N, 16)
                        walk(act, unit, epilogue)

                    @block.vector
                    def _(dve):
                        dve.sem_inc(s_yd if gated else s_wo, S)
                        dve.sem_inc(s_td, S)
                        dve.sem_inc(s_xa, 2)

                        def w_lo(N, slot):
                            dve.wait_ge(s_wh, N + 1)
                            dve.tensor_tensor(wlo[:, slot, :], wraw[:, slot, :], whi[:, slot, :].bitcast(F32),
                                              ALU.subtract).then_inc(s_wo, 1)

                        def y_lo(N, slot):
                            dve.wait_ge(s_yh, N + 1)
                            dve.tensor_tensor(ylo[:, slot, :], y[:, slot, :], yhi[:, slot, :].bitcast(F32),
                                              ALU.subtract).then_inc(s_yl, 1)

                        def unit(blk, N, n, slot, landed):
                            if not gated and not (is_int(N) and N + WA >= NU):
                                w_lo(N + WA, (slot + WA) % S)
                            dve.wait_ge(s_ac, N + 1)
                            dve.wait_ge(s_yd, N + 1)
                            if gated:
                                dve.tensor_tensor(t[:, slot, :], bank[slot % HB][:, 1, :], r[:, slot, :], ALU.mult).then_inc(s_td, 1)
                                dve.wait_ge(s_gl[slot], landed)
                                dve.wait_ge(s_td, N + S + 1)
                                dve.tensor_tensor(y[:, slot, :], t[:, slot, :], G[:, slot, :], ALU.mult).then_inc(s_yd, 1)
                            else:
                                dve.wait_ge(s_gl[slot], landed)
                                dve.tensor_tensor(t[:, slot, :], r[:, slot, :], G[:, slot, :], ALU.mult).then_inc(s_td, 1)
                            if YL == 0:
                                y_lo(N, slot)
                            elif not (is_int(N) and N == 0):
                                y_lo(N - 1, (slot - 1) % S)

                        def epilogue(blk):
                            if YL == 1 and blk == NBLK - 1:
                                y_lo(NU - 1, (NU - 1) % S)
                            dve.wait_ge(s_ot, blk + 1)
                            for i in range(2):
                                xv = X[:, blk * BPB + 2 * i:blk * BPB + 2 * i + 2, :].rearrange("p b d -> p (b d)")
                                last = dve.tensor_tensor(xv, acc(blk)[:, i, :], xv, ALU.add)
                            last.then_inc(s_xa, 1)
                            if not final:
                                dve.wait_ge(s_xa, blk + 3)
                                for b in range(blk * BPB, (blk + 1) * BPB):
                                    dve.bn_stats(stats[:, b, :], X[:, b, :]).then_inc(s_xs, 1)

                        for N in range(0 if gated else WA):
                            w_lo(N, N)
                        walk(dve, unit, epilogue, 2)

                    @block.tensor
                    def _(pe):
                        pe.sem_inc(s_od, S)

                        def h_prod(blk, N, slot):
                            pe.wait_ge(s_wo, S + N + 1)
                            if gated:
                                pe.wait_ge(s_td, N + S - HB + 1)
                            else:
                                pe.wait_ge(s_ac, N - HB + 1) if not (is_int(N) and N < HB) else None
                            xs = slice(blk * BLK, (blk + 1) * BLK)
                            for a in range(2 if gated else 1):
                                o = bank[slot % HB][:, a, :] if gated else bk(slot % HB)
                                m = 0
                                for c in range(2):
                                    wc = slice(a * D + c * P, a * D + (c + 1) * P)
                                    for w_, x_ in ((whi, xh), (whi, xl), (wlo, xh)):
                                        last = pe.matmul(o, w_[:, slot, wc], x_[:, c, xs], start=(m == 0), stop=(m == 5))
                                        m += 1
                            last.then_inc(s_hd, 1)

                        def o_prod(blk, N, n, slot):
                            pe.wait_ge(s_yl, N + 1)
                            first = is_int(n) and n == 0
                            end = is_int(n) and n == U - 1
                            if first:
                                pe.wait_ge(s_xa, blk + 1)
                            for c in range(2):
                                wc = slice(WC - D + c * P, WC - D + (c + 1) * P)
                                for m, (w_, y_) in enumerate(((whi, yhi), (whi, ylo), (wlo, yhi))):
                                    last = pe.matmul(acc(blk)[:, c, :], w_[:, slot, wc], y_[:, slot, :],
                                                     start=(first and m == 0), stop=(end and m == 2), skip_group_check=True)
                            last.then_inc(s_od, 1)

                        def unit(blk, N, n, slot, landed):
                            if not (is_int(N) and N + LA >= NU):
                                nxt = blk + 1 if is_int(n) and n + LA >= U else blk
                                h_prod(nxt, N + LA, (slot + LA) % S)
                            o_prod(blk, N, n, slot)

                        def epilogue(blk):
                            pe.wait_ge(s_os, blk + 1)
                            for j in range(BPB):
                                for c in range(2):
                                    last = pe.transpose(acc(blk)[:, j // 2, (j % 2) * D + c * P:(j % 2) * D + (c + 1) * P],
                                                        os_[:, c, j * P:(j + 1) * P], ident[:])
                            last.then_inc(s_ot, 1)

                        for N in range(LA):
                            h_prod(0, N, N)
                        walk(pe, unit, epilogue)

        class Route0:

            def __init__(self, ctx, tag, lg, gt, bias, s_ro, s_sg):
                self.lg, self.gt, self.bias, self.s, self.s_sg = lg, gt, bias, s_ro, s_sg
                self.sc = sb("sc0", [P, NB, E0], F32, ctx)
                self.pd = sb("pd0", [P, NB, E0 + 6], F32, ctx)
                self.rd = sb("rd0", [P, NB, E0 + 6], F32, ctx)
                self.m8 = sb("m80", [P, NB, 8], F32, ctx)
                self.wt = sb("wt0", [P, NB, E0], F32, ctx)
                self.sm = sb("sm0", [P, NB], F32, ctx)
                self.rc = sb("rc0", [P, NB], F32, ctx)

            def scalar(self, act):
                act.wait_ge(self.s, 1)
                act.activation(self.sc[:], self.lg[:], ACT.Sigmoid).then_inc(self.s_sg, 1)

            def vector(self, dve, s_gt):
                st = Steps(self.s)

                def step(ins):
                    dve.wait_ge(self.s, st.up(ins))

                st.up(dve.memset(self.pd[:], FILL))
                st.up(dve.memset(self.gt[:], 1.0))
                dve.wait_ge(self.s, st.n)
                dve.wait_ge(self.s_sg, 1)
                step(dve.tensor_tensor(self.pd[:, :, 0:E0], self.sc[:], self.bias[:].unsqueeze(1).broadcast_to((P, NB, E0)), ALU.add))
                top_k(dve, step, self.pd, self.rd, self.m8, E0, TOP0)
                step(dve.tensor_tensor(self.wt[:], self.rd[:, :, 0:E0], self.pd[:, :, 0:E0], ALU.not_equal))
                step(dve.tensor_tensor(self.wt[:], self.wt[:], self.sc[:], ALU.mult))
                step(dve.tensor_reduce(self.sm[:], self.wt[:], AX_X, ALU.add))
                step(dve.tensor_scalar(self.sm[:], self.sm[:], 1e-9, None, ALU.add))
                step(dve.reciprocal(self.rc[:], self.sm[:]))
                dve.tensor_tensor(self.gt[:, :, 0:E0], self.wt[:], self.rc[:].unsqueeze(2).broadcast_to((P, NB, E0)),
                                  ALU.mult).then_inc(s_gt, 1)

        def top_k(dve, step, pd, rd, m8, n, k):
            for b in range(NB):
                last = dve.max(m8[:, b, :], pd[:, b, 0:n])
            step(last)
            step(dve.memset(m8[:, :, k:8], FILL))
            for b in range(NB):
                last = dve.match_replace(rd[:, b, :], m8[:, b, :], pd[:, b, :], TAKEN)
            step(last)

        class Route1:

            def __init__(self, ctx, tag, lg, gt, bias, s_ro, s_sg):
                self.lg, self.gt, self.bias, self.s, self.s_sg = lg, gt, bias, s_ro, s_sg
                self.sc = sb("sc1", [P, NB, E1], F32, ctx)
                self.hi = [sb(f"hi1{i}", [P, NB, G1], F32, ctx) for i in range(2)]
                self.lo = [sb(f"lo1{i}", [P, NB, G1], F32, ctx) for i in range(2)]
                self.gd = sb("gd1", [P, NB, G1 + 8 - KG1], F32, ctx)
                self.gr = sb("gr1", [P, NB, G1 + 8 - KG1], F32, ctx)
                self.gm = sb("gm1", [P, NB, G1], F32, ctx)
                self.pd = sb("pd1", [P, NB, E1 + 8 - TOP1], F32, ctx)
                self.rd = sb("rd1", [P, NB, E1 + 8 - TOP1], F32, ctx)
                self.m8 = sb("m81", [P, NB, 8], F32, ctx)
                self.wt = sb("wt1", [P, NB, E1], F32, ctx)
                self.sm = sb("sm1", [P, NB], F32, ctx)
                self.rc = sb("rc1", [P, NB], F32, ctx)

            def scalar(self, act):
                act.wait_ge(self.s, 1)
                act.activation(self.sc[:], self.lg[:], ACT.Sigmoid).then_inc(self.s_sg, 1)

            def vector(self, dve, s_gt):
                st = Steps(self.s)

                def step(ins):
                    dve.wait_ge(self.s, st.up(ins))

                step(dve.tensor_tensor(self.lg[:], self.lg[:], self.bias[:].unsqueeze(1).broadcast_to((P, NB, E1)), ALU.add))
                st.up(dve.memset(self.pd[:], FILL))
                st.up(dve.memset(self.gd[:], FILL))
                st.up(dve.memset(self.gt[:], 1.0))
                dve.wait_ge(self.s, st.n)
                dve.wait_ge(self.s_sg, 1)
                q = self.sc[:].rearrange("p b (g k) -> p b g k", k=E1 // G1)
                for i in range(2):
                    a, c = q[:, :, :, 2 * i], q[:, :, :, 2 * i + 1]
                    st.up(dve.tensor_tensor(self.hi[i][:], a, c, ALU.max))
                    st.up(dve.tensor_tensor(self.lo[i][:], a, c, ALU.min))
                dve.wait_ge(self.s, st.n)
                for i in range(2):
                    st.up(dve.tensor_tensor(self.lo[i][:], self.lo[i][:], self.hi[i][:], ALU.add))
                st.up(dve.tensor_tensor(self.gm[:], self.hi[0][:], self.hi[1][:], ALU.add))
                dve.wait_ge(self.s, st.n)
                step(dve.tensor_tensor(self.lo[0][:], self.lo[0][:], self.lo[1][:], ALU.max))
                step(dve.tensor_tensor(self.gd[:, :, 0:G1], self.lo[0][:], self.gm[:], ALU.max))
                top_k(dve, step, self.gd, self.gr, self.m8, G1, KG1)
                step(dve.tensor_tensor(self.gm[:], self.gr[:, :, 0:G1], self.gd[:, :, 0:G1], ALU.not_equal))
                for k in range(E1 // G1):
                    last = dve.tensor_tensor(self.pd[:, :, 0:E1].rearrange("p b (g k) -> p b g k", k=E1 // G1)[:, :, :, k],
                                             q[:, :, :, k], self.gm[:], ALU.mult)
                step(last)
                top_k(dve, step, self.pd, self.rd, self.m8, E1, TOP1)
                step(dve.tensor_tensor(self.wt[:], self.rd[:, :, 0:E1], self.pd[:, :, 0:E1], ALU.not_equal))
                step(dve.tensor_tensor(self.wt[:], self.wt[:], self.sc[:], ALU.mult))
                step(dve.tensor_reduce(self.sm[:], self.wt[:], AX_X, ALU.add))
                step(dve.tensor_scalar(self.sm[:], self.sm[:], 1e-20, None, ALU.add))
                step(dve.reciprocal(self.rc[:], self.sm[:]))
                step(dve.tensor_tensor(self.wt[:], self.wt[:], self.rc[:].unsqueeze(2).broadcast_to((P, NB, E1)), ALU.mult))
                dve.tensor_scalar(self.gt[:, :, 0:E1], self.wt[:], ROUTE_SCALE, None, ALU.mult).then_inc(s_gt, 1)

        feed_forward("f0", E0, U0, True, rw0, eb0, wu0, gates0, 2, Route0, False)

        pc = ExitStack()
        with pc:
            V = sb("ctx_nat_sb", [P, NB, D], ctx=pc)
            KT = sb("ctx_nat_t_sb", [P, 2, T], ctx=pc)
            parity = sb("parity", [P, 2], ctx=pc)
            causal = sb("causal", [P, P], ctx=pc)
            KP = sb("k_parity", [P, 2, 2, 2, P], ctx=pc)
            Vb = sb("v_slot", [P, 2, D], ctx=pc)
            xn = sb("xn_c", [P, 2, D], ctx=pc)
            qT = sb("q_t", [P, 2, 2, P], ctx=pc)
            Sm = sb("s_masked", [P, 8, P], ctx=pc)
            nmax = sb("neg_max", [P, 2, NH1], ctx=pc)
            Pr = sb("probs", [P, 8, P], ctx=pc)
            den = sb("den", [P, 2, NH1], ctx=pc)
            rden = sb("rden", [P, 2, NH1], ctx=pc)
            PT = sb("probs_t", [P, 2, 4, P], ctx=pc)
            ov = sb("o_norm", [P, 2, D], ctx=pc)
            s_v, s_r = rstd_part("c")
            s_ag = sem("c_moments")
            s_cl = [sem(f"c_loaded{i}") for i in range(2)]
            s_cc = sem("c_consts")
            s_kp = sem("c_k_ready")
            s_n = sem("c_normed")
            s_xt = sem("c_x_t")
            s_qt = sem("c_q_ready")
            s_s = sem("c_scores")
            s_m = sem("c_masked")
            s_e = sem("c_exp")
            s_pt = sem("c_probs_t")
            s_pc = sem("c_probs_t_copied")
            s_pv = sem("c_quads_done")
            s_rd = sem("c_rden")
            s_xd = sem("c_residual")
            s_sd = sem("c_dve_step")

            with nc.Block() as block:
                @block.sync
                def _(sp):
                    sp.dma_start(parity[:], parity_c).then_inc(s_cc, 16)
                    sp.dma_start(causal[:], causal_c).then_inc(s_cc, 16)
                    for i in range(2):
                        h = slice(8 * i, 8 * i + 8)
                        ht = slice(T // 2 * i, T // 2 * (i + 1))
                        sp.dma_start(KT[:, :, ht], ctx_nat_t.rearrange("(c p) t -> p c t", p=P)[:, :, ht]).then_inc(s_cl[i], 16)
                        sp.dma_start(V[:, h, :], ctx_nat.rearrange("(b p) d -> p b d", p=P)[:, h, :]).then_inc(s_cl[i], 16)

                @block.gpsimd
                def _(pool):
                    pool.wait_ge(s_v, 1)
                    pool.tensor_tensor(rstd[:], vpe[:], mhalf[:], ALU.pow).then_inc(s_r, 1)

                    def operands(b, u):
                        pool.wait_ge(s_pv, 4 * b + 4)
                        for e in range(2):
                            last = pool.tensor_tensor(KP[:, u, :, e, :], KT[:, :, bass.ds(b * P, P)],
                                                      parity[:, e:e + 1].unsqueeze(2).broadcast_to((P, 2, P)), ALU.mult)
                        last.then_inc(s_kp, 1)

                    pool.wait_ge(s_cc, 32)
                    for i in range(2):
                        pool.wait_ge(s_cl[i], 32)
                        with pool.Fori(0, NB // 4) as j:
                            for u in range(2):
                                operands(8 * i + j * 2 + u, u)

                @block.tensor
                def _(pe):
                    pe.sem_inc(s_s, 16)
                    pe.sem_inc(s_pt, 2)
                    pe.sem_inc(s_pv, 8)

                    def queries(b, u):
                        pe.wait_ge(s_n, b + 1)
                        for c in range(2):
                            last = pe.transpose(bk(7)[:, c * P:(c + 1) * P], xn[:, u, c * P:(c + 1) * P], ident[:])
                        last.then_inc(s_xt, 1)

                    def scores(b, u, i):
                        if i == 0:
                            pe.wait_ge(s_kp, b + 1)
                            pe.wait_ge(s_qt, b + 1)
                        pe.wait_ge(s_m, 16 * b + 2 * i)
                        c, g = i // 4, i % 4
                        r_ = slice(32 * g, 32 * g + 32)
                        pe.matmul(bk(i % 4)[:, 0:2 * P], qT[r_, u, c, :], KP[r_, u, c, :, :].rearrange("p e k -> p (e k)"),
                                  start=True, stop=True).then_inc(s_s, 1)

                    def probs_t(b, u, t):
                        pe.wait_ge(s_pc, 4 * b + t + 1)
                        for h in range(4):
                            pe.wait_ge(s_e, 8 + 16 * b + 4 * t + h + 1)
                            last = pe.transpose(bk(4 + t % 2)[:, h * P:(h + 1) * P], Pr[:, (4 * t + h) % 8, :], ident[:])
                        last.then_inc(s_pt, 1)

                    def values(b, u, t):
                        pe.wait_ge(s_pc, 2 + 4 * b + t + 1)
                        if t == 0:
                            pe.wait_ge(s_xd, b + 2)
                        for h in range(4):
                            hc = (4 * t + h) * HD1
                            last = pe.matmul(bk(6)[:, hc:hc + HD1], PT[:, t % 2, h, :], Vs(b)[:, hc:hc + HD1],
                                             start=True, stop=True)
                        last.then_inc(s_pv, 1)

                    def Vs(b):
                        return V[:, bass.ds(b, 1), :].rearrange("p a d -> p (a d)")

                    def batch(b, u, has_next):
                        for t in range(4):
                            if t < 3:
                                scores(b, u, 2 * t + 2)
                                scores(b, u, 2 * t + 3)
                            elif has_next:
                                scores(b + 1, 1 - u, 0)
                                scores(b + 1, 1 - u, 1)
                            probs_t(b, u, t)
                            if t == 1 and has_next:
                                queries(b + 1, 1 - u)
                            values(b, u, t)

                    queries(0, 0)
                    scores(0, 0, 0)
                    scores(0, 0, 1)
                    with pe.Fori(0, NB // 2 - 1) as i:
                        for u in range(2):
                            batch(i * 2 + u, u, True)
                    batch(NB - 2, 0, True)
                    batch(NB - 1, 1, False)

                @block.scalar
                def _(act):
                    act.sem_inc(s_e, 8)

                    def batch(b, u):
                        for h in range(NH1):
                            act.wait_ge(s_m, 6 + 16 * b + h + 1)
                            if h % 4 == 0:
                                act.wait_ge(s_pt, 4 * b + h // 4 + 1)
                            act.activation(Pr[:, h % 8, :], Sm[:, h % 8, :], ACT.Exp, bias=nmax[:, u, h:h + 1], scale=-1.0,
                                           accum_out=den[:, u, h:h + 1]).then_inc(s_e, 1)

                    with act.Fori(0, NB // 2) as i:
                        for u in range(2):
                            batch(i * 2 + u, u)

                @block.vector
                def _(dve):
                    dve.sem_inc(s_m, 6)
                    dve.sem_inc(s_pc, 2)
                    dve.sem_inc(s_xd, 2)
                    variances(dve, s_ag, 0, s_v)
                    dve.wait_ge(s_r, 1)
                    dve.wait_ge(s_cc, 32)

                    def normed(b, u):
                        xb = X[:, bass.ds(b, 1), :].rearrange("p a d -> p (a d)")
                        dve.tensor_scalar(xn[:, u, :], xb, mv[:, bass.ds(b, 1), 0:1].rearrange("p a d -> p (a d)"),
                                          rstd[:, bass.ds(b, 1)], ALU.subtract, ALU.mult).then_inc(s_n, 1)

                    def q_copy(b, u):
                        dve.wait_ge(s_xt, b + 1)
                        dve.tensor_copy(qT[:, u, :, :].rearrange("p c k -> p (c k)"), bk(7)[:, 0:2 * P]).then_inc(s_qt, 1)

                    def masked(b, u, h):
                        if h % 2 == 0:
                            dve.wait_ge(s_s, 16 + 8 * b + h // 2 + 1)
                        dve.wait_ge(s_e, 16 * b + h + 1)
                        plain(dve)
                        dve.tensor_tensor_reduce(Sm[:, h % 8, :], bk((h // 2) % 4)[:, (h % 2) * P:(h % 2 + 1) * P], causal[:],
                                                 -SCALE1, 3.0e38, ALU.add, ALU.min, nmax[:, u, h:h + 1]).then_inc(s_m, 1)

                    def pt_copy(b, u, t):
                        dve.wait_ge(s_pt, 2 + 4 * b + t + 1)
                        dve.wait_ge(s_pv, 4 * b + t + 7)
                        dve.tensor_copy(PT[:, t % 2, :, :].rearrange("p h k -> p (h k)"), bk(4 + t % 2)).then_inc(s_pc, 1)

                    def residual(b, u):
                        n = 3 * b
                        dve.wait_ge(s_e, 8 + 16 * b + 16)
                        dve.reciprocal(rden[:, u, :], den[:, u, :]).then_inc(s_sd, 1)
                        dve.wait_ge(s_pv, 8 + 4 * b + 4)
                        dve.wait_ge(s_sd, n + 1)
                        dve.tensor_tensor(ov[:, u, :].rearrange("p (h d) -> p h d", d=HD1),
                                          bk(6)[:, 0:D].rearrange("p (h d) -> p h d", d=HD1),
                                          rden[:, u, :].unsqueeze(2).broadcast_to((P, NH1, HD1)), ALU.mult).then_inc(s_sd, 1)
                        dve.wait_ge(s_sd, n + 2)
                        xb = X[:, bass.ds(b, 1), :].rearrange("p a d -> p (a d)")
                        dve.scalar_tensor_tensor(xb, ov[:, u, :], tg[:, 1:2], xb, ALU.mult, ALU.add).then_inc(s_xd, 1)
                        dve.wait_ge(s_xd, b + 3)
                        plain(dve)
                        dve.bn_stats(stats[:, bass.ds(b, 1), :].rearrange("p a d -> p (a d)"), xb).then_inc(s_sd, 1)

                    def batch(b, u, has_next):
                        for t in range(4):
                            if t < 3:
                                for h in range(4 * t + 4, 4 * t + 8):
                                    masked(b, u, h)
                            elif has_next:
                                for h in range(4):
                                    masked(b + 1, 1 - u, h)
                            pt_copy(b, u, t)
                            if t == 0 and has_next:
                                normed(b + 1, 1 - u)
                            if t == 2 and has_next:
                                q_copy(b + 1, 1 - u)
                        residual(b, u)

                    normed(0, 0)
                    q_copy(0, 0)
                    for h in range(4):
                        masked(0, 0, h)
                    with dve.Fori(0, NB // 2 - 1) as i:
                        for u in range(2):
                            batch(i * 2 + u, u, True)
                    batch(NB - 2, 0, True)
                    batch(NB - 1, 1, False)

        feed_forward("f1", E1, U1, False, rw1, br1, wu1, gates1, 3, Route1, True)


def kernel(**inputs):
    import numpy as np
    import concourse.bacc as bacc
    from concourse.bass_utils import run_bass_kernel_spmd

    a = {k: np.asarray(v) for k, v in inputs.items()}
    x = a["x"].reshape(T, D)
    c = a["ctx_2048"].reshape(T, D)
    crev = np.ascontiguousarray(c[:, ::-1])
    kpad = np.zeros((NH0, 384), np.float32)
    kpad[:, P - 1:P - 1 + D] = a["L0_xattn_ssm_kernel"]

    def chunks(w):
        return w.T.reshape(2, P, P).transpose(1, 0, 2).reshape(P, 2 * P)

    sw1, sw2, sw3 = a["L0_ffn_sw1"], a["L0_ffn_sw2"], a["L0_ffn_sw3"]
    w12, w3 = a["L0_ffn_w12"], a["L0_ffn_w3"]
    wu0 = [np.concatenate([chunks(w12[e][:P]), chunks(w12[e][P:]), w3[e].T], 1) for e in range(E0)]
    wu0 += [np.concatenate([chunks(sw1[s:s + P]), chunks(sw2[s:s + P]), sw3[:, s:s + P].T], 1) for s in range(0, 1024, P)]
    W1, W2, Ws1, Ws2 = a["L1_ffn_W1"], a["L1_ffn_W2"], a["L1_ffn_Ws1"], a["L1_ffn_Ws2"]
    wu1 = [np.concatenate([chunks(W1[e]), W2[e].T], 1) for e in range(E1)]
    wu1 += [np.concatenate([chunks(Ws1[s:s + P]), Ws2[:, s:s + P].T], 1) for s in range(0, 256, P)]
    p = np.arange(P)
    arrays = {
        "x": x, "ctx_rev": crev, "ctx_rev_t": crev.T, "ctx_nat": c, "ctx_nat_t": c.T,
        "g_x": a["g_xattn"], "g_f": a["g_ffn"], "kpad": kpad, "d_skip": a["L0_xattn_D"],
        "wu0": np.stack(wu0), "rw0": a["L0_ffn_router_w"].T, "eb0": a["L0_ffn_expert_bias"],
        "wu1": np.stack(wu1), "rw1": a["L1_ffn_Wr"].T, "br1": a["L1_ffn_br"],
        "ident_c": np.eye(P, dtype=np.float32),
        "anti_c": np.ascontiguousarray(np.eye(P, dtype=np.float32)[::-1]),
        "rowmask_c": (p[:, None] // HD0 % 4 == np.arange(4)).astype(np.float32),
        "parity_c": (p[:, None] // HD1 % 2 == np.arange(2)).astype(np.float32),
        "causal_c": np.where(p[None, :] > p[:, None], np.float32(-1e30), np.float32(0)).astype(np.float32),
    }
    nc = bacc.Bacc("TRN2", target_bir_lowering=False, num_devices=1)
    feeds, aps = {}, []
    for name, v in arrays.items():
        v = np.ascontiguousarray(v)
        feeds[f"in_{name}"] = v
        aps.append(nc.dram_tensor(f"in_{name}", v.shape, mybir.dt.from_np(v.dtype), kind="ExternalInput").ap())
    aps.append(nc.dram_tensor("out_y", (T, D), F32, kind="ExternalOutput").ap())
    build(nc, *aps)
    r = run_bass_kernel_spmd(nc, [feeds], core_ids=[0])
    return r.results[0]["out_y"].reshape(NB, P, D)
```

```python
from contextlib import ExitStack

import concourse.bass as bass
from concourse import mybir

F32 = mybir.dt.float32
F32R = mybir.dt.float32r
BF16 = mybir.dt.bfloat16
ALU = mybir.AluOpType
ACT = mybir.ActivationFunctionType
AX_X = mybir.AxisListType.X

P = 128
NB = 16
D = 256
T = NB * P
NH0, HD0 = 16, 8
NH1, HD1 = 16, 16
E0, E1 = 8, 32
U0 = 1024 // P + E0
U1 = E1 + 256 // P
TOP0, TOP1, G1, KG1 = 2, 6, 8, 4
SCALE1 = HD1 ** -0.5
ROUTE_SCALE = 2.5
BLK = 512
NBLK = T // BLK
BPB = BLK // P
EPS = 1e-5
FILL = -1.0e30
TAKEN = -2.0e30
S = 4


class Steps:

    def __init__(self, sem, start=0):
        self.sem, self.n = sem, start

    def up(self, ins, by=1):
        ins.then_inc(self.sem, by)
        self.n += by
        return self.n


def ap_of(view, offset, dims):
    return bass.AP(view.tensor, view.offset + offset, [list(view.ap[0])] + dims)


def build(nc, x, ctx_rev, ctx_rev_t, ctx_nat, ctx_nat_t, g_x, g_f, kpad, d_skip, wu0, rw0, eb0, wu1, rw1, br1,
          ident_c, anti_c, identb_c, rowmask_c, headmask_c, causal_c, out):
    top = ExitStack()
    with top:
        def sb(name, shape, dt=F32, ctx=top):
            return ctx.enter_context(nc.sbuf_tensor(name, shape, dt))

        def sem(name):
            return top.enter_context(nc.semaphore(name))

        bank = [top.enter_context(nc.psum_tensor(f"bank{i}", [P, 2, 512], F32)) for i in range(4)]

        def bk(i):
            return bank[i // 2][:, i % 2, :]

        X = sb("X", [P, NB, D])
        mv = sb("mv", [P, NB, 2])
        rstd = sb("rstd", [P, NB])
        ident = sb("ident", [P, P])
        tg = sb("tg", [P, 4])
        stats = sb("stats", [P, NB, 6])
        mhalf = sb("mhalf", [P, NB])
        vpe = sb("vpe", [P, NB])

        gates0 = nc.dram_tensor("gates0", (U0, T), F32, kind="Internal").ap()
        gates1 = nc.dram_tensor("gates1", (U1, T), F32, kind="Internal").ap()

        s_x = [sem(f"x_loaded{i}") for i in range(4)]
        s_c = sem("identity_loaded")
        s_tl = sem("gates_loaded")
        s_tg = sem("gate_tanh")
        s_held = sem("held")
        s_st = sem("start_step")
        s_mh = sem("mhalf_set")
        s_ve0 = sem("var0_ready")
        s_rs = sem("rstd_ready")
        graw = sb("graw", [P, 4])

        def variances(dve, done, n, ready):
            for b in range(NB):
                last = dve.bn_aggr(mv[:, b, :], stats[:, b, :])
            last.then_inc(done, 1)
            dve.wait_ge(done, n + 1)
            dve.tensor_scalar(vpe[:], mv[:, :, 1], EPS, None, ALU.add).then_inc(ready, 1)

        def plain(eng):
            eng.sem_inc(s_held, 1)

        def rstd_part(phase):
            return sem(f"var_ready{phase}"), sem(f"rstd_ready{phase}")

        pa = ExitStack()
        with pa:
            KR = sb("k_rows", [P, 2, 4, D], ctx=pa)
            KA = sb("k_signed_hi", [P, 2, 4, D], F32R, pa)
            K4 = sb("k_terms", [P, 2, 4, D], F32R, pa)
            cRT = sb("ctx_rev_t_sb", [P, 2, T], ctx=pa)
            TM = sb("toeplitz", [P, 4, 4, 384], ctx=pa)
            dtmp = sb("d_diagonals", [P, 4, 4, P], ctx=pa)
            anti = sb("anti", [P, P], ctx=pa)
            dbc = sb("dbc", [P, NH0], ctx=pa)
            rowmask = sb("rowmask", [P, 6], ctx=pa)
            KM = sb("k_masked", [P, 2, 4, 4, D], F32R, pa)
            sel = sb("select", [P, 2, 4, P], F32R, pa)
            qf = sb("q_full", [P, 2, D], ctx=pa)
            qhi = sb("q_hi", [P, 2, D], F32R, pa)
            qlo = sb("q_lo", [P, 2, D], F32R, pa)
            Q4 = sb("q_terms", [P, 2, 4, D], F32R, pa)
            VP = sb("v_padded", [P, 2, 2, 4, P], ctx=pa)
            W = sb("w_decayed", [P, 4, 2, 384], ctx=pa)

            s_ca = sem("a_consts")
            s_cx = [sem(f"a_ctx{i}") for i in range(2)]
            s_ks = [sem(f"a_kernel_loaded{v}") for v in range(4)]
            s_ms = sem("a_masks_loaded")
            s_vz = sem("a_vpad_zeroed")
            s_tm = sem("a_toeplitz_step")
            s_kr = [sem(f"a_k_loaded{i}") for i in range(2)]
            s_sl = sem("a_select_ready")
            s_kh = sem("a_k_hi")
            s_kb = sem("a_k_share")
            s_k4 = sem("a_k_terms")
            s_km = sem("a_k_ready")
            s_qf = sem("a_q_full")
            s_qh = sem("a_q_hi")
            s_ql = sem("a_q_lo")
            s_qs = sem("a_q_selected")
            s_vp = sem("a_v_ready")
            s_q = sem("a_q_ready")
            s_a1 = sem("a_products_ready")
            s_w = sem("a_decayed_ready")
            s_a2 = sem("a_quads_done")
            s_xd = sem("a_residual_done")
            s_sd = sem("a_dve_step")
            NPAIR = NB * 8

            def pair_bank(n):
                return bank[n % 2]

            def acc_bank(b):
                return bk(4 + b % 2)[:, 0:D]

            with nc.Block() as block:
                @block.sync
                def _(sp):
                    def keys(start, u):
                        rows = ctx_rev[start, :].rearrange("(s r) d -> r s d", r=32)
                        for term in range(4):
                            sp.dma_start(KR[32 * term:32 * term + 32, u, :, :], rows).then_inc(s_kr[u], 16)

                    keys(slice(0, P), 0)
                    xv = x.rearrange("(b p) d -> p b d", p=P)
                    for i in range(4):
                        sp.dma_start(X[:, 4 * i:4 * i + 4, :], xv[:, 4 * i:4 * i + 4, :]).then_inc(s_x[i], 16)
                    for v in range(4):
                        src = bass.AP(kpad.tensor, kpad.offset + v * 384, [[1, P], [4 * 384, 4], [1, D]])
                        sp.dma_start(TM[:, v, :, 0:D], src).then_inc(s_ks[v], 16)
                    keys(slice(P, 2 * P), 1)
                    for i in range(2):
                        ht = slice(T // 2 * i, T // 2 * (i + 1))
                        sp.dma_start(cRT[:, :, ht], ctx_rev_t.rearrange("(c p) t -> p c t", p=P)[:, :, ht]).then_inc(s_cx[i], 16)
                    with sp.Fori(1, NB // 2) as i:
                        for u in range(2):
                            sp.wait_ge(s_k4, i * 2 + (u + 1))
                            keys(bass.ds(i * 2 * P + u * P, P), u)

                @block.gpsimd
                def _(pool):
                    pool.sem_inc(s_k4, 2)
                    pool.memset(mhalf[:], -0.5).then_inc(s_mh, 1)
                    pool.memset(VP[:], 0.0).then_inc(s_vz, 1)
                    pool.wait_ge(s_ms, 16)

                    def terms(b, u):
                        pool.wait_ge(s_kh, b + 1)
                        pool.wait_ge(s_km, b + 1)
                        raw = KR[:, u].rearrange("p s d -> p (s d)")
                        pool.tensor_tensor(raw, raw, rowmask[:, 5:6].broadcast_to((P, 4 * D)), ALU.mult).then_inc(s_kb, 1)
                        pool.wait_ge(s_kb, b + 1)
                        pool.tensor_tensor(K4[:, u].rearrange("p s d -> p (s d)"), raw,
                                           KA[:, u].rearrange("p s d -> p (s d)").bitcast(F32), ALU.add).then_inc(s_k4, 1)

                    terms(0, 0)
                    pool.wait_ge(s_mh, 1)
                    pool.wait_ge(s_ve0, 1)
                    pool.tensor_tensor(rstd[:], vpe[:], mhalf[:], ALU.pow).then_inc(s_rs, 1)
                    terms(1, 1)
                    with pool.Fori(1, NB // 2) as i:
                        for u in range(2):
                            terms(i * 2 + u, u)

                @block.scalar
                def _(act):
                    act.dma_start(rowmask[:], rowmask_c).then_inc(s_ms, 16)
                    act.dma_start(anti[:], anti_c).then_inc(s_ca, 16)
                    act.dma_start(dbc[:], d_skip.partition_broadcast(P)).then_inc(s_ca, 16)
                    act.dma_start(ident[:], ident_c).then_inc(s_c, 16)
                    act.dma_start(graw[:, 0:2], g_x.partition_broadcast(P)).then_inc(s_tl, 16)
                    act.dma_start(graw[:, 2:4], g_f.partition_broadcast(P)).then_inc(s_tl, 16)
                    act.sem_inc(s_km, 2)
                    act.wait_ge(s_ms, 16)
                    def k_hi(b, u, landed):
                        act.wait_ge(s_kr[u], landed)
                        act.wait_ge(s_k4, b + 1)
                        act.activation(KA[:, u].rearrange("p s d -> p (s d)"), KR[:, u].rearrange("p s d -> p (s d)"),
                                       ACT.Copy, scale=rowmask[:, 4:5]).then_inc(s_kh, 1)

                    def masks(b, u, vs):
                        for v in vs:
                            last = act.activation(KM[:, u, v].rearrange("p s d -> p (s d)"),
                                                  K4[:, u].rearrange("p s d -> p (s d)").bitcast(F32),
                                                  ACT.Copy, scale=rowmask[:, v:v + 1])
                        return last

                    def operands(b, u, landed, has_next=True, values_landed=None):
                        act.wait_ge(s_k4, b + 3)
                        act.wait_ge(s_a1, 8 * b + 8)
                        masks(b, u, (0, 1))
                        act.wait_ge(s_qf, b + 1)
                        act.wait_ge(s_qs, 2 * b + 2)
                        act.activation(qhi[:, u, :], qf[:, u, :], ACT.Copy).then_inc(s_qh, 1)
                        if has_next:
                            k_hi(b + 1, 1 - u, landed + 64 * u)
                        masks(b, u, (2, 3)).then_inc(s_km, 1)
                        for i in range(2):
                            act.wait_ge(s_qs, 2 * b + (5 + i))
                            act.activation(Q4[:, u, 2 * i:2 * i + 2].rearrange("p s d -> p (s d)"), bk(6 + i), ACT.Copy).then_inc(s_q, 1)
                        act.wait_ge(s_a2, 4 * b + 4)
                        if values_landed:
                            act.wait_ge(values_landed, 16)
                        for blk in range(2):
                            dst = ap_of(VP[:, u, blk].rearrange("p a b -> p (a b)"), 0, [[P, 4], [40, 4], [1, 8]])
                            src = cRT[:, 1 - blk, bass.ds(b * P, P)].rearrange("p (g v i) -> p g v i", g=4, v=4)
                            last = act.activation(dst, src, ACT.Copy)
                        last.then_inc(s_vp, 1)

                    k_hi(0, 0, 64)
                    act.wait_ge(s_c, 16)
                    act.activation(sel[:].rearrange("p a s m -> p (a s) m"), ident[:].unsqueeze(1).broadcast_to((P, 8, P)),
                                   ACT.Copy, scale=0.0).then_inc(s_sl, 1)
                    act.wait_ge(s_sl, 1)
                    for i in range(2):
                        for s in range(4):
                            act.activation(sel[:, i, s, 64 * i:64 * i + 64].rearrange("p (c r) -> p c r", c=2),
                                           ident[:, 32 * s:32 * s + 32].unsqueeze(1).broadcast_to((P, 2, 32)),
                                           ACT.Copy).then_inc(s_sl, 1)

                    act.wait_ge(s_tl, 32)
                    act.activation(tg[:], graw[:], ACT.Tanh).then_inc(s_tg, 1)
                    act.wait_ge(s_vz, 1)
                    operands(0, 0, 64, values_landed=s_cx[0])
                    operands(1, 1, 64)
                    for i in range(2):
                        if i:
                            act.wait_ge(s_cx[i], 16)
                        with act.Fori(1 - i, NB // 4 - i) as j:
                            for u in range(2):
                                operands(8 * i + j * 2 + u, u, j * 64 + (256 * i + 64))
                    operands(NB - 2, 0, 64 * (NB // 2))
                    operands(NB - 1, 1, 64 * (NB // 2), False)

                @block.tensor
                def _(pe):
                    pe.sem_inc(s_a1, 16)
                    pe.sem_inc(s_a2, 8)
                    pe.sem_inc(s_qs, 4)
                    pe.wait_ge(s_sl, 9)

                    def select(b, u, i):
                        pe.wait_ge(s_ql, b + 1)
                        pe.wait_ge(s_q, 2 * b + (i - 1)) if not isinstance(b, int) else None
                        for s in range(2):
                            o = bk(6 + i)[:, s * D:s * D + D]
                            pe.matmul(o, sel[:, 0, 2 * i + s, :], qhi[:, u, :], start=True, stop=False)
                            last = pe.matmul(o, sel[:, 1, 2 * i + s, :], qlo[:, u, :], start=False, stop=True)
                        last.then_inc(s_qs, 1)

                    def products(b, u, j):
                        n = 8 * b + j
                        if j == 0:
                            pe.wait_ge(s_km, b + 3)
                        if j < 2:
                            pe.wait_ge(s_q, 2 * b + (j + 1))
                        pe.wait_ge(s_w, n + 1)
                        v = j // 2
                        for hh in range(2):
                            g = 2 * (j % 2) + hh
                            o = bank[j % 2][:, hh, :]
                            pe.matmul(o[:, 0:D], KM[:, u, v, g, P:D], Q4[:, u, g, :], start=True, stop=True)
                            last = pe.matmul(o[:, D:384], KM[:, u, v, g, 0:P], Q4[:, u, g, P:D], start=True, stop=True)
                        last.then_inc(s_a1, 1)

                    def values(b, u, t):
                        pe.wait_ge(s_w, 2 + 8 * b + 2 * t + 2)
                        if t == 0:
                            pe.wait_ge(s_vp, b + 1)
                            pe.wait_ge(s_xd, b + 1)
                        for blk in range(2):
                            for g in range(4):
                                slot = (2 * t + g // 2) % 4
                                cols = slice(0, D) if blk == 0 else slice(P, D)
                                wc = slice(0, D) if blk == 0 else slice(D, 384)
                                last = pe.matmul(acc_bank(u)[32 * g:32 * g + 32, cols], VP[:, u, blk, g, 32 * t:32 * t + 32],
                                                 W[:, slot, g % 2, wc], start=(t == 0 and blk == 0),
                                                 stop=(t == 3 and blk == 1), skip_group_check=True)
                        last.then_inc(s_a2, 1)

                    def batch(b, u, has_next):
                        for t in range(4):
                            for j in (2 * t + 2, 2 * t + 3):
                                if j < 8:
                                    products(b, u, j)
                                elif has_next:
                                    products(b + 1, 1 - u, j - 8)
                                if j in (4, 6) and has_next:
                                    select(b + 1, 1 - u, (j - 4) // 2)
                            values(b, u, t)

                    select(0, 0, 0)
                    select(0, 0, 1)
                    products(0, 0, 0)
                    products(0, 0, 1)
                    with pe.Fori(0, NB // 2 - 1) as i:
                        for u in range(2):
                            batch(i * 2 + u, u, True)
                    batch(NB - 2, 0, True)
                    batch(NB - 1, 1, False)

                @block.vector
                def _(dve):
                    dve.sem_inc(s_w, 2)
                    dve.sem_inc(s_xd, 2)
                    st = Steps(s_st)
                    for b in range(NB):
                        if b % 4 == 0:
                            dve.wait_ge(s_x[b // 4], 16)
                        st.up(dve.bn_stats(stats[:, b, :], X[:, b, :]))
                    dve.wait_ge(s_st, st.n)
                    variances(dve, s_st, st.n, s_ve0)

                    def query(b, u):
                        dve.wait_ge(s_qs, 2 * b + 2)
                        xb = X[:, bass.ds(b, 1), :].rearrange("p a d -> p (a d)")
                        dve.tensor_scalar(qf[:, u, :], xb, mv[:, bass.ds(b, 1), 0:1].rearrange("p a d -> p (a d)"),
                                          rstd[:, bass.ds(b, 1)], ALU.subtract, ALU.mult).then_inc(s_qf, 1)

                    def query_lo(b, u):
                        dve.wait_ge(s_qh, b + 1)
                        dve.tensor_tensor(qlo[:, u, :], qf[:, u, :], qhi[:, u, :].bitcast(F32), ALU.subtract).then_inc(s_ql, 1)

                    def decay(b, u, j):
                        n = 8 * b + j
                        dve.wait_ge(s_a1, 16 + n + 1)
                        if j % 2 == 0:
                            dve.wait_ge(s_a2, 4 * b + j // 2 + 7)
                        v, g = j // 2, 2 * (j % 2)
                        dve.tensor_tensor(W[:, j % 4, :, :], bank[j % 2][:, :, 0:384], TM[:, v, g:g + 2, :],
                                          ALU.mult).then_inc(s_w, 1)

                    def residual(b, u):
                        dve.wait_ge(s_a2, 4 * b + 12)
                        xb = X[:, bass.ds(b, 1), :].rearrange("p a d -> p (a d)")
                        dve.scalar_tensor_tensor(xb, acc_bank(u), tg[:, 0:1], xb, ALU.mult, ALU.add).then_inc(s_xd, 1)

                    def moments(b):
                        dve.wait_ge(s_xd, b + 3)
                        plain(dve)
                        xb = X[:, bass.ds(b, 1), :].rearrange("p a d -> p (a d)")
                        dve.bn_stats(stats[:, bass.ds(b, 1), :].rearrange("p a d -> p (a d)"), xb).then_inc(s_sd, 1)

                    def batch(b, u, has_prev, has_next):
                        for j in range(8):
                            decay(b, u, j)
                            if j == 1 and has_prev:
                                residual(b - 1, 1 - u)
                            if j == 0 and has_next:
                                query(b + 1, 1 - u)
                            if j == 2 and has_next:
                                query_lo(b + 1, 1 - u)
                            if j == 2 and has_prev:
                                moments(b - 1)

                    dve.wait_ge(s_ca, 32)
                    tm = Steps(s_tm)
                    for v in range(4):
                        dv = dbc[:].rearrange("p (g v) -> p v g", v=4)[:, v, :]
                        tm.up(dve.tensor_tensor(dtmp[:, v], anti[:].unsqueeze(1).broadcast_to((P, 4, P)),
                                                dv.unsqueeze(2).broadcast_to((P, 4, P)), ALU.mult))
                    dve.wait_ge(s_rs, 1)
                    query(0, 0)
                    for v in range(4):
                        dve.wait_ge(s_ks[v], 16)
                        if v == 0:
                            dve.wait_ge(s_tm, tm.n)
                        tm.up(dve.tensor_tensor(TM[:, v, :, 0:P], TM[:, v, :, 0:P], dtmp[:, v], ALU.add))
                    query_lo(0, 0)
                    dve.wait_ge(s_tm, tm.n)
                    for v in range(4):
                        tm.up(dve.tensor_copy(TM[:, v, :, D:384], TM[:, v, :, 0:P]))
                    dve.wait_ge(s_tm, tm.n)
                    dve.wait_ge(s_tg, 1)
                    batch(0, 0, False, True)
                    batch(1, 1, True, True)
                    with dve.Fori(1, NB // 2 - 1) as i:
                        for u in range(2):
                            batch(i * 2 + u, u, True, True)
                    batch(NB - 2, 0, True, True)
                    batch(NB - 1, 1, True, False)
                    residual(NB - 1, 1)
                    moments(NB - 1)

        def feed_forward(tag, E, U, gated, rw, rbias, wu, gates, tgcol, route, final):
            WC = 768 if gated else 512
            HB = 2 if gated else 4
            LA = 1 if gated else 2
            WA = 2 if gated else 1
            YL = 0 if gated else 1
            NU = NBLK * U
            pf = ExitStack()
            with pf:
                xh = sb(f"xh{tag}", [P, 2, T], F32R, pf)
                xl = sb(f"xl{tag}", [P, 2, T], F32R, pf)
                pr = ExitStack()
                with pr:
                    xn = sb(f"xn{tag}", [P, BPB, D], F32, pr)
                    rwf = sb(f"rwf{tag}", [P, 2, E], F32, pr)
                    rwh = sb(f"rwh{tag}", [P, 2, E], F32R, pr)
                    rwl = sb(f"rwl{tag}", [P, 2, E], F32R, pr)
                    bias = sb(f"bias{tag}", [P, E], F32, pr)
                    lts = sb(f"lts{tag}", [E, BLK], F32, pr)
                    lg = sb(f"lg{tag}", [P, NB, E], F32, pr)
                    gt = sb(f"gt{tag}", [P, NB, U], F32, pr)
                    gts = sb(f"gts{tag}", [U, T], F32, pr)
                    s_v, s_r = rstd_part(tag)
                    s_ag = sem(f"{tag}_moments")
                    s_rl = sem(f"{tag}_router_loaded")
                    s_rw = sem(f"{tag}_router_split")
                    s_n = sem(f"{tag}_normed")
                    s_t = sem(f"{tag}_transposed")
                    s_h = sem(f"{tag}_hi_ready")
                    s_l = sem(f"{tag}_lo_ready")
                    s_lt = sem(f"{tag}_logits_t")
                    s_lc = sem(f"{tag}_logits_t_copied")
                    s_lg = sem(f"{tag}_logits")
                    s_lgc = sem(f"{tag}_logits_copied")
                    s_sg = sem(f"{tag}_sigmoid")
                    s_ro = sem(f"{tag}_route_step")
                    s_gt = sem(f"{tag}_gates_ready")
                    s_gT = sem(f"{tag}_gates_t")
                    s_gc = sem(f"{tag}_gates_t_copied")
                    s_gst = sem(f"{tag}_gates_stored")
                    rt = route(pr, tag, lg, gt, bias, s_ro, s_sg)
                    with nc.Block() as block:
                        @block.sync
                        def _(sp):
                            sp.dma_start(rwf[:], rw.rearrange("(c p) e -> p c e", p=P)).then_inc(s_rl, 16)
                            sp.dma_start(bias[:], rbias.partition_broadcast(P)).then_inc(s_rl, 16)
                            sp.wait_ge(s_gc, 4)
                            sp.dma_start(gates, gts[:]).then_inc(s_gst, 16)
                            sp.wait_ge(s_gst, 16)

                        @block.gpsimd
                        def _(pool):
                            pool.wait_ge(s_v, 1)
                            pool.tensor_tensor(rstd[:], vpe[:], mhalf[:], ALU.pow).then_inc(s_r, 1)

                        @block.tensor
                        def _(pe):
                            pe.sem_inc(s_t, 1)
                            pe.wait_ge(s_rw, 4)
                            with pe.Fori(0, NBLK) as k:
                                pe.wait_ge(s_n, k + 1)
                                pe.wait_ge(s_l, k + 1)
                                for c in range(2):
                                    for j in range(BPB):
                                        last = pe.transpose(bk(c)[:, j * P:(j + 1) * P], xn[:, j, c * P:(c + 1) * P], ident[:])
                                last.then_inc(s_t, 1)
                                pe.wait_ge(s_h, k + 1)
                                pe.wait_ge(s_l, k + 2)
                                m = 0
                                for c in range(2):
                                    for w_, x_ in ((rwh, xh), (rwh, xl), (rwl, xh)):
                                        last = pe.matmul(bk(2)[0:E, :], w_[:, c, :], x_[:, c, bass.ds(k * BLK, BLK)],
                                                         start=(m == 0), stop=(m == 5))
                                        m += 1
                                last.then_inc(s_lt, 1)
                                pe.wait_ge(s_lc, k + 1)
                                pe.wait_ge(s_lgc, k + 1)
                                plain(pe)
                                for j in range(BPB):
                                    last = pe.transpose(bk(3)[:, j * E:(j + 1) * E], lts[:, j * P:(j + 1) * P], ident[0:E, 0:E])
                                last.then_inc(s_lg, 1)
                            pe.wait_ge(s_gt, 1)
                            for b in range(NB):
                                last = pe.transpose(bk(4 + b // 4)[0:U, (b % 4) * P:(b % 4 + 1) * P], gt[:, b, :], ident[:])
                                if b % 4 == 3:
                                    last.then_inc(s_gT, 1)

                        @block.scalar
                        def _(act):
                            act.wait_ge(s_rl, 32)
                            act.activation(rwh[:].rearrange("p c e -> p (c e)"), rwf[:].rearrange("p c e -> p (c e)"), ACT.Copy).then_inc(s_rw, 1)
                            with act.Fori(0, NBLK) as k:
                                act.wait_ge(s_t, k + 2)
                                for c in range(2):
                                    last = act.activation(xh[:, c, bass.ds(k * BLK, BLK)], bk(c), ACT.Copy)
                                last.then_inc(s_h, 1)
                                act.wait_ge(s_lt, k + 1)
                                act.activation(lts[:], bk(2)[0:E, :], ACT.Copy).then_inc(s_lc, 1)
                            rt.scalar(act)
                            for i in range(4):
                                act.wait_ge(s_gT, i + 1)
                                act.activation(gts[:, i * BLK:(i + 1) * BLK], bk(4 + i)[0:U, :], ACT.Copy).then_inc(s_gc, 1)

                        @block.vector
                        def _(dve):
                            dve.sem_inc(s_l, 1)
                            dve.sem_inc(s_lgc, 1)
                            variances(dve, s_ag, 0, s_v)
                            dve.wait_ge(s_rw, 1)
                            dve.tensor_tensor(rwl[:], rwf[:], rwh[:].bitcast(F32), ALU.subtract).then_inc(s_rw, 3)
                            dve.wait_ge(s_r, 1)
                            with dve.Fori(0, NBLK) as k:
                                dve.wait_ge(s_t, k + 1)
                                for j in range(BPB):
                                    last = dve.tensor_scalar(xn[:, j, :], X[:, bass.ds(k * BPB + j, 1), :].rearrange("p a d -> p (a d)"),
                                                             mv[:, bass.ds(k * BPB + j, 1), 0:1].rearrange("p a d -> p (a d)"),
                                                             rstd[:, bass.ds(k * BPB + j, 1)], ALU.subtract, ALU.mult)
                                last.then_inc(s_n, 1)
                                dve.wait_ge(s_h, k + 1)
                                for c in range(2):
                                    last = dve.tensor_tensor(xl[:, c, bass.ds(k * BLK, BLK)], bk(c),
                                                             xh[:, c, bass.ds(k * BLK, BLK)].bitcast(F32), ALU.subtract)
                                last.then_inc(s_l, 1)
                                dve.wait_ge(s_lg, k + 1)
                                dve.tensor_copy(lg[:, bass.ds(k * BPB, BPB), :].rearrange("p b e -> p (b e)"),
                                                bk(3)[:, 0:BPB * E]).then_inc(s_lgc, 1)
                            dve.wait_ge(s_lgc, NBLK + 1)
                            rt.vector(dve, s_gt)

                wraw = sb(f"wraw{tag}", [P, S, WC], F32, pf)
                whi = sb(f"whi{tag}", [P, S, WC], F32R, pf)
                wlo = sb(f"wlo{tag}", [P, S, WC], F32R, pf)
                G = sb(f"G{tag}", [P, S, BLK], F32, pf)
                r = sb(f"r{tag}", [P, S, BLK], F32, pf)
                t = sb(f"t{tag}", [P, S, BLK], F32, pf)
                y = sb(f"y{tag}", [P, S, BLK], F32, pf)
                yhi = sb(f"yhi{tag}", [P, S, BLK], F32R, pf)
                ylo = sb(f"ylo{tag}", [P, S, BLK], F32R, pf)
                os_ = sb(f"os{tag}", [P, 2, BLK], F32, pf)
                s_wl = [sem(f"{tag}_w_loaded{i}") for i in range(S)]
                s_gl = [sem(f"{tag}_g_loaded{i}") for i in range(S)]
                s_wh = sem(f"{tag}_w_hi")
                s_wo = sem(f"{tag}_w_lo")
                s_hd = sem(f"{tag}_hidden")
                s_ac = sem(f"{tag}_activated")
                s_td = sem(f"{tag}_t_done")
                s_yd = sem(f"{tag}_y_done")
                s_yh = sem(f"{tag}_y_hi")
                s_yl = sem(f"{tag}_y_lo")
                s_od = sem(f"{tag}_unit_out")
                s_os = sem(f"{tag}_out_scaled")
                s_ot = sem(f"{tag}_out_t")
                s_xa = sem(f"{tag}_x_added")
                s_xs = sem(f"{tag}_x_step")
                s_fin = sem(f"{tag}_stored")

                def acc(blk):
                    return bank[2 + blk % 2]

                with nc.Block() as block:
                    def slot_value(blk, n, loop):
                        if loop is None:
                            return 16 * ((blk * U + n) // S + 1)
                        i, u = loop
                        return i * 16 + 16 * ((blk * U + u) // S + 1)

                    def walk(eng, unit, epilogue=None, after=1):
                        for blk in range(NBLK):
                            base = blk * U
                            groups = U // S - 2
                            for n in range(S):
                                unit(blk, base + n, n, (base + n) % S, slot_value(blk, n, None))
                                if n == after and blk > 0 and epilogue:
                                    epilogue(blk - 1)
                            with eng.Fori(1, 1 + groups) as i:
                                for u in range(S):
                                    unit(blk, i * S + (base + u), i * S + u, (base + u) % S, slot_value(blk, None, (i, u)))
                            for n in range((1 + groups) * S, U):
                                unit(blk, base + n, n, (base + n) % S, slot_value(blk, n, None))
                        if epilogue:
                            epilogue(NBLK - 1)

                    def is_int(v):
                        return isinstance(v, int)

                    @block.sync
                    def _(sp):
                        def unit(blk, N, n, slot, landed):
                            sp.wait_ge(s_wo, N + 1)
                            src = wu[n] if is_int(n) else wu[bass.ds(n, 1), :, :].rearrange("a p c -> (a p) c")
                            sp.dma_start(wraw[:, slot, :], src).then_inc(s_wl[slot], 16)
                            sp.wait_ge(s_yd, N + 1)
                            cols = slice(blk * BLK, (blk + 1) * BLK)
                            row = gates[n:n + 1, cols] if is_int(n) else gates[bass.ds(n, 1), cols]
                            sp.dma_start(G[:, slot, :], row.rearrange("a t -> (a t)").partition_broadcast(P)).then_inc(s_gl[slot], 16)

                        walk(sp, unit)
                        if final:
                            for blk in range(NBLK):
                                sp.wait_ge(s_xa, blk + 3)
                                sp.dma_start(out.rearrange("(b p) d -> p b d", p=P)[:, blk * BPB:(blk + 1) * BPB, :],
                                             X[:, blk * BPB:(blk + 1) * BPB, :]).then_inc(s_fin, 16)
                            sp.wait_ge(s_fin, 16 * NBLK)

                    @block.gpsimd
                    def _(pool):
                        pool.sem_inc(s_wo if gated else s_yd, S)

                        def mult(blk, N, n, slot, landed):
                            pool.wait_ge(s_td, N + S + 1)
                            pool.tensor_tensor(y[:, slot, :], t[:, slot, :], r[:, slot, :], ALU.mult).then_inc(s_yd, 1)

                        def w_lo(blk, N, n, slot, landed):
                            pool.wait_ge(s_wh, N + 1)
                            pool.tensor_tensor(wlo[:, slot, :], wraw[:, slot, :], whi[:, slot, :].bitcast(F32),
                                               ALU.subtract).then_inc(s_wo, 1)

                        walk(pool, w_lo if gated else mult)

                    @block.scalar
                    def _(act):
                        def w_hi(N, slot, landed):
                            act.wait_ge(s_wl[slot], landed)
                            act.wait_ge(s_od, N + 1)
                            act.activation(whi[:, slot, :], wraw[:, slot, :], ACT.Copy).then_inc(s_wh, 1)

                        def y_hi(N, slot):
                            act.wait_ge(s_yd, N + S + 1)
                            act.wait_ge(s_od, N + 1)
                            act.activation(yhi[:, slot, :], y[:, slot, :], ACT.Copy).then_inc(s_yh, 1)

                        def hidden(N, slot, hb):
                            act.wait_ge(s_hd, N + 1)
                            act.wait_ge(s_yd, N + 1)
                            if gated:
                                act.activation(r[:, slot, :], bank[hb][:, 0, :], ACT.Silu).then_inc(s_ac, 1)
                            else:
                                act.activation(r[:, slot, :], bk(hb), ACT.Relu).then_inc(s_ac, 1)

                        def unit(blk, N, n, slot, landed):
                            def weights():
                                if not (is_int(N) and N + WA >= NU):
                                    w_hi(N + WA, (slot + WA) % S, landed + 16 * ((slot + WA) // S))

                            if not gated:
                                weights()
                            hidden(N, slot, slot % HB)
                            if gated:
                                weights()
                            if YL == 0:
                                y_hi(N, slot)
                            elif not (is_int(N) and N == 0):
                                y_hi(N - 1, (slot - 1) % S)

                        def epilogue(blk):
                            if YL == 1 and blk == NBLK - 1:
                                y_hi(NU - 1, (NU - 1) % S)
                            act.wait_ge(s_od, S + (blk + 1) * U)
                            if blk > 0:
                                act.wait_ge(s_ot, blk)
                            for c in range(2):
                                last = act.activation(os_[:, c, :], acc(blk)[:, c, :], ACT.Copy, scale=tg[:, tgcol:tgcol + 1])
                            last.then_inc(s_os, 1)

                        for N in range(WA):
                            w_hi(N, N, 16)
                        walk(act, unit, epilogue)

                    @block.vector
                    def _(dve):
                        dve.sem_inc(s_yd if gated else s_wo, S)
                        dve.sem_inc(s_td, S)
                        dve.sem_inc(s_xa, 2)

                        def w_lo(N, slot):
                            dve.wait_ge(s_wh, N + 1)
                            dve.tensor_tensor(wlo[:, slot, :], wraw[:, slot, :], whi[:, slot, :].bitcast(F32),
                                              ALU.subtract).then_inc(s_wo, 1)

                        def y_lo(N, slot):
                            dve.wait_ge(s_yh, N + 1)
                            dve.tensor_tensor(ylo[:, slot, :], y[:, slot, :], yhi[:, slot, :].bitcast(F32),
                                              ALU.subtract).then_inc(s_yl, 1)

                        def unit(blk, N, n, slot, landed):
                            if not gated and not (is_int(N) and N + WA >= NU):
                                w_lo(N + WA, (slot + WA) % S)
                            dve.wait_ge(s_ac, N + 1)
                            dve.wait_ge(s_yd, N + 1)
                            if gated:
                                dve.tensor_tensor(t[:, slot, :], bank[slot % HB][:, 1, :], r[:, slot, :], ALU.mult).then_inc(s_td, 1)
                                dve.wait_ge(s_gl[slot], landed)
                                dve.wait_ge(s_td, N + S + 1)
                                dve.tensor_tensor(y[:, slot, :], t[:, slot, :], G[:, slot, :], ALU.mult).then_inc(s_yd, 1)
                            else:
                                dve.wait_ge(s_gl[slot], landed)
                                dve.tensor_tensor(t[:, slot, :], r[:, slot, :], G[:, slot, :], ALU.mult).then_inc(s_td, 1)
                            if YL == 0:
                                y_lo(N, slot)
                            elif not (is_int(N) and N == 0):
                                y_lo(N - 1, (slot - 1) % S)

                        def epilogue(blk):
                            if YL == 1 and blk == NBLK - 1:
                                y_lo(NU - 1, (NU - 1) % S)
                            dve.wait_ge(s_ot, blk + 1)
                            for i in range(2):
                                xv = X[:, blk * BPB + 2 * i:blk * BPB + 2 * i + 2, :].rearrange("p b d -> p (b d)")
                                last = dve.tensor_tensor(xv, acc(blk)[:, i, :], xv, ALU.add)
                            last.then_inc(s_xa, 1)
                            if not final:
                                dve.wait_ge(s_xa, blk + 3)
                                for b in range(blk * BPB, (blk + 1) * BPB):
                                    dve.bn_stats(stats[:, b, :], X[:, b, :]).then_inc(s_xs, 1)

                        for N in range(0 if gated else WA):
                            w_lo(N, N)
                        walk(dve, unit, epilogue, 2)

                    @block.tensor
                    def _(pe):
                        pe.sem_inc(s_od, S)

                        def h_prod(blk, N, slot):
                            pe.wait_ge(s_wo, S + N + 1)
                            if gated:
                                pe.wait_ge(s_td, N + S - HB + 1)
                            else:
                                pe.wait_ge(s_ac, N - HB + 1) if not (is_int(N) and N < HB) else None
                            xs = slice(blk * BLK, (blk + 1) * BLK)
                            for a in range(2 if gated else 1):
                                o = bank[slot % HB][:, a, :] if gated else bk(slot % HB)
                                m = 0
                                for c in range(2):
                                    wc = slice(a * D + c * P, a * D + (c + 1) * P)
                                    for w_, x_ in ((whi, xh), (whi, xl), (wlo, xh)):
                                        last = pe.matmul(o, w_[:, slot, wc], x_[:, c, xs], start=(m == 0), stop=(m == 5))
                                        m += 1
                            last.then_inc(s_hd, 1)

                        def o_prod(blk, N, n, slot):
                            pe.wait_ge(s_yl, N + 1)
                            first = is_int(n) and n == 0
                            end = is_int(n) and n == U - 1
                            if first:
                                pe.wait_ge(s_xa, blk + 1)
                            for c in range(2):
                                wc = slice(WC - D + c * P, WC - D + (c + 1) * P)
                                for m, (w_, y_) in enumerate(((whi, yhi), (whi, ylo), (wlo, yhi))):
                                    last = pe.matmul(acc(blk)[:, c, :], w_[:, slot, wc], y_[:, slot, :],
                                                     start=(first and m == 0), stop=(end and m == 2), skip_group_check=True)
                            last.then_inc(s_od, 1)

                        def unit(blk, N, n, slot, landed):
                            if not (is_int(N) and N + LA >= NU):
                                nxt = blk + 1 if is_int(n) and n + LA >= U else blk
                                h_prod(nxt, N + LA, (slot + LA) % S)
                            o_prod(blk, N, n, slot)

                        def epilogue(blk):
                            pe.wait_ge(s_os, blk + 1)
                            for j in range(BPB):
                                for c in range(2):
                                    last = pe.transpose(acc(blk)[:, j // 2, (j % 2) * D + c * P:(j % 2) * D + (c + 1) * P],
                                                        os_[:, c, j * P:(j + 1) * P], ident[:])
                            last.then_inc(s_ot, 1)

                        for N in range(LA):
                            h_prod(0, N, N)
                        walk(pe, unit, epilogue)

        class Route0:

            def __init__(self, ctx, tag, lg, gt, bias, s_ro, s_sg):
                self.lg, self.gt, self.bias, self.s, self.s_sg = lg, gt, bias, s_ro, s_sg
                self.sc = sb("sc0", [P, NB, E0], F32, ctx)
                self.pd = sb("pd0", [P, NB, E0 + 6], F32, ctx)
                self.rd = sb("rd0", [P, NB, E0 + 6], F32, ctx)
                self.m8 = sb("m80", [P, NB, 8], F32, ctx)
                self.wt = sb("wt0", [P, NB, E0], F32, ctx)
                self.sm = sb("sm0", [P, NB], F32, ctx)
                self.rc = sb("rc0", [P, NB], F32, ctx)

            def scalar(self, act):
                act.wait_ge(self.s, 1)
                act.activation(self.sc[:], self.lg[:], ACT.Sigmoid).then_inc(self.s_sg, 1)

            def vector(self, dve, s_gt):
                st = Steps(self.s)

                def step(ins):
                    dve.wait_ge(self.s, st.up(ins))

                st.up(dve.memset(self.pd[:], FILL))
                st.up(dve.memset(self.gt[:], 1.0))
                dve.wait_ge(self.s, st.n)
                dve.wait_ge(self.s_sg, 1)
                step(dve.tensor_tensor(self.pd[:, :, 0:E0], self.sc[:], self.bias[:].unsqueeze(1).broadcast_to((P, NB, E0)), ALU.add))
                top_k(dve, step, self.pd, self.rd, self.m8, E0, TOP0)
                step(dve.tensor_tensor(self.wt[:], self.rd[:, :, 0:E0], self.pd[:, :, 0:E0], ALU.not_equal))
                step(dve.tensor_tensor(self.wt[:], self.wt[:], self.sc[:], ALU.mult))
                step(dve.tensor_reduce(self.sm[:], self.wt[:], AX_X, ALU.add))
                step(dve.tensor_scalar(self.sm[:], self.sm[:], 1e-9, None, ALU.add))
                step(dve.reciprocal(self.rc[:], self.sm[:]))
                dve.tensor_tensor(self.gt[:, :, 0:E0], self.wt[:], self.rc[:].unsqueeze(2).broadcast_to((P, NB, E0)),
                                  ALU.mult).then_inc(s_gt, 1)

        def top_k(dve, step, pd, rd, m8, n, k):
            for b in range(NB):
                last = dve.max(m8[:, b, :], pd[:, b, 0:n])
            step(last)
            step(dve.memset(m8[:, :, k:8], FILL))
            for b in range(NB):
                last = dve.match_replace(rd[:, b, :], m8[:, b, :], pd[:, b, :], TAKEN)
            step(last)

        class Route1:

            def __init__(self, ctx, tag, lg, gt, bias, s_ro, s_sg):
                self.lg, self.gt, self.bias, self.s, self.s_sg = lg, gt, bias, s_ro, s_sg
                self.sc = sb("sc1", [P, NB, E1], F32, ctx)
                self.hi = [sb(f"hi1{i}", [P, NB, G1], F32, ctx) for i in range(2)]
                self.lo = [sb(f"lo1{i}", [P, NB, G1], F32, ctx) for i in range(2)]
                self.gd = sb("gd1", [P, NB, G1 + 8 - KG1], F32, ctx)
                self.gr = sb("gr1", [P, NB, G1 + 8 - KG1], F32, ctx)
                self.gm = sb("gm1", [P, NB, G1], F32, ctx)
                self.pd = sb("pd1", [P, NB, E1 + 8 - TOP1], F32, ctx)
                self.rd = sb("rd1", [P, NB, E1 + 8 - TOP1], F32, ctx)
                self.m8 = sb("m81", [P, NB, 8], F32, ctx)
                self.wt = sb("wt1", [P, NB, E1], F32, ctx)
                self.sm = sb("sm1", [P, NB], F32, ctx)
                self.rc = sb("rc1", [P, NB], F32, ctx)

            def scalar(self, act):
                act.wait_ge(self.s, 1)
                act.activation(self.sc[:], self.lg[:], ACT.Sigmoid).then_inc(self.s_sg, 1)

            def vector(self, dve, s_gt):
                st = Steps(self.s)

                def step(ins):
                    dve.wait_ge(self.s, st.up(ins))

                step(dve.tensor_tensor(self.lg[:], self.lg[:], self.bias[:].unsqueeze(1).broadcast_to((P, NB, E1)), ALU.add))
                st.up(dve.memset(self.pd[:], FILL))
                st.up(dve.memset(self.gd[:], FILL))
                st.up(dve.memset(self.gt[:], 1.0))
                dve.wait_ge(self.s, st.n)
                dve.wait_ge(self.s_sg, 1)
                q = self.sc[:].rearrange("p b (g k) -> p b g k", k=E1 // G1)
                for i in range(2):
                    a, c = q[:, :, :, 2 * i], q[:, :, :, 2 * i + 1]
                    st.up(dve.tensor_tensor(self.hi[i][:], a, c, ALU.max))
                    st.up(dve.tensor_tensor(self.lo[i][:], a, c, ALU.min))
                dve.wait_ge(self.s, st.n)
                for i in range(2):
                    st.up(dve.tensor_tensor(self.lo[i][:], self.lo[i][:], self.hi[i][:], ALU.add))
                st.up(dve.tensor_tensor(self.gm[:], self.hi[0][:], self.hi[1][:], ALU.add))
                dve.wait_ge(self.s, st.n)
                step(dve.tensor_tensor(self.lo[0][:], self.lo[0][:], self.lo[1][:], ALU.max))
                step(dve.tensor_tensor(self.gd[:, :, 0:G1], self.lo[0][:], self.gm[:], ALU.max))
                top_k(dve, step, self.gd, self.gr, self.m8, G1, KG1)
                step(dve.tensor_tensor(self.gm[:], self.gr[:, :, 0:G1], self.gd[:, :, 0:G1], ALU.not_equal))
                for k in range(E1 // G1):
                    last = dve.tensor_tensor(self.pd[:, :, 0:E1].rearrange("p b (g k) -> p b g k", k=E1 // G1)[:, :, :, k],
                                             q[:, :, :, k], self.gm[:], ALU.mult)
                step(last)
                top_k(dve, step, self.pd, self.rd, self.m8, E1, TOP1)
                step(dve.tensor_tensor(self.wt[:], self.rd[:, :, 0:E1], self.pd[:, :, 0:E1], ALU.not_equal))
                step(dve.tensor_tensor(self.wt[:], self.wt[:], self.sc[:], ALU.mult))
                step(dve.tensor_reduce(self.sm[:], self.wt[:], AX_X, ALU.add))
                step(dve.tensor_scalar(self.sm[:], self.sm[:], 1e-20, None, ALU.add))
                step(dve.reciprocal(self.rc[:], self.sm[:]))
                step(dve.tensor_tensor(self.wt[:], self.wt[:], self.rc[:].unsqueeze(2).broadcast_to((P, NB, E1)), ALU.mult))
                dve.tensor_scalar(self.gt[:, :, 0:E1], self.wt[:], ROUTE_SCALE, None, ALU.mult).then_inc(s_gt, 1)

        feed_forward("f0", E0, U0, True, rw0, eb0, wu0, gates0, 2, Route0, False)

        pc = ExitStack()
        with pc:
            KT = sb("ctx_nat_t_sb", [P, 2, T], ctx=pc)
            headmask = sb("headmask", [P, 8], ctx=pc)
            causal = sb("causal", [P, 4, P], BF16, pc)
            identb = sb("identb", [P, P], BF16, pc)
            KP = sb("k_heads", [P, 2, 2, 8, P], ctx=pc)
            V = sb("v_slot", [P, 2, D + HD1], ctx=pc)
            xn = sb("xn_c", [P, 2, D], ctx=pc)
            rstdq = sb("rstd_scaled", [P, NB], ctx=pc)
            qT = sb("q_t", [P, 2, 2, P], ctx=pc)
            nmax = sb("neg_max", [P, 2, NH1], ctx=pc)
            Pr = sb("probs", [P, 8, P], ctx=pc)
            den = sb("den", [P, 2, NH1], ctx=pc)
            rden = sb("rden", [P, 2, NH1], ctx=pc)
            PT = sb("probs_t", [P, 2, 4, P], ctx=pc)
            oT = sb("o_t", [P, 4, P], ctx=pc)
            ov = sb("o_norm", [P, D], ctx=pc)
            s_v, s_r = rstd_part("c")
            s_ag = sem("c_moments")
            s_cl = [sem(f"c_k_loaded{i}") for i in range(2)]
            s_vl = [sem(f"c_v_loaded{i}") for i in range(2)]
            s_vz = sem("c_v_pad_zeroed")
            s_cc = sem("c_consts")
            s_kp = sem("c_k_ready")
            s_n = sem("c_normed")
            s_xt = sem("c_x_t")
            s_qt = sem("c_q_ready")
            s_s = sem("c_scores")
            s_m = sem("c_max")
            s_e = sem("c_exp")
            s_pt = sem("c_probs_t")
            s_pc = sem("c_probs_t_copied")
            s_pv = sem("c_quads_done")
            s_oe = sem("c_out_t_copied")
            s_ot = sem("c_out_ready")
            s_xd = sem("c_residual")
            s_sd = sem("c_dve_step")
            s_rq = sem("c_rstd_scaled")

            def batches(eng, batch):
                batch(0, 0, False, True)
                batch(1, 1, True, True)
                with eng.Fori(1, NB // 2 - 1) as i:
                    for u in range(2):
                        batch(i * 2 + u, u, True, True)
                batch(NB - 2, 0, True, True)
                batch(NB - 1, 1, True, False)

            with nc.Block() as block:
                @block.sync
                def _(sp):
                    sp.dma_start(headmask[:], headmask_c).then_inc(s_cc, 16)
                    sp.dma_start(causal[:], causal_c).then_inc(s_cc, 16)
                    sp.dma_start(identb[:], identb_c).then_inc(s_cc, 16)
                    for i in range(2):
                        ht = slice(T // 2 * i, T // 2 * (i + 1))
                        sp.dma_start(KT[:, :, ht], ctx_nat_t.rearrange("(c p) t -> p c t", p=P)[:, :, ht]).then_inc(s_cl[i], 16)
                    with sp.Fori(0, NB // 2) as i:
                        for u in range(2):
                            sp.wait_ge(s_pv, 8 * i + (4 * u + 4))
                            sp.dma_start(V[:, u, 0:D], ctx_nat[bass.ds(i * 2 * P + u * P, P), :]).then_inc(s_vl[u], 16)

                @block.gpsimd
                def _(pool):
                    pool.memset(V[:, :, D:D + HD1], 0.0).then_inc(s_vz, 1)
                    pool.wait_ge(s_v, 1)
                    pool.tensor_tensor(rstd[:], vpe[:], mhalf[:], ALU.pow).then_inc(s_r, 1)

                    def operands(b, u):
                        pool.wait_ge(s_s, 4 * b + 4)
                        for c in range(2):
                            last = pool.tensor_tensor(KP[:, u, c, :, :], KT[:, c, bass.ds(b * P, P)].unsqueeze(1).broadcast_to((P, 8, P)),
                                                      headmask[:].unsqueeze(2).broadcast_to((P, 8, P)), ALU.mult)
                        last.then_inc(s_kp, 1)

                    pool.wait_ge(s_cc, 48)
                    for i in range(2):
                        pool.wait_ge(s_cl[i], 16)
                        with pool.Fori(0, NB // 4) as j:
                            for u in range(2):
                                operands(8 * i + j * 2 + u, u)

                @block.tensor
                def _(pe):
                    pe.sem_inc(s_s, 8)
                    pe.sem_inc(s_xt, 2)
                    pe.sem_inc(s_pt, 2)
                    pe.sem_inc(s_pv, 8)
                    pe.sem_inc(s_ot, 1)
                    pe.wait_ge(s_cc, 48)
                    pe.wait_ge(s_vz, 1)

                    def queries(b, u, first=False):
                        pe.wait_ge(s_n, b + 1)
                        if not first:
                            pe.wait_ge(s_xd, b)
                        for c in range(2):
                            last = pe.transpose(bk(7)[:, c * P:(c + 1) * P], xn[:, u, c * P:(c + 1) * P], ident[:])
                        last.then_inc(s_xt, 1)

                    def scores(b, u, t):
                        if t == 0:
                            pe.wait_ge(s_kp, b + 1)
                            pe.wait_ge(s_qt, b + 1)
                        pe.wait_ge(s_e, 16 * b + 4 * t + 4)
                        pe.matmul(bk(t), identb[:], causal[:].rearrange("p h k -> p (h k)"), start=True, stop=False)
                        h = 4 * (t % 2)
                        pe.matmul(bk(t), qT[:, u, t // 2, :], KP[:, u, t // 2, h:h + 4, :].rearrange("p h k -> p (h k)"),
                                  start=False, stop=True).then_inc(s_s, 1)

                    def probs_t(b, u, t):
                        pe.wait_ge(s_pc, 4 * b + t + 1)
                        for h in range(4):
                            pe.wait_ge(s_e, 16 + 16 * b + 4 * t + h + 1)
                            last = pe.transpose(bk(4 + t % 2)[:, h * P:(h + 1) * P], Pr[:, (4 * t + h) % 8, :], ident[:])
                        last.then_inc(s_pt, 1)

                    def values(b, u, t, loads):
                        pe.wait_ge(s_pc, 2 + 4 * b + t + 1)
                        if t == 0:
                            pe.wait_ge(s_oe, b + 1)
                            pe.wait_ge(s_vl[u], loads)
                        for g in range(4):
                            hc = (4 * t + g) * HD1
                            last = pe.matmul(bk(6)[32 * g:32 * g + 32, t * P:(t + 1) * P], V[:, u, hc:hc + 32], PT[:, t % 2, g, :],
                                             start=True, stop=True, skip_group_check=True)
                        last.then_inc(s_pv, 1)

                    def out_rows(b, copied):
                        pe.wait_ge(s_oe, b + 2)
                        copied()
                        for t in range(4):
                            last = pe.transpose(bk(7)[:, t * P:(t + 1) * P], oT[:, t, :], ident[:])
                        last.then_inc(s_ot, 1)

                    def loads_of(b, u):
                        return 8 * b + (16 - 8 * u)

                    def batch(b, u, has_prev, has_next):
                        scores(b, u, 2)
                        probs_t(b, u, 0)
                        if has_next:
                            queries(b + 1, 1 - u, first=not has_prev)
                        if has_prev:
                            values(b - 1, 1 - u, 3, None)
                        scores(b, u, 3)
                        probs_t(b, u, 1)
                        values(b, u, 0, loads_of(b, u))
                        if has_next:
                            scores(b + 1, 1 - u, 0)
                        probs_t(b, u, 2)
                        if has_prev:
                            out_rows(b - 1, lambda: pe.wait_ge(s_qt, b + 2 if has_next else NB))
                        values(b, u, 1, None)
                        if has_next:
                            scores(b + 1, 1 - u, 1)
                        probs_t(b, u, 3)
                        values(b, u, 2, None)

                    queries(0, 0, first=True)
                    scores(0, 0, 0)
                    scores(0, 0, 1)
                    batches(pe, batch)
                    values(NB - 1, 1, 3, None)
                    out_rows(NB - 1, lambda: pe.wait_ge(s_xd, NB + 1))

                @block.scalar
                def _(act):
                    act.sem_inc(s_e, 16)
                    act.sem_inc(s_oe, 1)

                    def probs(b, u, t):
                        act.wait_ge(s_m, 4 * b + t + 1)
                        act.wait_ge(s_pt, 4 * b + t + 1)
                        for g in range(4):
                            h = 4 * t + g
                            act.activation(Pr[:, h % 8, :], bk(t)[:, g * P:(g + 1) * P], ACT.Exp, bias=nmax[:, u, h:h + 1],
                                           accum_out=den[:, u, h:h + 1]).then_inc(s_e, 1)

                    def out_copy(b):
                        act.wait_ge(s_pv, 8 + 4 * b + 4)
                        act.wait_ge(s_ot, b + 1)
                        act.activation(oT[:].rearrange("p t q -> p (t q)"), bk(6), ACT.Copy).then_inc(s_oe, 1)

                    def batch(b, u, has_prev, has_next):
                        for t in range(4):
                            probs(b, u, t)
                            if t == 1 and has_prev:
                                out_copy(b - 1)

                    batches(act, batch)
                    out_copy(NB - 1)

                @block.vector
                def _(dve):
                    dve.sem_inc(s_pc, 2)
                    dve.sem_inc(s_xd, 2)
                    variances(dve, s_ag, 0, s_v)
                    dve.wait_ge(s_r, 1)
                    dve.tensor_scalar(rstdq[:], rstd[:], SCALE1, None, ALU.mult).then_inc(s_rq, 1)
                    dve.wait_ge(s_rq, 1)

                    def normed(b, u):
                        dve.wait_ge(s_xt, b + 1)
                        xb = X[:, bass.ds(b, 1), :].rearrange("p a d -> p (a d)")
                        dve.tensor_scalar(xn[:, u, :], xb, mv[:, bass.ds(b, 1), 0:1].rearrange("p a d -> p (a d)"),
                                          rstdq[:, bass.ds(b, 1)], ALU.subtract, ALU.mult).then_inc(s_n, 1)

                    def q_copy(b, u):
                        dve.wait_ge(s_xt, b + 3)
                        dve.tensor_copy(qT[:, u, :, :].rearrange("p c k -> p (c k)"), bk(7)[:, 0:2 * P]).then_inc(s_qt, 1)

                    def maxima(b, u, t):
                        dve.wait_ge(s_s, 8 + 4 * b + t + 1)
                        dve.tensor_reduce(nmax[:, u, 4 * t:4 * t + 4], bk(t).rearrange("p (h k) -> p h k", k=P), AX_X, ALU.max,
                                          negate=True).then_inc(s_m, 1)

                    def pt_copy(b, u, t):
                        dve.wait_ge(s_pt, 2 + 4 * b + t + 1)
                        dve.wait_ge(s_pv, 4 * b + t + 7)
                        dve.tensor_copy(PT[:, t % 2, :, :].rearrange("p h k -> p (h k)"), bk(4 + t % 2)).then_inc(s_pc, 1)

                    def inverse(b, u):
                        dve.wait_ge(s_e, 16 + 16 * b + 16)
                        dve.reciprocal(rden[:, u, :], den[:, u, :]).then_inc(s_sd, 1)

                    def residual(b, u):
                        n = 3 * b
                        dve.wait_ge(s_ot, b + 2)
                        dve.wait_ge(s_sd, n + 1)
                        dve.tensor_tensor(ov[:].rearrange("p (h d) -> p h d", d=HD1),
                                          bk(7).rearrange("p (h d) -> p h d", d=32)[:, :, 0:HD1],
                                          rden[:, u, :].unsqueeze(2).broadcast_to((P, NH1, HD1)), ALU.mult).then_inc(s_sd, 1)
                        dve.wait_ge(s_sd, n + 2)
                        xb = X[:, bass.ds(b, 1), :].rearrange("p a d -> p (a d)")
                        dve.scalar_tensor_tensor(xb, ov[:], tg[:, 1:2], xb, ALU.mult, ALU.add).then_inc(s_xd, 1)
                        dve.wait_ge(s_xd, b + 3)
                        plain(dve)
                        dve.bn_stats(stats[:, bass.ds(b, 1), :].rearrange("p a d -> p (a d)"), xb).then_inc(s_sd, 1)

                    def batch(b, u, has_prev, has_next):
                        if has_next:
                            normed(b + 1, 1 - u)
                        maxima(b, u, 2)
                        pt_copy(b, u, 0)
                        if has_next:
                            q_copy(b + 1, 1 - u)
                        maxima(b, u, 3)
                        if has_prev:
                            inverse(b - 1, 1 - u)
                        pt_copy(b, u, 1)
                        if has_next:
                            maxima(b + 1, 1 - u, 0)
                        pt_copy(b, u, 2)
                        if has_next:
                            maxima(b + 1, 1 - u, 1)
                        if has_prev:
                            residual(b - 1, 1 - u)
                        pt_copy(b, u, 3)

                    normed(0, 0)
                    q_copy(0, 0)
                    maxima(0, 0, 0)
                    maxima(0, 0, 1)
                    batches(dve, batch)
                    inverse(NB - 1, 1)
                    residual(NB - 1, 1)

        feed_forward("f1", E1, U1, False, rw1, br1, wu1, gates1, 3, Route1, True)


def kernel(**inputs):
    import numpy as np
    import concourse.bacc as bacc
    from concourse.bass_utils import run_bass_kernel_spmd

    a = {k: np.asarray(v) for k, v in inputs.items()}
    x = a["x"].reshape(T, D)
    c = a["ctx_2048"].reshape(T, D)
    crev = np.ascontiguousarray(c[:, ::-1])
    kpad = np.zeros((NH0, 384), np.float32)
    kpad[:, P - 1:P - 1 + D] = a["L0_xattn_ssm_kernel"]

    def chunks(w):
        return w.T.reshape(2, P, P).transpose(1, 0, 2).reshape(P, 2 * P)

    sw1, sw2, sw3 = a["L0_ffn_sw1"], a["L0_ffn_sw2"], a["L0_ffn_sw3"]
    w12, w3 = a["L0_ffn_w12"], a["L0_ffn_w3"]
    wu0 = [np.concatenate([chunks(w12[e][:P]), chunks(w12[e][P:]), w3[e].T], 1) for e in range(E0)]
    wu0 += [np.concatenate([chunks(sw1[s:s + P]), chunks(sw2[s:s + P]), sw3[:, s:s + P].T], 1) for s in range(0, 1024, P)]
    W1, W2, Ws1, Ws2 = a["L1_ffn_W1"], a["L1_ffn_W2"], a["L1_ffn_Ws1"], a["L1_ffn_Ws2"]
    wu1 = [np.concatenate([chunks(W1[e]), W2[e].T], 1) for e in range(E1)]
    wu1 += [np.concatenate([chunks(Ws1[s:s + P]), Ws2[:, s:s + P].T], 1) for s in range(0, 256, P)]
    p = np.arange(P)
    bf16 = mybir.dt.np(BF16) if hasattr(mybir.dt, "np") else np.dtype("bfloat16")
    arrays = {
        "x": x, "ctx_rev": crev, "ctx_rev_t": crev.T, "ctx_nat": c, "ctx_nat_t": c.T,
        "g_x": a["g_xattn"], "g_f": a["g_ffn"], "kpad": kpad, "d_skip": a["L0_xattn_D"],
        "wu0": np.stack(wu0), "rw0": a["L0_ffn_router_w"].T, "eb0": a["L0_ffn_expert_bias"],
        "wu1": np.stack(wu1), "rw1": a["L1_ffn_Wr"].T, "br1": a["L1_ffn_br"],
        "ident_c": np.eye(P, dtype=np.float32),
        "anti_c": np.ascontiguousarray(np.eye(P, dtype=np.float32)[::-1]),
        "identb_c": np.eye(P, dtype=np.float32).astype(bf16),
        "rowmask_c": np.concatenate([p[:, None] % 32 // HD0 == np.arange(4), 1 - 2 * (p[:, None] // 32 % 2), p[:, None] // 32 % 2],
                                    1).astype(np.float32),
        "headmask_c": (p[:, None] // HD1 == np.arange(8)).astype(np.float32),
        "causal_c": np.tile(np.where(p[None, :] > p[:, None], -1e30, 0.0), (1, 4)).reshape(P, 4, P).astype(bf16),
    }
    nc = bacc.Bacc("TRN2", target_bir_lowering=False, num_devices=1)
    feeds, aps = {}, []
    for name, v in arrays.items():
        v = np.ascontiguousarray(v)
        feeds[f"in_{name}"] = v
        aps.append(nc.dram_tensor(f"in_{name}", v.shape, mybir.dt.from_np(v.dtype), kind="ExternalInput").ap())
    aps.append(nc.dram_tensor("out_y", (T, D), F32, kind="ExternalOutput").ap())
    build(nc, *aps)
    r = run_bass_kernel_spmd(nc, [feeds], core_ids=[0])
    return r.results[0]["out_y"].reshape(NB, P, D)
```

```python
from contextlib import ExitStack

import concourse.bass as bass
from concourse import mybir

F32 = mybir.dt.float32
F32R = mybir.dt.float32r
BF16 = mybir.dt.bfloat16
ALU = mybir.AluOpType
ACT = mybir.ActivationFunctionType
AX_X = mybir.AxisListType.X

P = 128
NB = 16
D = 256
T = NB * P
NH0, HD0 = 16, 8
NH1, HD1 = 16, 16
E0, E1 = 8, 32
U0 = 1024 // P + E0
U1 = E1 + 256 // P
TOP0, TOP1, G1, KG1 = 2, 6, 8, 4
SCALE1 = HD1 ** -0.5
ROUTE_SCALE = 2.5
BLK = 512
NBLK = T // BLK
BPB = BLK // P
EPS = 1e-5
FILL = -1.0e30
TAKEN = -2.0e30
S = 4
ROUTE_PARTS = 6


class Steps:

    def __init__(self, sem, start=0):
        self.sem, self.n = sem, start

    def up(self, ins, by=1):
        ins.then_inc(self.sem, by)
        self.n += by
        return self.n


def ap_of(view, offset, dims):
    return bass.AP(view.tensor, view.offset + offset, [list(view.ap[0])] + dims)


def build(nc, x, ctx_rev, ctx_rev_t, ctx_nat, ctx_nat_t, g_x, g_f, kpad, d_skip, wu0, rw0, eb0, wu1, rw1, br1,
          ident_c, anti_c, identb_c, rowmask_c, headmask_c, causal_c, out):
    top = ExitStack()
    with top:
        def sb(name, shape, dt=F32, ctx=top):
            return ctx.enter_context(nc.sbuf_tensor(name, shape, dt))

        def sem(name):
            return top.enter_context(nc.semaphore(name))

        bank = [top.enter_context(nc.psum_tensor(f"bank{i}", [P, 2, 512], F32)) for i in range(4)]

        def bk(i):
            return bank[i // 2][:, i % 2, :]

        X = sb("X", [P, NB, D])
        stats = sb("stats", [P, NB, 6])
        mv = sb("mv", [P, NB, 2])
        rstd = sb("rstd", [P, NB])
        ident = sb("ident", [P, P])
        tg = sb("tg", [P, 4])
        router = {tag: (sb(f"router_{tag}", [P, 2, E]), sb(f"router_bias_{tag}", [P, E])) for tag, E in (("f0", E0), ("f1", E1))}
        mhalf = sb("mhalf", [P, NB])
        vpe = sb("vpe", [P, NB])

        gates0 = nc.dram_tensor("gates0", (U0, T), F32, kind="Internal").ap()
        gates1 = nc.dram_tensor("gates1", (U1, T), F32, kind="Internal").ap()

        s_x = [sem(f"x_loaded{i}") for i in range(4)]
        s_c = sem("identity_loaded")
        s_tl = sem("gates_loaded")
        s_tg = sem("gate_tanh")
        s_rl = sem("routers_loaded")
        s_held = sem("held")
        s_st = sem("start_step")
        s_mh = sem("mhalf_set")
        graw = sb("graw", [P, 4])

        def plain(eng):
            eng.sem_inc(s_held, 1)

        def keep_clock(pe, bank_, n):
            for _ in range(n):
                pe.matmul(bank_[:, 0:P], ident[:], ident[:], start=True, stop=True)

        deviation_sems = {p: (sem(f"{p}_moments"), sem(f"{p}_var_ready"), sem(f"{p}_rstd_ready")) for p in ("a", "f0", "c", "f1")}

        def part_of(phase, part):
            first = BPB if phase == "a" else 2 * BPB
            return slice(first, NB) if part else slice(0, first)

        def variances(dve, phase, part):
            moments_made, ready, _ = deviation_sems[phase]
            bs = part_of(phase, part)
            for b in range(NB)[bs]:
                last = dve.bn_aggr(mv[:, b, :], stats[:, b, :])
            last.then_inc(moments_made, 1)
            dve.wait_ge(moments_made, part + 1)
            dve.tensor_scalar(vpe[:, bs], mv[:, bs, 1], EPS, None, ALU.add).then_inc(ready, 1)

        def deviations(pool, phase, part):
            _, ready, done = deviation_sems[phase]
            bs = part_of(phase, part)
            pool.wait_ge(ready, part + 1)
            pool.tensor_tensor(rstd[:, bs], vpe[:, bs], mhalf[:, bs], ALU.pow).then_inc(done, 1)

        pa = ExitStack()
        with pa:
            KR = sb("k_rows", [P, 2, 4, D], ctx=pa)
            KA = sb("k_signed_hi", [P, 2, 4, D], F32R, pa)
            K4 = sb("k_terms", [P, 2, 4, D], F32R, pa)
            cRT = sb("ctx_rev_t_sb", [P, 2, T], ctx=pa)
            TM = sb("toeplitz", [P, 4, 4, 384], ctx=pa)
            dtmp = sb("d_diagonals", [P, 4, 4, P], ctx=pa)
            anti = sb("anti", [P, P], ctx=pa)
            dbc = sb("dbc", [P, NH0], ctx=pa)
            rowmask = sb("rowmask", [P, 6], ctx=pa)
            KM = sb("k_masked", [P, 2, 4, 4, D], F32R, pa)
            sel = sb("select", [P, 2, 4, P], F32R, pa)
            qf = sb("q_full", [P, 2, D], ctx=pa)
            qhi = sb("q_hi", [P, 2, D], F32R, pa)
            qlo = sb("q_lo", [P, 2, D], F32R, pa)
            Q4 = sb("q_terms", [P, 2, 4, D], F32R, pa)
            VP = sb("v_padded", [P, 2, 2, 4, P], ctx=pa)
            W = sb("w_decayed", [P, 8, 2, 384], ctx=pa)

            s_r = deviation_sems["a"][2]
            s_ca = sem("a_consts")
            s_cx = [sem(f"a_ctx{i}") for i in range(2)]
            s_ks = [sem(f"a_kernel_loaded{v}") for v in range(4)]
            s_ms = sem("a_masks_loaded")
            s_vz = sem("a_vpad_zeroed")
            s_tm = sem("a_diagonal_step")
            s_td = sem("a_table_added")
            s_tc = sem("a_table_repeated")
            s_kr = [sem(f"a_k_loaded{i}") for i in range(2)]
            s_sl = sem("a_select_ready")
            s_kh = sem("a_k_hi")
            s_kb = sem("a_k_share")
            s_k4 = sem("a_k_terms")
            s_km = sem("a_k_ready")
            s_qf = sem("a_q_full")
            s_qh = sem("a_q_hi")
            s_ql = sem("a_q_lo")
            s_qs = sem("a_q_selected")
            s_vp = sem("a_v_ready")
            s_q = sem("a_q_ready")
            s_a1 = sem("a_products_ready")
            s_w = sem("a_decayed_ready")
            s_a2 = sem("a_quads_done")
            s_xd = sem("a_residual_done")
            s_sd = sem("a_dve_step")

            PAIR_BANKS = (0, 1, 2) * 5 + (1,)
            SINCE = (4, 2, 4) + (3,) * 12 + (2,)
            acc_bank = bk(6)[:, 0:D]
            select_bank = bk(7)

            with nc.Block() as block:
                @block.sync
                def _(sp):
                    def keys(start, u):
                        rows = ctx_rev[start, :].rearrange("(s r) d -> r s d", r=32)
                        for term in range(4):
                            sp.dma_start(KR[32 * term:32 * term + 32, u, :, :], rows).then_inc(s_kr[u], 16)

                    keys(slice(0, P), 0)
                    xv = x.rearrange("(b p) d -> p b d", p=P)

                    def rows(i):
                        sp.dma_start(X[:, 4 * i:4 * i + 4, :], xv[:, 4 * i:4 * i + 4, :]).then_inc(s_x[i], 16)

                    def kernel_table(v):
                        src = bass.AP(kpad.tensor, kpad.offset + v * 384, [[1, P], [4 * 384, 4], [1, D]])
                        sp.dma_start(TM[:, v, :, 0:D], src).then_inc(s_ks[v], 16)

                    def values(i):
                        ht = slice(T // 2 * i, T // 2 * (i + 1))
                        sp.dma_start(cRT[:, :, ht], ctx_rev_t.rearrange("(c p) t -> p c t", p=P)[:, :, ht]).then_inc(s_cx[i], 16)

                    rows(0)
                    kernel_table(0)
                    rows(1)
                    kernel_table(1)
                    kernel_table(2)
                    rows(2)
                    kernel_table(3)
                    keys(slice(P, 2 * P), 1)
                    values(0)
                    rows(3)
                    values(1)
                    for tag, rw, rbias in (("f0", rw0, eb0), ("f1", rw1, br1)):
                        sp.dma_start(router[tag][0][:], rw.rearrange("(c p) e -> p c e", p=P)).then_inc(s_rl, 16)
                        sp.dma_start(router[tag][1][:], rbias.partition_broadcast(P)).then_inc(s_rl, 16)
                    with sp.Fori(1, NB // 2) as i:
                        for u in range(2):
                            sp.wait_ge(s_k4, i * 2 + (u + 1))
                            keys(bass.ds(i * 2 * P + u * P, P), u)

                @block.gpsimd
                def _(pool):
                    pool.sem_inc(s_k4, 2)
                    pool.memset(mhalf[:], -0.5).then_inc(s_mh, 1)
                    pool.memset(VP[:], 0.0).then_inc(s_vz, 1)
                    pool.wait_ge(s_ms, 16)

                    def query_lo(b, u):
                        pool.wait_ge(s_qh, b + 1)
                        pool.tensor_tensor(qlo[:, u, :], qf[:, u, :], qhi[:, u, :].bitcast(F32), ALU.subtract).then_inc(s_ql, 1)

                    def terms(b, u):
                        pool.wait_ge(s_kh, b + 1)
                        pool.wait_ge(s_km, b + 1)
                        raw = KR[:, u].rearrange("p s d -> p (s d)")
                        pool.tensor_tensor(raw, raw, rowmask[:, 5:6].broadcast_to((P, 4 * D)), ALU.mult).then_inc(s_kb, 1)
                        pool.wait_ge(s_kb, b + 1)
                        pool.tensor_tensor(K4[:, u].rearrange("p s d -> p (s d)"), raw,
                                           KA[:, u].rearrange("p s d -> p (s d)").bitcast(F32), ALU.add).then_inc(s_k4, 1)

                    terms(0, 0)
                    pool.wait_ge(s_mh, 1)
                    deviations(pool, "a", 0)
                    query_lo(0, 0)
                    terms(1, 1)
                    query_lo(1, 1)
                    terms(2, 0)
                    deviations(pool, "a", 1)
                    query_lo(2, 0)
                    terms(3, 1)
                    query_lo(3, 1)
                    with pool.Fori(2, NB // 2) as i:
                        for u in range(2):
                            terms(i * 2 + u, u)
                            query_lo(i * 2 + u, u)
                    deviations(pool, "f0", 0)

                @block.scalar
                def _(act):
                    act.dma_start(rowmask[:], rowmask_c).then_inc(s_ms, 16)
                    act.dma_start(anti[:], anti_c).then_inc(s_ca, 16)
                    act.dma_start(dbc[:], d_skip.partition_broadcast(P)).then_inc(s_ca, 16)
                    act.dma_start(ident[:], ident_c).then_inc(s_c, 16)
                    act.dma_start(graw[:, 0:2], g_x.partition_broadcast(P)).then_inc(s_tl, 16)
                    act.dma_start(graw[:, 2:4], g_f.partition_broadcast(P)).then_inc(s_tl, 16)
                    act.sem_inc(s_km, 2)
                    act.wait_ge(s_ms, 16)
                    def k_hi(b, u, landed):
                        act.wait_ge(s_kr[u], landed)
                        act.wait_ge(s_k4, b + 1)
                        act.activation(KA[:, u].rearrange("p s d -> p (s d)"), KR[:, u].rearrange("p s d -> p (s d)"),
                                       ACT.Copy, scale=rowmask[:, 4:5]).then_inc(s_kh, 1)

                    def masks(b, u, vs):
                        for v in vs:
                            last = act.activation(KM[:, u, v].rearrange("p s d -> p (s d)"),
                                                  K4[:, u].rearrange("p s d -> p (s d)").bitcast(F32),
                                                  ACT.Copy, scale=rowmask[:, v:v + 1])
                        return last

                    def repeat(v):
                        act.wait_ge(s_td, v + 1)
                        act.activation(TM[:, v, :, D:384], TM[:, v, :, 0:P], ACT.Copy).then_inc(s_tc, 1)

                    def operands(b, u, landed, has_next=True, first=False):
                        if first:
                            repeat(0)
                        act.wait_ge(s_qf, b + 1)
                        act.wait_ge(s_qs, 2 * b + 2)
                        act.activation(qhi[:, u, :], qf[:, u, :], ACT.Copy).then_inc(s_qh, 1)
                        act.wait_ge(s_k4, b + 3)
                        act.wait_ge(s_a1, 8 * b + 8)
                        masks(b, u, (0, 1))
                        if first:
                            repeat(1)
                        if has_next and not first:
                            k_hi(b + 1, 1 - u, landed + 64 * u)
                        masks(b, u, (2, 3)).then_inc(s_km, 1)
                        if first:
                            k_hi(b + 1, 1 - u, landed + 64 * u)
                        if first:
                            repeat(2)
                        for i in range(2):
                            act.wait_ge(s_qs, 2 * b + (5 + i))
                            act.activation(Q4[:, u, 2 * i:2 * i + 2].rearrange("p s d -> p (s d)"), select_bank, ACT.Copy).then_inc(s_q, 1)
                        act.wait_ge(s_a2, 4 * b + 4)
                        if first:
                            repeat(3)
                            act.wait_ge(s_cx[0], 16)
                        for blk in range(2):
                            dst = ap_of(VP[:, u, blk].rearrange("p a b -> p (a b)"), 0, [[P, 4], [40, 4], [1, 8]])
                            src = cRT[:, 1 - blk, bass.ds(b * P, P)].rearrange("p (g v i) -> p g v i", g=4, v=4)
                            last = act.activation(dst, src, ACT.Copy)
                        last.then_inc(s_vp, 1)

                    k_hi(0, 0, 64)
                    act.wait_ge(s_c, 16)
                    act.activation(sel[:].rearrange("p a s m -> p (a s) m"), ident[:].unsqueeze(1).broadcast_to((P, 8, P)),
                                   ACT.Copy, scale=0.0).then_inc(s_sl, 1)
                    act.wait_ge(s_sl, 1)
                    for i in range(2):
                        for s in range(4):
                            act.activation(sel[:, i, s, 64 * i:64 * i + 64].rearrange("p (c r) -> p c r", c=2),
                                           ident[:, 32 * s:32 * s + 32].unsqueeze(1).broadcast_to((P, 2, 32)),
                                           ACT.Copy).then_inc(s_sl, 1)

                    act.wait_ge(s_tl, 32)
                    act.activation(tg[:], graw[:], ACT.Tanh).then_inc(s_tg, 1)
                    act.wait_ge(s_vz, 1)
                    operands(0, 0, 64, first=True)
                    operands(1, 1, 64)
                    for i in range(2):
                        if i:
                            act.wait_ge(s_cx[i], 16)
                        with act.Fori(1 - i, NB // 4 - i) as j:
                            for u in range(2):
                                operands(8 * i + j * 2 + u, u, j * 64 + (256 * i + 64))
                    operands(NB - 2, 0, 64 * (NB // 2))
                    operands(NB - 1, 1, 64 * (NB // 2), False)

                @block.tensor
                def _(pe):
                    pe.sem_inc(s_a1, 16)
                    pe.sem_inc(s_a2, 8)
                    pe.sem_inc(s_qs, 4)
                    pe.wait_ge(s_sl, 9)

                    def select(b, u, i):
                        pe.wait_ge(s_ql, b + 1)
                        if not (isinstance(b, int) and b == 0 and i == 0):
                            pe.wait_ge(s_q, 2 * b + i)
                        for s in range(2):
                            o = select_bank[:, s * D:s * D + D]
                            pe.matmul(o, sel[:, 0, 2 * i + s, :], qhi[:, u, :], start=True, stop=False)
                            last = pe.matmul(o, sel[:, 1, 2 * i + s, :], qlo[:, u, :], start=False, stop=True)
                        last.then_inc(s_qs, 1)

                    def products(b, u, j):
                        n = 8 * b + j
                        if j == 0:
                            pe.wait_ge(s_km, b + 3)
                        if j < 2:
                            pe.wait_ge(s_q, 2 * b + (j + 1))
                        pe.wait_ge(s_w, n + (5 - SINCE[8 * u + j]))
                        v = j // 2
                        for hh in range(2):
                            g = 2 * (j % 2) + hh
                            o = bank[PAIR_BANKS[8 * u + j]][:, hh, :]
                            pe.matmul(o[:, 0:D], KM[:, u, v, g, P:D], Q4[:, u, g, :], start=True, stop=True)
                            last = pe.matmul(o[:, D:384], KM[:, u, v, g, 0:P], Q4[:, u, g, P:D], start=True, stop=True)
                        last.then_inc(s_a1, 1)

                    def values(b, u, t):
                        pe.wait_ge(s_w, 4 + 8 * b + 2 * t + 2)
                        if t == 0:
                            pe.wait_ge(s_vp, b + 1)
                            pe.wait_ge(s_xd, b + 2)
                        for blk in range(2):
                            for g in range(4):
                                slot = 2 * t + g // 2
                                cols = slice(0, D) if blk == 0 else slice(P, D)
                                wc = slice(0, D) if blk == 0 else slice(D, 384)
                                last = pe.matmul(acc_bank[32 * g:32 * g + 32, cols], VP[:, u, blk, g, 32 * t:32 * t + 32],
                                                 W[:, slot, g % 2, wc], start=(t == 0 and blk == 0),
                                                 stop=(t == 3 and blk == 1), skip_group_check=True)
                        last.then_inc(s_a2, 1)

                    def batch(b, u, has_next):
                        for t in range(4):
                            for j in (2 * t + 3, 2 * t + 4):
                                if j < 8:
                                    products(b, u, j)
                                elif has_next:
                                    products(b + 1, 1 - u, j - 8)
                                if j in (5, 7) and has_next:
                                    select(b + 1, 1 - u, (j - 5) // 2)
                            values(b, u, t)

                    select(0, 0, 0)
                    select(0, 0, 1)
                    for j in range(3):
                        products(0, 0, j)
                    with pe.Fori(0, NB // 2 - 1) as i:
                        for u in range(2):
                            batch(i * 2 + u, u, True)
                    batch(NB - 2, 0, True)
                    batch(NB - 1, 1, False)

                @block.vector
                def _(dve):
                    dve.sem_inc(s_w, 4)
                    dve.sem_inc(s_xd, 2)
                    def query(b, u):
                        dve.wait_ge(s_qs, 2 * b + 2)
                        xb = X[:, bass.ds(b, 1), :].rearrange("p a d -> p (a d)")
                        dve.tensor_scalar(qf[:, u, :], xb, mv[:, bass.ds(b, 1), 0:1].rearrange("p a d -> p (a d)"),
                                          rstd[:, bass.ds(b, 1)], ALU.subtract, ALU.mult).then_inc(s_qf, 1)

                    def decay(b, u, j):
                        n = 8 * b + j
                        dve.wait_ge(s_a1, 16 + n + 1)
                        if j % 2 == 0:
                            dve.wait_ge(s_a2, 4 * b + (j // 2 + 5))
                        v, g = j // 2, 2 * (j % 2)
                        dve.tensor_tensor(W[:, j, :, :], bank[PAIR_BANKS[8 * u + j]][:, :, 0:384], TM[:, v, g:g + 2, :],
                                          ALU.mult).then_inc(s_w, 1)

                    def residual(b, u):
                        dve.wait_ge(s_a2, 4 * b + 12)
                        xb = X[:, bass.ds(b, 1), :].rearrange("p a d -> p (a d)")
                        dve.scalar_tensor_tensor(xb, acc_bank, tg[:, 0:1], xb, ALU.mult, ALU.add).then_inc(s_xd, 1)

                    def moments(b):
                        dve.wait_ge(s_xd, b + 3)
                        plain(dve)
                        xb = X[:, bass.ds(b, 1), :].rearrange("p a d -> p (a d)")
                        dve.bn_stats(stats[:, bass.ds(b, 1), :].rearrange("p a d -> p (a d)"), xb).then_inc(s_sd, 1)

                    def batch(b, u, has_prev, has_next):
                        for j in range(8):
                            decay(b, u, j)
                            if j == 1 and has_prev:
                                residual(b - 1, 1 - u)
                            if j == 4 and not (isinstance(b, int) and b + 2 >= NB):
                                query(b + 2, u)
                            if j == 2 and has_prev:
                                moments(b - 1)

                    st = Steps(s_st)

                    def input_moments(i):
                        dve.wait_ge(s_x[i], 16)
                        for b in range(4 * i, 4 * i + 4):
                            st.up(dve.bn_stats(stats[:, b, :], X[:, b, :]))

                    input_moments(0)
                    dve.wait_ge(s_st, st.n)
                    variances(dve, "a", 0)
                    dve.wait_ge(s_ca, 32)
                    tm = Steps(s_tm)
                    for v in range(4):
                        dv = dbc[:].rearrange("p (g v) -> p v g", v=4)[:, v, :]
                        tm.up(dve.tensor_tensor(dtmp[:, v], anti[:].unsqueeze(1).broadcast_to((P, 4, P)),
                                                dv.unsqueeze(2).broadcast_to((P, 4, P)), ALU.mult))

                    def table(v):
                        dve.wait_ge(s_ks[v], 16)
                        dve.tensor_tensor(TM[:, v, :, 0:P], TM[:, v, :, 0:P], dtmp[:, v], ALU.add).then_inc(s_td, 1)

                    dve.wait_ge(s_tm, tm.n)
                    table(0)
                    input_moments(1)
                    dve.wait_ge(s_r, 1)
                    query(0, 0)
                    query(1, 1)
                    table(1)
                    table(2)
                    input_moments(2)
                    table(3)
                    dve.wait_ge(s_tc, 4)
                    dve.wait_ge(s_tg, 1)
                    batch(0, 0, False, True)
                    input_moments(3)
                    dve.wait_ge(s_st, st.n)
                    variances(dve, "a", 1)
                    batch(1, 1, True, True)
                    dve.wait_ge(s_r, 2)
                    with dve.Fori(1, NB // 2 - 1) as i:
                        for u in range(2):
                            batch(i * 2 + u, u, True, True)
                    dve.wait_ge(s_sd, 2 * BPB)
                    variances(dve, "f0", 0)
                    batch(NB - 2, 0, True, True)
                    batch(NB - 1, 1, True, False)
                    residual(NB - 1, 1)
                    moments(NB - 1)

        def feed_forward(tag, E, U, gated, wu, gates, tgcol, route, final):
            WC = 768 if gated else 512
            HB = 2 if gated else 4
            LA = 1 if gated else 2
            WA = 2
            YL = 0 if gated else 1
            YC = 0 if gated else S
            NU = NBLK * U
            pf = ExitStack()
            with pf:
                xh = sb(f"xh{tag}", [P, 2, T], F32R, pf)
                xl = sb(f"xl{tag}", [P, 2, T], F32R, pf)
                xn = sb(f"xn{tag}", [P, 2, BPB, D], F32, pf)
                rwf, bias = router[tag]
                rwh = sb(f"rwh{tag}", [P, 2, E], F32R, pf)
                rwl = sb(f"rwl{tag}", [P, 2, E], F32R, pf)
                lts = sb(f"lts{tag}", [E, BLK], F32, pf)
                lg = sb(f"lg{tag}", [P, BPB, E], F32, pf)
                gt = sb(f"gt{tag}", [P, BPB, E], F32, pf)
                gts = sb(f"gts{tag}", [E, BLK], F32, pf)
                ones = sb(f"ones{tag}", [U - E, BLK], F32, pf)
                s_r = deviation_sems[tag][2]
                s_rw = sem(f"{tag}_router_split")
                s_n = sem(f"{tag}_normed")
                s_l = sem(f"{tag}_lo_ready")
                s_t = sem(f"{tag}_transposed")
                s_h = sem(f"{tag}_hi_ready")
                s_lt = sem(f"{tag}_logits_t")
                s_lc = sem(f"{tag}_logits_t_copied")
                s_lg = sem(f"{tag}_logits")
                s_lgc = sem(f"{tag}_logits_copied")
                s_sg = sem(f"{tag}_sigmoid")
                s_gt = sem(f"{tag}_gates_ready")
                s_gT = sem(f"{tag}_gates_t")
                s_gc = sem(f"{tag}_gates_t_copied")
                s_gst = sem(f"{tag}_gates_stored")
                s_ro = sem(f"{tag}_route_step")
                s_on = sem(f"{tag}_ones_set")
                s_os1 = sem(f"{tag}_ones_stored")
                rt = route(pf, lg, gt, bias, s_ro)

                wraw = sb(f"wraw{tag}", [P, S, WC], F32, pf)
                whi = sb(f"whi{tag}", [P, S, WC], F32R, pf)
                wlo = sb(f"wlo{tag}", [P, S, WC], F32R, pf)
                G = sb(f"G{tag}", [P, S, BLK], F32, pf)
                r = sb(f"r{tag}", [P, S, BLK], F32, pf)
                t = sb(f"t{tag}", [P, S, BLK], F32, pf)
                y = sb(f"y{tag}", [P, S, BLK], F32, pf)
                yhi = sb(f"yhi{tag}", [P, S, BLK], F32R, pf)
                ylo = sb(f"ylo{tag}", [P, S, BLK], F32R, pf)
                os_ = sb(f"os{tag}", [P, 2, BLK], F32, pf)
                s_wl = [sem(f"{tag}_w_loaded{i}") for i in range(S)]
                s_gl = [sem(f"{tag}_g_loaded{i}") for i in range(S)]
                s_wh = sem(f"{tag}_w_hi")
                s_wo = sem(f"{tag}_w_lo")
                s_hd = sem(f"{tag}_hidden")
                s_ac = sem(f"{tag}_activated")
                s_td = sem(f"{tag}_t_done")
                s_re = sem(f"{tag}_rectified")
                s_yd = sem(f"{tag}_y_done")
                s_yh = sem(f"{tag}_y_hi")
                s_yl = sem(f"{tag}_y_lo")
                s_od = sem(f"{tag}_unit_out")
                s_os = sem(f"{tag}_out_scaled")
                s_ot = sem(f"{tag}_out_t")
                s_xa = sem(f"{tag}_x_added")
                s_xs = sem(f"{tag}_x_step")
                s_fin = sem(f"{tag}_stored")

                def acc(blk):
                    return bank[2 + blk % 2]

                NS = U - E
                TAIL = (U // S - 1) * S

                def head(blk):
                    return S if gated and blk > 0 else 2 * S

                TRA, SPLIT, LOG = (2, (3, 3), TAIL) if gated else (3, (4, 5), 5)
                ADD = (2, 2) if gated else (2, 3)
                ROUTE0 = (0,) if gated else (0, 0, 0, 1, 1, 1)
                ROUTE1 = (2,) if gated else (2, 2, 3, 3, 4, 4)
                ROUTE = (TAIL + 3,) if gated else tuple(TAIL + i for i in range(ROUTE_PARTS))
                GT0 = 1 if gated else 0
                GT1 = S if gated else S + 2

                def prep_banks(m):
                    pair = bank[(2, 3, 3, 2)[m]]
                    return pair[:, 0, :], pair[:, 1, :]

                def gates_bank(m):
                    return bank[2 if m == 3 else 3][0:E, 0, :]

                with nc.Block() as block:
                    def slot_value(blk, n, loop):
                        if loop is None:
                            return 16 * ((blk * U + n) // S + 1)
                        i, u = loop
                        return i * 16 + 16 * ((blk * U + u) // S + 1)

                    def walk(eng, unit, between=None):
                        for blk in range(NBLK):
                            base = blk * U
                            for n in range(head(blk)):
                                unit(blk, base + n, n, (base + n) % S, slot_value(blk, n, None))
                                if between:
                                    between(blk, n)
                            if TAIL - head(blk) == S:
                                for n in range(head(blk), TAIL):
                                    unit(blk, base + n, n, (base + n) % S, slot_value(blk, n, None))
                            else:
                                with eng.Fori(head(blk) // S, TAIL // S) as i:
                                    for u in range(S):
                                        unit(blk, i * S + (base + u), i * S + u, (base + u) % S, slot_value(blk, None, (i, u)))
                            for n in range(TAIL, U):
                                unit(blk, base + n, n, (base + n) % S, slot_value(blk, n, None))
                                if between:
                                    between(blk, n)

                    def is_int(v):
                        return isinstance(v, int)

                    @block.sync
                    def _(sp):
                        EARLY = S if gated else S + 2

                        def weights(N, n, slot):
                            sp.wait_ge(s_wo, N + 1)
                            src = wu[n] if is_int(n) else wu[bass.ds(n, 1), :, :].rearrange("a p c -> (a p) c")
                            sp.dma_start(wraw[:, slot, :], src).then_inc(s_wl[slot], 16)

                        def store_gates(m):
                            sp.wait_ge(s_gc, m + 1)
                            sp.dma_start(gates[NS:U, m * BLK:(m + 1) * BLK], gts[:]).then_inc(s_gst, 16)

                        def unit(blk, N, n, slot, landed):
                            if not (blk == 0 and is_int(n) and n < EARLY):
                                weights(N, n, slot)
                            if is_int(n) and blk == 0 and n == min(NS, S + 1):
                                for e in range(S, EARLY):
                                    weights(e, e, e % S)
                                store_gates(0)
                            if is_int(n) and n == (NS if blk == 0 else 0):
                                sp.wait_ge(s_gst, 16 * (blk + 1))
                            sp.wait_ge(s_yd, N + 1)
                            cols = slice(blk * BLK, (blk + 1) * BLK)
                            row = gates[n:n + 1, cols] if is_int(n) else gates[bass.ds(n, 1), cols]
                            sp.dma_start(G[:, slot, :], row.rearrange("a t -> (a t)").partition_broadcast(P)).then_inc(s_gl[slot], 16)

                        def between(blk, n):
                            if n == (TAIL if blk == 0 else S - 1) and blk < NBLK - 1:
                                store_gates(blk + 1)

                        weights(0, 0, 0)
                        sp.wait_ge(s_on, 1)
                        sp.dma_start(gates[0:NS, :].rearrange("s (b t) -> s b t", b=NBLK),
                                     ones[:].unsqueeze(1).broadcast_to((NS, NBLK, BLK))).then_inc(s_os1, 16)
                        for N in range(1, S):
                            weights(N, N, N)
                        sp.wait_ge(s_os1, 16)
                        walk(sp, unit, between)
                        if final:
                            for blk in range(NBLK):
                                for half in range(2):
                                    sp.wait_ge(s_xa, 2 * blk + half + 5)
                                    bs = slice(blk * BPB + 2 * half, blk * BPB + 2 * half + 2)
                                    sp.dma_start(out.rearrange("(b p) d -> p b d", p=P)[:, bs, :], X[:, bs, :]).then_inc(s_fin, 16)
                            sp.wait_ge(s_fin, 2 * 16 * NBLK)

                    @block.gpsimd
                    def _(pool):
                        pool.sem_inc(s_wo if gated else s_yd, S)
                        pool.memset(ones[:], 1.0).then_inc(s_on, 1)
                        deviations(pool, tag, 1)

                        def mult(blk, N, n, slot, landed):
                            pool.wait_ge(s_ac, N + 1)
                            pool.wait_ge(s_gl[slot], landed)
                            pool.wait_ge(s_yl, N + 1)
                            pool.tensor_tensor(y[:, slot, :], t[:, slot, :], G[:, slot, :], ALU.mult).then_inc(s_yd, 1)

                        def w_lo(blk, N, n, slot, landed):
                            pool.wait_ge(s_wh, N + 1)
                            pool.tensor_tensor(wlo[:, slot, :], wraw[:, slot, :], whi[:, slot, :].bitcast(F32),
                                               ALU.subtract).then_inc(s_wo, 1)

                        walk(pool, w_lo if gated else mult)
                        if not final:
                            deviations(pool, "c", 0)

                    @block.scalar
                    def _(act):
                        def w_hi(N, slot, landed):
                            act.wait_ge(s_wl[slot], landed)
                            act.wait_ge(s_od, N + 1)
                            act.activation(whi[:, slot, :], wraw[:, slot, :], ACT.Copy).then_inc(s_wh, 1)

                        def y_hi(N, slot):
                            act.wait_ge(s_yd, N + S + 1)
                            act.wait_ge(s_od, N + 1)
                            act.activation(yhi[:, slot, :], y[:, slot, :], ACT.Copy).then_inc(s_yh, 1)

                        def hidden(N, slot, hb):
                            act.wait_ge(s_hd, N + 1)
                            act.wait_ge(s_yd, N + 1)
                            if gated:
                                act.activation(r[:, slot, :], bank[hb][:, 0, :], ACT.Silu).then_inc(s_ac, 1)
                            else:
                                act.activation(r[:, slot, :], bk(hb), ACT.Relu).then_inc(s_re, 1)

                        def square(N, slot):
                            act.wait_ge(s_re, N + 1)
                            act.activation(t[:, slot, :], r[:, slot, :], ACT.Square).then_inc(s_ac, 1)

                        def unit(blk, N, n, slot, landed):
                            def weights():
                                if not (is_int(N) and N + WA >= NU):
                                    w_hi(N + WA, (slot + WA) % S, landed + 16 * ((slot + WA) // S))

                            hidden(N, slot, slot % HB)
                            if gated:
                                weights()
                            if YL == 0:
                                y_hi(N, slot)
                            elif not (is_int(N) and N == 0):
                                y_hi(N - 1, (slot - 1) % S)
                            if not gated:
                                square(N, slot)
                                weights()

                        def epilogue(blk):
                            if YL == 1 and blk == NBLK - 1:
                                y_hi(NU - 1, (NU - 1) % S)
                            act.wait_ge(s_od, S + (blk + 1) * U)
                            if blk > 0:
                                act.wait_ge(s_ot, blk)
                            for c in range(2):
                                last = act.activation(os_[:, c, :], acc(blk)[:, c, :], ACT.Copy, scale=tg[:, tgcol:tgcol + 1])
                            last.then_inc(s_os, 1)

                        def x_hi(m):
                            act.wait_ge(s_t, m + 1)
                            for c in range(2):
                                last = act.activation(xh[:, c, m * BLK:(m + 1) * BLK], prep_banks(m)[c], ACT.Copy)
                            last.then_inc(s_h, 1)

                        def logits_t_copy(m):
                            act.wait_ge(s_lt, m + 1)
                            if m > 0:
                                act.wait_ge(s_lg, m)
                            act.activation(lts[:], prep_banks(m)[0][0:E, :], ACT.Copy).then_inc(s_lc, 1)

                        def sigmoid(m):
                            act.wait_ge(s_lgc, m + 1)
                            if m > 0:
                                act.wait_ge(s_gt, m)
                            act.activation(rt.sc[:], lg[:], ACT.Sigmoid).then_inc(s_sg, 1)

                        def gates_t_copy(m):
                            act.wait_ge(s_gT, m + 1)
                            if m > 0:
                                act.wait_ge(s_gst, 16 * m)
                            act.activation(gts[:], gates_bank(m), ACT.Copy).then_inc(s_gc, 1)

                        def between(blk, n):
                            if n == 1 and blk > 0:
                                epilogue(blk - 1)
                            if n == GT0 + 1 and blk == 0:
                                gates_t_copy(0)
                                sigmoid(1)
                            if n == GT1 + 1 and blk == 0:
                                gates_t_copy(1)
                            if blk + 2 < NBLK:
                                if n == SPLIT[0]:
                                    x_hi(blk + 2)
                                if n == LOG + 1:
                                    logits_t_copy(blk + 2)
                                if n == LOG + 2:
                                    sigmoid(blk + 2)
                            if n == 0 and 0 < blk < NBLK - 1:
                                gates_t_copy(blk + 1)

                        act.wait_ge(s_rl, 64)
                        act.activation(rwh[:].rearrange("p c e -> p (c e)"), rwf[:].rearrange("p c e -> p (c e)"), ACT.Copy).then_inc(s_rw, 1)
                        x_hi(0)
                        logits_t_copy(0)
                        x_hi(1)
                        for N in range(WA):
                            w_hi(N, N, 16)
                        logits_t_copy(1)
                        sigmoid(0)
                        walk(act, unit, between)
                        epilogue(NBLK - 1)

                    @block.vector
                    def _(dve):
                        dve.sem_inc(s_yd if gated else s_wo, S)
                        dve.sem_inc(s_td if gated else s_yl, S)
                        dve.sem_inc(s_xa, 4)

                        def w_lo(N, slot):
                            dve.wait_ge(s_wh, N + 1)
                            dve.tensor_tensor(wlo[:, slot, :], wraw[:, slot, :], whi[:, slot, :].bitcast(F32),
                                              ALU.subtract).then_inc(s_wo, 1)

                        def y_lo(N, slot):
                            dve.wait_ge(s_yh, N + 1)
                            dve.tensor_tensor(ylo[:, slot, :], y[:, slot, :], yhi[:, slot, :].bitcast(F32),
                                              ALU.subtract).then_inc(s_yl, 1)

                        def unit(blk, N, n, slot, landed):
                            if gated:
                                dve.wait_ge(s_ac, N + 1)
                                dve.wait_ge(s_yd, N + 1)
                                dve.tensor_tensor(t[:, slot, :], bank[slot % HB][:, 1, :], r[:, slot, :], ALU.mult).then_inc(s_td, 1)
                                dve.wait_ge(s_gl[slot], landed)
                                dve.wait_ge(s_td, N + S + 1)
                                dve.tensor_tensor(y[:, slot, :], t[:, slot, :], G[:, slot, :], ALU.mult).then_inc(s_yd, 1)
                            if YL == 0:
                                y_lo(N, slot)
                            elif not (is_int(N) and N == 0):
                                y_lo(N - 1, (slot - 1) % S)
                            if not gated and not (is_int(N) and N + WA >= NU):
                                w_lo(N + WA, (slot + WA) % S)

                        def residual(blk, i):
                            dve.wait_ge(s_ot, blk + 1)
                            xv = X[:, blk * BPB + 2 * i:blk * BPB + 2 * i + 2, :].rearrange("p b d -> p (b d)")
                            dve.tensor_tensor(xv, acc(blk)[:, i, :], xv, ALU.add).then_inc(s_xa, 1)
                            if i == 1 and not final:
                                dve.wait_ge(s_xa, 2 * blk + 6)
                                for b in range(blk * BPB, (blk + 1) * BPB):
                                    dve.bn_stats(stats[:, b, :], X[:, b, :]).then_inc(s_xs, 1)

                        def normed(m, half):
                            if m > 1:
                                dve.wait_ge(s_t, m - 1)
                            dve.wait_ge(s_r, m // 2 + 1)
                            for j in (2 * half, 2 * half + 1):
                                b = m * BPB + j
                                last = dve.tensor_scalar(xn[:, m % 2, j, :], X[:, b, :], mv[:, b, 0:1], rstd[:, b:b + 1],
                                                         ALU.subtract, ALU.mult)
                            last.then_inc(s_n, 1)

                        def x_lo(m, c):
                            dve.wait_ge(s_h, m + 1)
                            tok = slice(m * BLK, (m + 1) * BLK)
                            dve.tensor_tensor(xl[:, c, tok], prep_banks(m)[c], xh[:, c, tok].bitcast(F32),
                                              ALU.subtract).then_inc(s_l, 1)

                        def logits(m):
                            dve.wait_ge(s_lg, m + 1)
                            if m > 0:
                                dve.wait_ge(s_sg, m)
                            rt.logits(dve, prep_banks(m)[1][:, 0:BPB * E].rearrange("p (b e) -> p b e", e=E), s_lgc)

                        def gates_of(m):
                            dve.wait_ge(s_sg, m + 1)
                            yield from rt.gates(dve)
                            if m > 0:
                                dve.wait_ge(s_gT, m)
                            rt.scaled(dve, s_gt)
                            yield

                        making = {m: gates_of(m) for m in range(NBLK)}

                        def route_parts(m, places, n):
                            for _ in range(places.count(n)):
                                next(making[m])
                            if n == places[-1]:
                                for _ in making[m]:
                                    pass

                        def between(blk, n):
                            if blk == 0:
                                route_parts(0, ROUTE0, n)
                                route_parts(1, ROUTE1, n)
                            for i in range(2):
                                if n == ADD[i] and blk > 0:
                                    residual(blk - 1, i)
                            if n == TAIL and blk == 2 and not final:
                                dve.wait_ge(s_xs, 2 * BPB)
                                variances(dve, "c", 0)
                            if blk + 2 < NBLK:
                                if n < 2:
                                    normed(blk + 2, n)
                                for c in range(2):
                                    if n == SPLIT[c]:
                                        x_lo(blk + 2, c)
                                if n == LOG + 2:
                                    logits(blk + 2)
                                route_parts(blk + 2, ROUTE, n)

                        for half in range(2):
                            normed(0, half)
                        variances(dve, tag, 1)
                        rt.constants(dve)
                        for c in range(2):
                            x_lo(0, c)
                        dve.wait_ge(s_rw, 1)
                        dve.tensor_tensor(rwl[:], rwf[:], rwh[:].bitcast(F32), ALU.subtract).then_inc(s_rw, 1)
                        for half in range(2):
                            normed(1, half)
                        for c in range(2):
                            x_lo(1, c)
                        for N in range(0 if gated else WA):
                            w_lo(N, N)
                        logits(0)
                        logits(1)
                        walk(dve, unit, between)
                        if YL == 1:
                            y_lo(NU - 1, (NU - 1) % S)
                        for i in range(2):
                            residual(NBLK - 1, i)

                    @block.tensor
                    def _(pe):
                        pe.sem_inc(s_od, S)

                        def h_prod(blk, N, slot):
                            pe.wait_ge(s_wo, S + N + 1)
                            if gated:
                                pe.wait_ge(s_td, N + S - HB + 1)
                            else:
                                pe.wait_ge(s_re, N - HB + 1) if not (is_int(N) and N < HB) else None
                            xs = slice(blk * BLK, (blk + 1) * BLK)
                            for a in range(2 if gated else 1):
                                o = bank[slot % HB][:, a, :] if gated else bk(slot % HB)
                                m = 0
                                for c in range(2):
                                    wc = slice(a * D + c * P, a * D + (c + 1) * P)
                                    for w_, x_ in ((whi, xh), (whi, xl), (wlo, xh)):
                                        last = pe.matmul(o, w_[:, slot, wc], x_[:, c, xs], start=(m == 0), stop=(m == 5))
                                        m += 1
                            last.then_inc(s_hd, 1)

                        def o_prod(blk, N, n, slot):
                            pe.wait_ge(s_yl, N + 1 + YC)
                            first = is_int(n) and n == 0
                            end = is_int(n) and n == U - 1
                            if first:
                                pe.wait_ge(s_xa, 2 * blk + 2)
                                if blk == 0:
                                    pe.wait_ge(s_lgc, 1)
                                else:
                                    pe.wait_ge(s_gc, min(blk + 2, NBLK))
                            for c in range(2):
                                wc = slice(WC - D + c * P, WC - D + (c + 1) * P)
                                for m, (w_, y_) in enumerate(((whi, yhi), (whi, ylo), (wlo, yhi))):
                                    last = pe.matmul(acc(blk)[:, c, :], w_[:, slot, wc], y_[:, slot, :],
                                                     start=(first and m == 0), stop=(end and m == 2), skip_group_check=True)
                            last.then_inc(s_od, 1)

                        def unit(blk, N, n, slot, landed):
                            if not (is_int(N) and N + LA >= NU):
                                nxt = blk + 1 if is_int(n) and n + LA >= U else blk
                                h_prod(nxt, N + LA, (slot + LA) % S)
                            o_prod(blk, N, n, slot)

                        def epilogue(blk):
                            pe.wait_ge(s_os, blk + 1)
                            for j in range(BPB):
                                for c in range(2):
                                    last = pe.transpose(acc(blk)[:, j // 2, (j % 2) * D + c * P:(j % 2) * D + (c + 1) * P],
                                                        os_[:, c, j * P:(j + 1) * P], ident[:])
                            last.then_inc(s_ot, 1)

                        def transposed(m):
                            pe.wait_ge(s_n, 2 * m + 2)
                            if m == 2:
                                pe.wait_ge(s_lgc, 2)
                                pe.wait_ge(s_gc, 1)
                            if m == 3:
                                pe.wait_ge(s_xa, 6)
                            for c in range(2):
                                for j in range(BPB):
                                    last = pe.transpose(prep_banks(m)[c][:, j * P:(j + 1) * P], xn[:, m % 2, j, c * P:(c + 1) * P], ident[:])
                            last.then_inc(s_t, 1)

                        def logits_t(m):
                            pe.wait_ge(s_l, 2 * m + 2)
                            if m == 2 and GT1 < LOG:
                                pe.wait_ge(s_gc, 2)
                            tok = slice(m * BLK, (m + 1) * BLK)
                            i = 0
                            for c in range(2):
                                for w_, x_ in ((rwh, xh), (rwh, xl), (rwl, xh)):
                                    last = pe.matmul(prep_banks(m)[0][0:E, :], w_[:, c, :], x_[:, c, tok], start=(i == 0), stop=(i == 5))
                                    i += 1
                            last.then_inc(s_lt, 1)

                        def logits(m):
                            pe.wait_ge(s_lc, m + 1)
                            for j in range(BPB):
                                last = pe.transpose(prep_banks(m)[1][:, j * E:(j + 1) * E], lts[:, j * P:(j + 1) * P], ident[0:E, 0:E])
                            last.then_inc(s_lg, 1)

                        def gates_t(m):
                            pe.wait_ge(s_gt, m + 1)
                            if m == 0:
                                pe.wait_ge(s_lc, 2)
                            if m == 1:
                                pe.wait_ge(s_gc, 1)
                                pe.wait_ge(s_l, 6) if GT1 < LOG else pe.wait_ge(s_lc, 3)
                            if m == 2:
                                pe.wait_ge(s_gc, 2)
                            for j in range(BPB):
                                last = pe.transpose(gates_bank(m)[:, j * P:(j + 1) * P], gt[:, j, :], ident[:])
                            last.then_inc(s_gT, 1)

                        def between(blk, n):
                            if n == 1 and blk > 0:
                                epilogue(blk - 1)
                            if blk + 2 < NBLK:
                                if n == TRA:
                                    transposed(blk + 2)
                                if n == LOG:
                                    logits_t(blk + 2)
                                if n == LOG + 1:
                                    logits(blk + 2)
                                if n == U - 1:
                                    gates_t(blk + 2)
                            if blk == 0 and n == GT0:
                                gates_t(0)
                            if blk == 0 and n == GT1:
                                gates_t(1)

                        keep_clock(pe, bk(0), 10)
                        transposed(0)
                        keep_clock(pe, bk(0), 12)
                        pe.wait_ge(s_rw, 2)
                        logits_t(0)
                        transposed(1)
                        logits(0)
                        keep_clock(pe, bk(0), 10)
                        logits_t(1)
                        logits(1)
                        for N in range(LA):
                            h_prod(0, N, N)
                        walk(pe, unit, between)
                        epilogue(NBLK - 1)

        def top_k(dve, step, pd, rd, m8, n, k):
            for b in range(BPB):
                last = dve.max(m8[:, b, :], pd[:, b, 0:n])
            step(last)
            step(dve.memset(m8[:, :, k:8], FILL))
            yield
            for b in range(BPB):
                last = dve.match_replace(rd[:, b, :], m8[:, b, :], pd[:, b, :], TAKEN)
            step(last)

        class Route0:

            def __init__(self, ctx, lg, gt, bias, s_ro):
                self.lg, self.gt, self.bias, self.st = lg, gt, bias, Steps(s_ro)
                self.sc = sb("sc0", [P, BPB, E0], F32, ctx)
                self.pd = sb("pd0", [P, BPB, E0 + 6], F32, ctx)
                self.rd = sb("rd0", [P, BPB, E0 + 6], F32, ctx)
                self.m8 = sb("m80", [P, BPB, 8], F32, ctx)
                self.wt = sb("wt0", [P, BPB, E0], F32, ctx)
                self.sm = sb("sm0", [P, BPB], F32, ctx)
                self.rc = sb("rc0", [P, BPB], F32, ctx)

            def constants(self, dve):
                self.st.up(dve.memset(self.pd[:], FILL))
                dve.wait_ge(self.st.sem, self.st.n)

            def logits(self, dve, src, ready):
                dve.tensor_copy(self.lg[:], src).then_inc(ready, 1)

            def gates(self, dve):
                def step(ins):
                    dve.wait_ge(self.st.sem, self.st.up(ins))

                step(dve.tensor_tensor(self.pd[:, :, 0:E0], self.sc[:], self.bias[:].unsqueeze(1).broadcast_to((P, BPB, E0)), ALU.add))
                yield from top_k(dve, step, self.pd, self.rd, self.m8, E0, TOP0)
                step(dve.tensor_tensor(self.wt[:], self.rd[:, :, 0:E0], self.pd[:, :, 0:E0], ALU.not_equal))
                step(dve.tensor_tensor(self.wt[:], self.wt[:], self.sc[:], ALU.mult))
                step(dve.tensor_reduce(self.sm[:], self.wt[:], AX_X, ALU.add))
                step(dve.tensor_scalar(self.sm[:], self.sm[:], 1e-9, None, ALU.add))
                step(dve.reciprocal(self.rc[:], self.sm[:]))

            def scaled(self, dve, ready):
                dve.tensor_tensor(self.gt[:], self.wt[:], self.rc[:].unsqueeze(2).broadcast_to((P, BPB, E0)),
                                  ALU.mult).then_inc(ready, 1)

        class Route1:

            def __init__(self, ctx, lg, gt, bias, s_ro):
                self.lg, self.gt, self.bias, self.st = lg, gt, bias, Steps(s_ro)
                self.sc = sb("sc1", [P, BPB, E1], F32, ctx)
                self.hi = [sb(f"hi1{i}", [P, BPB, G1], F32, ctx) for i in range(2)]
                self.lo = [sb(f"lo1{i}", [P, BPB, G1], F32, ctx) for i in range(2)]
                self.gd = sb("gd1", [P, BPB, G1 + 8 - KG1], F32, ctx)
                self.gr = sb("gr1", [P, BPB, G1 + 8 - KG1], F32, ctx)
                self.gm = sb("gm1", [P, BPB, G1], F32, ctx)
                self.pd = sb("pd1", [P, BPB, E1 + 8 - TOP1], F32, ctx)
                self.rd = sb("rd1", [P, BPB, E1 + 8 - TOP1], F32, ctx)
                self.m8 = sb("m81", [P, BPB, 8], F32, ctx)
                self.wt = sb("wt1", [P, BPB, E1], F32, ctx)
                self.sm = sb("sm1", [P, BPB], F32, ctx)
                self.rc = sb("rc1", [P, BPB], F32, ctx)

            def constants(self, dve):
                self.st.up(dve.memset(self.pd[:], FILL))
                self.st.up(dve.memset(self.gd[:], FILL))
                dve.wait_ge(self.st.sem, self.st.n)

            def logits(self, dve, src, ready):
                dve.tensor_tensor(self.lg[:], src, self.bias[:].unsqueeze(1).broadcast_to((P, BPB, E1)), ALU.add).then_inc(ready, 1)

            def gates(self, dve):
                st = self.st

                def step(ins):
                    dve.wait_ge(st.sem, st.up(ins))

                q = self.sc[:].rearrange("p b (g k) -> p b g k", k=E1 // G1)
                for i in range(2):
                    a, c = q[:, :, :, 2 * i], q[:, :, :, 2 * i + 1]
                    st.up(dve.tensor_tensor(self.hi[i][:], a, c, ALU.max))
                    st.up(dve.tensor_tensor(self.lo[i][:], a, c, ALU.min))
                dve.wait_ge(st.sem, st.n)
                yield
                for i in range(2):
                    st.up(dve.tensor_tensor(self.lo[i][:], self.lo[i][:], self.hi[i][:], ALU.add))
                st.up(dve.tensor_tensor(self.gm[:], self.hi[0][:], self.hi[1][:], ALU.add))
                dve.wait_ge(st.sem, st.n)
                step(dve.tensor_tensor(self.lo[0][:], self.lo[0][:], self.lo[1][:], ALU.max))
                step(dve.tensor_tensor(self.gd[:, :, 0:G1], self.lo[0][:], self.gm[:], ALU.max))
                yield
                yield from top_k(dve, step, self.gd, self.gr, self.m8, G1, KG1)
                step(dve.tensor_tensor(self.gm[:], self.gr[:, :, 0:G1], self.gd[:, :, 0:G1], ALU.not_equal))
                for k in range(E1 // G1):
                    last = dve.tensor_tensor(self.pd[:, :, 0:E1].rearrange("p b (g k) -> p b g k", k=E1 // G1)[:, :, :, k],
                                             q[:, :, :, k], self.gm[:], ALU.mult)
                step(last)
                yield from top_k(dve, step, self.pd, self.rd, self.m8, E1, TOP1)
                yield
                step(dve.tensor_tensor(self.wt[:], self.rd[:, :, 0:E1], self.pd[:, :, 0:E1], ALU.not_equal))
                step(dve.tensor_tensor(self.wt[:], self.wt[:], self.sc[:], ALU.mult))
                step(dve.tensor_reduce(self.sm[:], self.wt[:], AX_X, ALU.add))
                step(dve.tensor_scalar(self.sm[:], self.sm[:], 1e-20, None, ALU.add))
                step(dve.reciprocal(self.rc[:], self.sm[:]))
                step(dve.tensor_tensor(self.wt[:], self.wt[:], self.rc[:].unsqueeze(2).broadcast_to((P, BPB, E1)), ALU.mult))

            def scaled(self, dve, ready):
                dve.tensor_scalar(self.gt[:], self.wt[:], ROUTE_SCALE, None, ALU.mult).then_inc(ready, 1)

        feed_forward("f0", E0, U0, True, wu0, gates0, 2, Route0, False)

        pc = ExitStack()
        with pc:
            KT = sb("ctx_nat_t_sb", [P, 2, T], ctx=pc)
            headmask = sb("headmask", [P, 8], ctx=pc)
            causal = sb("causal", [P, 4, P], BF16, pc)
            identb = sb("identb", [P, P], BF16, pc)
            KP = sb("k_heads", [P, 2, 2, 8, P], ctx=pc)
            V = sb("v_slot", [P, 2, D + HD1], ctx=pc)
            xn = sb("xn_c", [P, 2, D], ctx=pc)
            qT = sb("q_t", [P, 2, 2, P], ctx=pc)
            nmax = sb("neg_max", [P, 2, NH1], ctx=pc)
            Pr = sb("probs", [P, 8, P], ctx=pc)
            den = sb("den", [P, 2, NH1], ctx=pc)
            rden = sb("rden", [P, 2, NH1], ctx=pc)
            PT = sb("probs_t", [P, 2, 4, P], ctx=pc)
            oT = sb("o_t", [P, 4, P], ctx=pc)
            ov = sb("o_norm", [P, D], ctx=pc)
            s_r = deviation_sems["c"][2]
            s_cl = [sem(f"c_k_loaded{i}") for i in range(3)]
            s_vl = [sem(f"c_v_loaded{i}") for i in range(2)]
            s_vz = sem("c_v_pad_zeroed")
            s_cc = sem("c_causal_loaded")
            s_hm = sem("c_headmask_loaded")
            s_kp = sem("c_k_ready")
            s_n = sem("c_normed")
            s_xt = sem("c_x_t")
            s_qt = sem("c_q_ready")
            s_s = sem("c_scores")
            s_m = sem("c_max")
            s_e = sem("c_exp")
            s_pt = sem("c_probs_t")
            s_pc = sem("c_probs_t_copied")
            s_pv = sem("c_quads_done")
            s_oe = sem("c_out_t_copied")
            s_ot = sem("c_out_ready")
            s_xd = sem("c_residual")
            s_sd = sem("c_dve_step")

            def batches(eng, batch, after_second=None, before_last=None):
                batch(0, 0, False, True)
                batch(1, 1, True, True)
                if after_second:
                    after_second()
                with eng.Fori(1, NB // 2 - 1) as i:
                    for u in range(2):
                        batch(i * 2 + u, u, True, True)
                if before_last:
                    before_last()
                batch(NB - 2, 0, True, True)
                batch(NB - 1, 1, True, False)

            with nc.Block() as block:
                @block.sync
                def _(sp):
                    sp.dma_start(headmask[:], headmask_c).then_inc(s_hm, 16)
                    for i, (first, end) in enumerate(((0, 2), (2, NB // 2), (NB // 2, NB))):
                        ht = slice(first * P, end * P)
                        sp.dma_start(KT[:, :, ht], ctx_nat_t.rearrange("(c p) t -> p c t", p=P)[:, :, ht]).then_inc(s_cl[i], 16)
                        if i == 0:
                            sp.dma_start(causal[:], causal_c).then_inc(s_cc, 16)
                            sp.dma_start(identb[:], identb_c).then_inc(s_cc, 16)
                    with sp.Fori(0, NB // 2) as i:
                        for u in range(2):
                            sp.wait_ge(s_pv, 8 * i + (4 * u + 4))
                            sp.dma_start(V[:, u, 0:D], ctx_nat[bass.ds(i * 2 * P + u * P, P), :]).then_inc(s_vl[u], 16)

                @block.gpsimd
                def _(pool):
                    pool.memset(V[:, :, D:D + HD1], 0.0).then_inc(s_vz, 1)

                    def operands(b, u):
                        pool.wait_ge(s_s, 4 * b + 4)
                        for c in range(2):
                            last = pool.tensor_tensor(KP[:, u, c, :, :], KT[:, c, bass.ds(b * P, P)].unsqueeze(1).broadcast_to((P, 8, P)),
                                                      headmask[:].unsqueeze(2).broadcast_to((P, 8, P)), ALU.mult)
                        last.then_inc(s_kp, 1)

                    pool.wait_ge(s_hm, 16)
                    pool.wait_ge(s_cl[0], 16)
                    operands(0, 0)
                    operands(1, 1)
                    deviations(pool, "c", 1)
                    for i in range(2):
                        pool.wait_ge(s_cl[i + 1], 16)
                        with pool.Fori(1 - i, NB // 4) as j:
                            for u in range(2):
                                operands(8 * i + j * 2 + u, u)
                    deviations(pool, "f1", 0)

                @block.tensor
                def _(pe):
                    pe.sem_inc(s_s, 8)
                    pe.sem_inc(s_xt, 2)
                    pe.sem_inc(s_pt, 2)
                    pe.sem_inc(s_pv, 8)
                    pe.sem_inc(s_ot, 1)

                    def queries(b, u, first=False):
                        pe.wait_ge(s_n, b + 1)
                        if not first:
                            pe.wait_ge(s_xd, b)
                        for c in range(2):
                            last = pe.transpose(bk(7)[:, c * P:(c + 1) * P], xn[:, u, c * P:(c + 1) * P], ident[:])
                        last.then_inc(s_xt, 1)

                    def scores(b, u, t):
                        if t == 0:
                            pe.wait_ge(s_kp, b + 1)
                            pe.wait_ge(s_qt, b + 1)
                        pe.wait_ge(s_e, 16 * b + 4 * t + 4)
                        pe.matmul(bk(t), identb[:], causal[:].rearrange("p h k -> p (h k)"), start=True, stop=False)
                        h = 4 * (t % 2)
                        pe.matmul(bk(t), qT[:, u, t // 2, :], KP[:, u, t // 2, h:h + 4, :].rearrange("p h k -> p (h k)"),
                                  start=False, stop=True).then_inc(s_s, 1)

                    def probs_t(b, u, t):
                        pe.wait_ge(s_pc, 4 * b + t + 1)
                        for h in range(4):
                            pe.wait_ge(s_e, 16 + 16 * b + 4 * t + h + 1)
                            last = pe.transpose(bk(4 + t % 2)[:, h * P:(h + 1) * P], Pr[:, (4 * t + h) % 8, :], ident[:])
                        last.then_inc(s_pt, 1)

                    def values(b, u, t, loads):
                        pe.wait_ge(s_pc, 2 + 4 * b + t + 1)
                        if t == 0:
                            pe.wait_ge(s_oe, b + 1)
                            pe.wait_ge(s_vl[u], loads)
                        for g in range(4):
                            hc = (4 * t + g) * HD1
                            last = pe.matmul(bk(6)[32 * g:32 * g + 32, t * P:(t + 1) * P], V[:, u, hc:hc + 32], PT[:, t % 2, g, :],
                                             start=True, stop=True, skip_group_check=True)
                        last.then_inc(s_pv, 1)

                    def out_rows(b, copied):
                        pe.wait_ge(s_oe, b + 2)
                        copied()
                        for t in range(4):
                            last = pe.transpose(bk(7)[:, t * P:(t + 1) * P], oT[:, t, :], ident[:])
                        last.then_inc(s_ot, 1)

                    def loads_of(b, u):
                        return 8 * b + (16 - 8 * u)

                    def batch(b, u, has_prev, has_next):
                        scores(b, u, 2)
                        probs_t(b, u, 0)
                        if has_prev:
                            values(b - 1, 1 - u, 3, None)
                        scores(b, u, 3)
                        if has_next:
                            queries(b + 1, 1 - u, first=not has_prev)
                        probs_t(b, u, 1)
                        values(b, u, 0, loads_of(b, u))
                        if has_next:
                            scores(b + 1, 1 - u, 0)
                        probs_t(b, u, 2)
                        if has_prev:
                            out_rows(b - 1, lambda: pe.wait_ge(s_qt, b + 2 if has_next else NB))
                        values(b, u, 1, None)
                        if has_next:
                            scores(b + 1, 1 - u, 1)
                        probs_t(b, u, 3)
                        values(b, u, 2, None)

                    keep_clock(pe, bk(7), 4)
                    queries(0, 0, first=True)
                    keep_clock(pe, bk(6), 16)
                    pe.wait_ge(s_cc, 32)
                    pe.wait_ge(s_vz, 1)
                    scores(0, 0, 0)
                    scores(0, 0, 1)
                    batches(pe, batch)
                    values(NB - 1, 1, 3, None)
                    out_rows(NB - 1, lambda: pe.wait_ge(s_xd, NB + 1))

                @block.scalar
                def _(act):
                    act.sem_inc(s_e, 16)
                    act.sem_inc(s_oe, 1)

                    def probs(b, u, t):
                        act.wait_ge(s_m, 4 * b + t + 1)
                        act.wait_ge(s_pt, 4 * b + t + 1)
                        for g in range(4):
                            h = 4 * t + g
                            act.activation(Pr[:, h % 8, :], bk(t)[:, g * P:(g + 1) * P], ACT.Exp, bias=nmax[:, u, h:h + 1],
                                           accum_out=den[:, u, h:h + 1]).then_inc(s_e, 1)

                    def out_copy(b):
                        act.wait_ge(s_pv, 8 + 4 * b + 4)
                        act.wait_ge(s_ot, b + 1)
                        act.activation(oT[:].rearrange("p t q -> p (t q)"), bk(6), ACT.Copy).then_inc(s_oe, 1)

                    def batch(b, u, has_prev, has_next):
                        for t in range(4):
                            probs(b, u, t)
                            if t == 1 and has_prev:
                                out_copy(b - 1)

                    batches(act, batch)
                    out_copy(NB - 1)

                @block.vector
                def _(dve):
                    dve.sem_inc(s_pc, 2)
                    dve.sem_inc(s_xd, 2)
                    variances(dve, "c", 1)

                    def normed(b, u):
                        dve.wait_ge(s_xt, b + 1)
                        xb = X[:, bass.ds(b, 1), :].rearrange("p a d -> p (a d)")
                        dve.tensor_scalar(xn[:, u, :], xb, mv[:, bass.ds(b, 1), 0:1].rearrange("p a d -> p (a d)"),
                                          rstd[:, bass.ds(b, 1)], ALU.subtract, ALU.mult).then_inc(s_n, 1)

                    def q_copy(b, u):
                        dve.wait_ge(s_xt, b + 3)
                        dve.tensor_copy(qT[:, u, :, :].rearrange("p c k -> p (c k)"), bk(7)[:, 0:2 * P]).then_inc(s_qt, 1)

                    def maxima(b, u, t):
                        dve.wait_ge(s_s, 8 + 4 * b + t + 1)
                        dve.tensor_reduce(nmax[:, u, 4 * t:4 * t + 4], bk(t).rearrange("p (h k) -> p h k", k=P), AX_X, ALU.max,
                                          negate=True).then_inc(s_m, 1)

                    def pt_copy(b, u, t):
                        dve.wait_ge(s_pt, 2 + 4 * b + t + 1)
                        dve.wait_ge(s_pv, 4 * b + t + 7)
                        dve.tensor_copy(PT[:, t % 2, :, :].rearrange("p h k -> p (h k)"), bk(4 + t % 2)).then_inc(s_pc, 1)

                    def inverse(b, u):
                        dve.wait_ge(s_e, 16 + 16 * b + 16)
                        dve.reciprocal(rden[:, u, :], den[:, u, :]).then_inc(s_sd, 1)

                    def scaled(b, u):
                        n = 3 * b
                        dve.wait_ge(s_ot, b + 2)
                        dve.wait_ge(s_sd, n + 1)
                        dve.tensor_tensor(ov[:].rearrange("p (h d) -> p h d", d=HD1),
                                          bk(7).rearrange("p (h d) -> p h d", d=32)[:, :, 0:HD1],
                                          rden[:, u, :].unsqueeze(2).broadcast_to((P, NH1, HD1)), ALU.mult).then_inc(s_sd, 1)

                    def residual(b, u):
                        dve.wait_ge(s_sd, 3 * b + 2)
                        xb = X[:, bass.ds(b, 1), :].rearrange("p a d -> p (a d)")
                        dve.scalar_tensor_tensor(xb, ov[:], tg[:, 1:2], xb, ALU.mult, ALU.add).then_inc(s_xd, 1)

                    def moments(b):
                        xb = X[:, bass.ds(b, 1), :].rearrange("p a d -> p (a d)")
                        dve.wait_ge(s_xd, b + 3)
                        plain(dve)
                        dve.bn_stats(stats[:, bass.ds(b, 1), :].rearrange("p a d -> p (a d)"), xb).then_inc(s_sd, 1)

                    def batch(b, u, has_prev, has_next):
                        if has_next:
                            normed(b + 1, 1 - u)
                        maxima(b, u, 2)
                        pt_copy(b, u, 0)
                        maxima(b, u, 3)
                        if has_next:
                            q_copy(b + 1, 1 - u)
                        if has_prev:
                            inverse(b - 1, 1 - u)
                        pt_copy(b, u, 1)
                        if has_next:
                            maxima(b + 1, 1 - u, 0)
                        pt_copy(b, u, 2)
                        if has_prev:
                            scaled(b - 1, 1 - u)
                        if has_next:
                            maxima(b + 1, 1 - u, 1)
                        if has_prev:
                            residual(b - 1, 1 - u)
                        pt_copy(b, u, 3)
                        if has_prev:
                            moments(b - 1)

                    normed(0, 0)
                    q_copy(0, 0)
                    maxima(0, 0, 0)
                    maxima(0, 0, 1)
                    def next_phase():
                        dve.wait_ge(s_sd, 3 * 2 * BPB)
                        variances(dve, "f1", 0)

                    batches(dve, batch, lambda: dve.wait_ge(s_r, 2), next_phase)
                    inverse(NB - 1, 1)
                    scaled(NB - 1, 1)
                    residual(NB - 1, 1)
                    moments(NB - 1)

        feed_forward("f1", E1, U1, False, wu1, gates1, 3, Route1, True)


def kernel(**inputs):
    import numpy as np
    import concourse.bacc as bacc
    from concourse.bass_utils import run_bass_kernel_spmd

    a = {k: np.asarray(v) for k, v in inputs.items()}
    x = a["x"].reshape(T, D)
    c = a["ctx_2048"].reshape(T, D)
    crev = np.ascontiguousarray(c[:, ::-1])
    kpad = np.zeros((NH0, 384), np.float32)
    kpad[:, P - 1:P - 1 + D] = a["L0_xattn_ssm_kernel"]

    def chunks(w):
        return w.T.reshape(2, P, P).transpose(1, 0, 2).reshape(P, 2 * P)

    sw1, sw2, sw3 = a["L0_ffn_sw1"], a["L0_ffn_sw2"], a["L0_ffn_sw3"]
    w12, w3 = a["L0_ffn_w12"], a["L0_ffn_w3"]
    wu0 = [np.concatenate([chunks(sw1[s:s + P]), chunks(sw2[s:s + P]), sw3[:, s:s + P].T], 1) for s in range(0, 1024, P)]
    wu0 += [np.concatenate([chunks(w12[e][:P]), chunks(w12[e][P:]), w3[e].T], 1) for e in range(E0)]
    W1, W2, Ws1, Ws2 = a["L1_ffn_W1"], a["L1_ffn_W2"], a["L1_ffn_Ws1"], a["L1_ffn_Ws2"]
    wu1 = [np.concatenate([chunks(Ws1[s:s + P]), Ws2[:, s:s + P].T], 1) for s in range(0, 256, P)]
    wu1 += [np.concatenate([chunks(W1[e]), W2[e].T], 1) for e in range(E1)]
    p = np.arange(P)
    bf16 = mybir.dt.np(BF16)
    arrays = {
        "x": x, "ctx_rev": crev, "ctx_rev_t": crev.T, "ctx_nat": c, "ctx_nat_t": c.T,
        "g_x": a["g_xattn"], "g_f": a["g_ffn"], "kpad": kpad, "d_skip": a["L0_xattn_D"],
        "wu0": np.stack(wu0), "rw0": a["L0_ffn_router_w"].T, "eb0": a["L0_ffn_expert_bias"],
        "wu1": np.stack(wu1), "rw1": a["L1_ffn_Wr"].T, "br1": a["L1_ffn_br"],
        "ident_c": np.eye(P, dtype=np.float32),
        "anti_c": np.ascontiguousarray(np.eye(P, dtype=np.float32)[::-1]),
        "identb_c": np.eye(P, dtype=np.float32).astype(bf16),
        "rowmask_c": np.concatenate([p[:, None] % 32 // HD0 == np.arange(4), 1 - 2 * (p[:, None] // 32 % 2), p[:, None] // 32 % 2],
                                    1).astype(np.float32),
        "headmask_c": np.where(p[:, None] // HD1 == np.arange(8), SCALE1, 0.0).astype(np.float32),
        "causal_c": np.tile(np.where(p[None, :] > p[:, None], -1e30, 0.0), (1, 4)).reshape(P, 4, P).astype(bf16),
    }
    nc = bacc.Bacc("TRN2", target_bir_lowering=False, num_devices=1)
    feeds, aps = {}, []
    for name, v in arrays.items():
        v = np.ascontiguousarray(v)
        feeds[f"in_{name}"] = v
        aps.append(nc.dram_tensor(f"in_{name}", v.shape, mybir.dt.from_np(v.dtype), kind="ExternalInput").ap())
    aps.append(nc.dram_tensor("out_y", (T, D), F32, kind="ExternalOutput").ap())
    build(nc, *aps)
    r = run_bass_kernel_spmd(nc, [feeds], core_ids=[0])
    return r.results[0]["out_y"].reshape(NB, P, D)
```
